# Optimizing a Trainium2 kernel written in Bass

```python
import numpy as np
import jax
import jax.numpy as jnp

def _softmax(x, axis=-1):
    return jax.nn.softmax(x, axis=axis)

def _gelu(x):
    return jax.nn.gelu(x, approximate=True)

def _silu(x):
    return jax.nn.silu(x)

def _sigmoid(x):
    return jax.nn.sigmoid(x)

def _layernorm(x, axis=-1, eps=1e-05):
    m = jnp.mean(x, axis=axis, keepdims=True)
    v = jnp.var(x, axis=axis, keepdims=True)
    return (x - m) / jnp.sqrt(v + eps)

def _scatter_add(tgt, idx, src, axis=0):
    return tgt.at[idx].add(src)

def _segment_sum(src, seg, n):
    return jax.ops.segment_sum(src, seg, n)
kernel_name = 'mk_flamingo_gated_d2_seqx_r8_ae8bbb'

def setup_inputs(seed: int=0):
    np.random.seed(seed)
    _w = jnp.asarray

    def _rec_inputs():
        import jax
        import jax.numpy as jnp
        _rk = jax.random.key(seed)
        x = -0.0005146 + 1 * jax.random.normal(jax.random.fold_in(_rk, 1), (1, 1024, 128), jnp.float32)
        _lenS = 1024 - jax.random.randint(jax.random.fold_in(_rk, 7), (1,), 0, max(1, 1024 // 4) + 1, jnp.int32)
        _lenS2 = 6404 - jax.random.randint(jax.random.fold_in(_rk, 8), (1,), 0, max(1, 6404 // 4) + 1, jnp.int32)
        _ctx_1024P = jax.random.normal(jax.random.fold_in(_rk, 11), (1, 16, 128), jnp.float32)
        _ctx_1024c = jax.random.dirichlet(jax.random.fold_in(_rk, 511), 0.3 * jnp.ones((16,), jnp.float32), (1, 6404))
        _ctx_1024t = jnp.einsum('bsk,bkd->bsd', _ctx_1024c, _ctx_1024P)
        _ctx_1024t = _ctx_1024t * jax.lax.rsqrt(jnp.mean(jnp.square(_ctx_1024t)) + 1e-12) * 0.953939
        ctx_1024 = -0.000392918 + 0.999932 * (_ctx_1024t + 0.3 * jax.random.normal(jax.random.fold_in(_rk, 611), (1, 6404, 128), jnp.float32))
        _validS = jnp.arange(1024)[None, :] < _lenS[:, None]
        _validS2 = jnp.arange(6404)[None, :] < _lenS2[:, None]
        _causal = jnp.tril(jnp.ones((1024, 1024), dtype=bool))
        mask_BxS2_bf1 = jnp.ones((1, 6404), dtype=bool)
        _g = jax.random.normal(jax.random.fold_in(_rk, 9001), (2, 2), jnp.float32)
        _g = jnp.sign(_g) * jnp.maximum(jnp.abs(_g), 1.0) + (_g == 0) * 1.0
        g_xattn = _g[0]
        g_ffn = _g[1]
        return (x, ctx_1024, mask_BxS2_bf1, g_xattn, g_ffn)
    x, ctx_1024, mask_BxS2_bf1, g_xattn, g_ffn = _rec_inputs()

    def _L0_xattn_setup():
        import jax, jax.numpy as jnp
        import numpy as np
        DIM = 128
        DIM_LATENT = 128
        DIM_HEAD = 64
        HEADS = 16
        INNER = HEADS * DIM_HEAD

        def layernorm(x, g, b, eps=1e-05):
            m = jnp.mean(x, axis=-1, keepdims=True)
            v = jnp.mean((x - m) ** 2, axis=-1, keepdims=True)
            return (x - m) / jnp.sqrt(v + eps) * g + b

        def rmsnorm(x, gamma, eps=1e-08):
            n = jnp.linalg.norm(x, axis=-1, keepdims=True) * x.shape[-1] ** (-0.5)
            return x / jnp.maximum(n, eps) * gamma
        key = jax.random.key(seed)
        ks = jax.random.split(key, 8)
        b, n, m = (4, 512, 64)
        x = jax.random.normal(ks[0], (b, n, DIM), dtype=jnp.float32)
        latents = jax.random.normal(ks[1], (b, m, DIM_LATENT), dtype=jnp.float32)
        mask = jnp.ones((b, n), dtype=bool)
        s = 0.02
        return {'x': x, 'latents': latents, 'mask': mask, 'ln_x_g': jnp.ones((DIM,), jnp.float32), 'ln_x_b': jnp.zeros((DIM,), jnp.float32), 'ln_l_g': jnp.ones((DIM_LATENT,), jnp.float32), 'ln_l_b': jnp.zeros((DIM_LATENT,), jnp.float32), 'qn_g': jnp.ones((DIM_HEAD,), jnp.float32), 'kn_g': jnp.ones((DIM_HEAD,), jnp.float32), 'Wq': jax.random.normal(ks[2], (DIM_LATENT, INNER), jnp.float32) * s, 'Wkv': jax.random.normal(ks[3], (DIM, 2 * INNER), jnp.float32) * s, 'Wout': jax.random.normal(ks[4], (INNER, DIM_LATENT), jnp.float32) * s, 'bout': jnp.zeros((DIM_LATENT,), jnp.float32)}
    _L0_xattn_all = _L0_xattn_setup()
    _L0_xattn_in = {k: v for k, v in _L0_xattn_all.items() if k in ('ln_x_g', 'ln_x_b', 'ln_l_g', 'ln_l_b', 'qn_g', 'kn_g', 'Wq', 'Wkv', 'Wout', 'bout')}
    del _L0_xattn_all

    def _L0_ffn_setup():
        import jax, jax.numpy as jnp
        import numpy as np
        D_MODEL = 128
        NUM_EXPERTS = 8
        TOP_K = 2
        key = jax.random.key(seed)
        k_x, k_g, k_w1, k_w2 = jax.random.split(key, 4)
        B, S, D, E = (4, 256, D_MODEL, NUM_EXPERTS)
        s_in = 1.0 / np.sqrt(D)
        s_hid = 1.0 / np.sqrt(4 * D)
        return {'x': jax.random.normal(k_x, (B, S, D), dtype=jnp.float32), 'gate_w': jax.random.uniform(k_g, (E, D), jnp.float32, -s_in, s_in), 'w1': jax.random.uniform(k_w1, (E, 4 * D, D), jnp.float32, -s_in, s_in), 'w2': jax.random.uniform(k_w2, (E, D, 4 * D), jnp.float32, -s_hid, s_hid)}
    _L0_ffn_all = _L0_ffn_setup()
    _L0_ffn_in = {k: v for k, v in _L0_ffn_all.items() if k in ('gate_w', 'w1', 'w2')}
    del _L0_ffn_all

    def _L1_xattn_setup():
        import jax, jax.numpy as jnp
        import numpy as np
        DIM = 128
        HEADS = 16
        DIM_HEAD = 64
        SCALE = DIM_HEAD ** (-0.5)
        EPS = 1e-05

        def stable_layernorm(x, g):
            x = x / jax.lax.stop_gradient(jnp.max(x, axis=-1, keepdims=True))
            mean = jnp.mean(x, axis=-1, keepdims=True)
            var = jnp.mean(jnp.square(x - mean), axis=-1, keepdims=True)
            return (x - mean) * jax.lax.rsqrt(var + EPS) * g
        key = jax.random.key(seed)
        ks = jax.random.split(key, 6)
        b, n, m = (4, 256, 256)
        inner = HEADS * DIM_HEAD
        return {'x': jax.random.normal(ks[0], (b, n, DIM), jnp.float32), 'context': jax.random.normal(ks[1], (b, m, DIM), jnp.float32), 'Wq': jax.random.normal(ks[2], (DIM, inner), jnp.float32) * 0.02, 'Wkv': jax.random.normal(ks[3], (DIM, 2 * inner), jnp.float32) * 0.02, 'Wo': jax.random.normal(ks[4], (inner, DIM), jnp.float32) * 0.02, 'g_in': jnp.ones((DIM,), jnp.float32), 'g_out': jnp.ones((DIM,), jnp.float32), 'null_kv': jax.random.normal(ks[5], (2, DIM_HEAD), jnp.float32)}
    _L1_xattn_all = _L1_xattn_setup()
    _L1_xattn_in = {k: v for k, v in _L1_xattn_all.items() if k in ('Wq', 'Wkv', 'Wo', 'g_in', 'g_out', 'null_kv')}
    del _L1_xattn_all

    def _L1_ffn_setup():
        import jax, jax.numpy as jnp
        import numpy as np
        E = 8
        TOP_K = 2
        H = 128
        I = 64
        B, S = (2, 256)

        def _moe_forward(hidden_states, w_gate, w_fc, w_proj):
            b, s, h = hidden_states.shape
            x = hidden_states.reshape(-1, h)
            T = x.shape[0]
            router_logits = x @ w_gate.T
            topk_vals, topk_idx = jax.lax.top_k(router_logits, TOP_K)
            router_weights = jax.nn.softmax(topk_vals.astype(jnp.float32), axis=-1).astype(x.dtype)
            gates = jnp.zeros((T, E), x.dtype).at[jnp.arange(T)[:, None], topk_idx].add(router_weights)
            hmid = jax.nn.gelu(jnp.einsum('th,eih->tei', x, w_fc), approximate=False)
            y = jnp.einsum('tei,ehi->teh', hmid, w_proj)
            out = jnp.einsum('teh,te->th', y, gates)
            return out.reshape(b, s, h)
        key = jax.random.key(seed)
        k0, k1, k2, k3 = jax.random.split(key, 4)
        std = 0.02
        return {'hidden_states': jax.random.normal(k0, (B, S, H), dtype=jnp.float32), 'w_gate': jax.random.normal(k1, (E, H), dtype=jnp.float32) * std, 'w_fc': jax.random.normal(k2, (E, I, H), dtype=jnp.float32) * std, 'w_proj': jax.random.normal(k3, (E, H, I), dtype=jnp.float32) * (std / np.sqrt(48.0))}
    _L1_ffn_all = _L1_ffn_setup()
    _L1_ffn_in = {k: v for k, v in _L1_ffn_all.items() if k in ('w_gate', 'w_fc', 'w_proj')}
    del _L1_ffn_all
    return {'x': x, 'ctx_1024': ctx_1024, 'mask_BxS2_bf1': mask_BxS2_bf1, 'g_xattn': g_xattn, 'g_ffn': g_ffn, 'L0_xattn_ln_x_g': _L0_xattn_in['ln_x_g'], 'L0_xattn_ln_x_b': _L0_xattn_in['ln_x_b'], 'L0_xattn_ln_l_g': _L0_xattn_in['ln_l_g'], 'L0_xattn_ln_l_b': _L0_xattn_in['ln_l_b'], 'L0_xattn_qn_g': _L0_xattn_in['qn_g'], 'L0_xattn_kn_g': _L0_xattn_in['kn_g'], 'L0_xattn_Wq': _L0_xattn_in['Wq'], 'L0_xattn_Wkv': _L0_xattn_in['Wkv'], 'L0_xattn_Wout': _L0_xattn_in['Wout'], 'L0_xattn_bout': _L0_xattn_in['bout'], 'L0_ffn_gate_w': _L0_ffn_in['gate_w'], 'L0_ffn_w1': _L0_ffn_in['w1'], 'L0_ffn_w2': _L0_ffn_in['w2'], 'L1_xattn_Wq': _L1_xattn_in['Wq'], 'L1_xattn_Wkv': _L1_xattn_in['Wkv'], 'L1_xattn_Wo': _L1_xattn_in['Wo'], 'L1_xattn_g_in': _L1_xattn_in['g_in'], 'L1_xattn_g_out': _L1_xattn_in['g_out'], 'L1_xattn_null_kv': _L1_xattn_in['null_kv'], 'L1_ffn_w_gate': _L1_ffn_in['w_gate'], 'L1_ffn_w_fc': _L1_ffn_in['w_fc'], 'L1_ffn_w_proj': _L1_ffn_in['w_proj']}

def reference(x, ctx_1024, mask_BxS2_bf1, g_xattn, g_ffn, L0_xattn_ln_x_g, L0_xattn_ln_x_b, L0_xattn_ln_l_g, L0_xattn_ln_l_b, L0_xattn_qn_g, L0_xattn_kn_g, L0_xattn_Wq, L0_xattn_Wkv, L0_xattn_Wout, L0_xattn_bout, L0_ffn_gate_w, L0_ffn_w1, L0_ffn_w2, L1_xattn_Wq, L1_xattn_Wkv, L1_xattn_Wo, L1_xattn_g_in, L1_xattn_g_out, L1_xattn_null_kv, L1_ffn_w_gate, L1_ffn_w_fc, L1_ffn_w_proj):
    import jax
    import jax.numpy as jnp

    def _L0_xattn_ref(x, latents, mask, ln_x_g, ln_x_b, ln_l_g, ln_l_b, qn_g, kn_g, Wq, Wkv, Wout, bout):
        import jax, jax.numpy as jnp
        import numpy as np
        DIM = 128
        DIM_LATENT = 128
        DIM_HEAD = 64
        HEADS = 16
        INNER = HEADS * DIM_HEAD

        def layernorm(x, g, b, eps=1e-05):
            m = jnp.mean(x, axis=-1, keepdims=True)
            v = jnp.mean((x - m) ** 2, axis=-1, keepdims=True)
            return (x - m) / jnp.sqrt(v + eps) * g + b

        def rmsnorm(x, gamma, eps=1e-08):
            n = jnp.linalg.norm(x, axis=-1, keepdims=True) * x.shape[-1] ** (-0.5)
            return x / jnp.maximum(n, eps) * gamma
        b, n, _ = x.shape
        m = latents.shape[1]
        h, d = (HEADS, DIM_HEAD)
        scale = d ** (-0.5)
        xn = layernorm(x, ln_x_g, ln_x_b)
        ln = layernorm(latents, ln_l_g, ln_l_b)
        q = (ln @ Wq).reshape(b, m, h, d).transpose(0, 2, 1, 3)
        kv = jnp.concatenate([xn @ Wkv, ln @ Wkv], axis=1)
        kv = kv.reshape(b, n + m, 2, h, d)
        k = kv[:, :, 0].transpose(0, 2, 1, 3)
        v = kv[:, :, 1].transpose(0, 2, 1, 3)
        qn = rmsnorm(q, qn_g) * scale
        kn = rmsnorm(k, kn_g)
        sim = jnp.einsum('bhid,bhjd->bhij', qn, kn)
        max_neg = -jnp.finfo(sim.dtype).max
        padded_mask = jnp.concatenate([mask, jnp.ones((b, m), bool)], axis=1)
        sim = jnp.where(padded_mask[:, None, None, :], sim, max_neg)
        attn = jax.nn.softmax(sim.astype(jnp.float32), axis=-1).astype(sim.dtype)
        out = jnp.einsum('bhij,bhjd->bhid', attn, v)
        out = out.transpose(0, 2, 1, 3).reshape(b, m, h * d)
        return out @ Wout + bout

    def _L0_ffn_ref(x, gate_w, w1, w2):
        import jax, jax.numpy as jnp
        import numpy as np
        D_MODEL = 128
        NUM_EXPERTS = 8
        TOP_K = 2
        gate_logits = jnp.einsum('bsd,ed->bse', x, gate_w)
        top_v, top_i = jax.lax.top_k(gate_logits, TOP_K)
        gates = jax.nn.softmax(top_v, axis=-1)
        combine = jnp.sum(jax.nn.one_hot(top_i, NUM_EXPERTS, dtype=x.dtype) * gates[..., None], axis=-2)
        out = jnp.zeros_like(x)
        for e in range(NUM_EXPERTS):
            h = jax.nn.relu(jnp.einsum('bsd,fd->bsf', x, w1[e]))
            y = jnp.einsum('bsf,df->bsd', h, w2[e])
            out = out + combine[..., e, None] * y
        return out

    def _L1_xattn_ref(x, context, Wq, Wkv, Wo, g_in, g_out, null_kv):
        import jax, jax.numpy as jnp
        import numpy as np
        DIM = 128
        HEADS = 16
        DIM_HEAD = 64
        SCALE = DIM_HEAD ** (-0.5)
        EPS = 1e-05

        def stable_layernorm(x, g):
            x = x / jax.lax.stop_gradient(jnp.max(x, axis=-1, keepdims=True))
            mean = jnp.mean(x, axis=-1, keepdims=True)
            var = jnp.mean(jnp.square(x - mean), axis=-1, keepdims=True)
            return (x - mean) * jax.lax.rsqrt(var + EPS) * g
        b, n, _ = x.shape
        x = stable_layernorm(x, g_in)
        q = x @ Wq
        kv = context @ Wkv
        k, v = jnp.split(kv, 2, axis=-1)

        def to_heads(t):
            return t.reshape(b, t.shape[1], HEADS, DIM_HEAD).transpose(0, 2, 1, 3)
        q, k, v = (to_heads(q), to_heads(k), to_heads(v))
        nk = jnp.broadcast_to(null_kv[0], (b, HEADS, 1, DIM_HEAD))
        nv = jnp.broadcast_to(null_kv[1], (b, HEADS, 1, DIM_HEAD))
        k = jnp.concatenate([nk, k], axis=2)
        v = jnp.concatenate([nv, v], axis=2)
        q = q * SCALE
        sim = jnp.einsum('bhid,bhjd->bhij', q, k)
        attn = jax.nn.softmax(sim.astype(jnp.float32), axis=-1).astype(sim.dtype)
        out = jnp.einsum('bhij,bhjd->bhid', attn, v)
        out = out.transpose(0, 2, 1, 3).reshape(b, n, HEADS * DIM_HEAD)
        out = out @ Wo
        return stable_layernorm(out, g_out)

    def _L1_ffn_ref(hidden_states, w_gate, w_fc, w_proj):
        import jax, jax.numpy as jnp
        import numpy as np
        E = 8
        TOP_K = 2
        H = 128
        I = 64
        B, S = (2, 256)

        def _moe_forward(hidden_states, w_gate, w_fc, w_proj):
            b, s, h = hidden_states.shape
            x = hidden_states.reshape(-1, h)
            T = x.shape[0]
            router_logits = x @ w_gate.T
            topk_vals, topk_idx = jax.lax.top_k(router_logits, TOP_K)
            router_weights = jax.nn.softmax(topk_vals.astype(jnp.float32), axis=-1).astype(x.dtype)
            gates = jnp.zeros((T, E), x.dtype).at[jnp.arange(T)[:, None], topk_idx].add(router_weights)
            hmid = jax.nn.gelu(jnp.einsum('th,eih->tei', x, w_fc), approximate=False)
            y = jnp.einsum('tei,ehi->teh', hmid, w_proj)
            out = jnp.einsum('teh,te->th', y, gates)
            return out.reshape(b, s, h)
        return _moe_forward(hidden_states, w_gate, w_proj=w_proj, w_fc=w_fc)
    x = x + jnp.tanh(g_xattn[0]) * _L0_xattn_ref(ctx_1024, _layernorm(x, axis=-1), mask_BxS2_bf1, L0_xattn_ln_x_g, L0_xattn_ln_x_b, L0_xattn_ln_l_g, L0_xattn_ln_l_b, L0_xattn_qn_g, L0_xattn_kn_g, L0_xattn_Wq, L0_xattn_Wkv, L0_xattn_Wout, L0_xattn_bout)
    x = x + jnp.tanh(g_ffn[0]) * _L0_ffn_ref(_layernorm(x, axis=-1), L0_ffn_gate_w, L0_ffn_w1, L0_ffn_w2)
    x = x + jnp.tanh(g_xattn[1]) * _L1_xattn_ref(_layernorm(x, axis=-1), ctx_1024, L1_xattn_Wq, L1_xattn_Wkv, L1_xattn_Wo, L1_xattn_g_in, L1_xattn_g_out, L1_xattn_null_kv)
    x = x + jnp.tanh(g_ffn[1]) * _L1_ffn_ref(_layernorm(x, axis=-1), L1_ffn_w_gate, L1_ffn_w_fc, L1_ffn_w_proj)
    return x

_drawn_inputs = setup_inputs


def setup_inputs(seed=0):
    import zlib

    import numpy as np

    out = dict(_drawn_inputs(seed))
    spreads = {'g_ffn': (-1.0, 0.6),
     'L0_xattn_ln_x_g': (1.0, 0.6),
     'L0_xattn_ln_x_b': (0.0, 0.767),
     'L0_xattn_ln_l_g': (1.0, 0.6),
     'L0_xattn_ln_l_b': (0.0, 0.8),
     'L0_xattn_qn_g': (1.0, 0.6),
     'L0_xattn_kn_g': (1.0, 0.6),
     'L0_xattn_bout': (0.0, 0.1),
     'L1_xattn_g_in': (1.0, 0.6),
     'L1_xattn_g_out': (1.0, 0.2)}
    factors = {'L0_xattn_Wq': 3.243,
     'L1_xattn_Wq': 3.9,
     'L1_xattn_null_kv': 8.0,
     'L1_ffn_w_gate': 8.0,
     'L1_ffn_w_fc': 8.0,
     'L1_ffn_w_proj': 8.0}
    for name, (base, spread) in spreads.items():
        noise = np.random.default_rng([zlib.crc32(name.encode()), seed]).standard_normal(out[name].shape)
        drawn = base * np.exp(spread * noise) if base else spread * noise
        out[name] = jnp.asarray(drawn.astype(out[name].dtype))
    for name, factor in factors.items():
        out[name] = (out[name] * factor).astype(out[name].dtype)
    return out
```

```python
import concourse.bass as bass
from concourse import mybir
from contextlib import ExitStack

F32, R32, U8, U32 = mybir.dt.float32, mybir.dt.float32r, mybir.dt.uint8, mybir.dt.uint32
ALU = mybir.AluOpType
ACT = mybir.ActivationFunctionType
AX = mybir.AxisListType
RADD = bass.bass_isa.ReduceOp.add
RMAX = bass.bass_isa.ReduceOp.max

P = 128
D = 128
NQ = 1024
QT = NQ // P
NCTX = 6404
CTX_FULL = NCTX // P
CTX_REST = NCTX - CTX_FULL * P
H, DH = 16, 64
GH = 4
NG = H // GH
CT = 4
TAIL = 3
NE = 8
LN_EPS = 1e-5
SCALE = DH ** -0.5


class Steps:

    def __init__(self, eng, sem, base=0):
        self.eng, self.sem, self.base, self.n = eng, sem, base, 0

    def __call__(self, ins):
        ins.then_inc(self.sem, 1)
        self.n += 1
        self.eng.wait_ge(self.sem, self.base + self.n)


def over(ap, shape):
    return ap.unsqueeze(2).broadcast_to(shape)


def flamingo(nc, A, out):
    ctx = ExitStack()
    with ctx:
        def sb(name, shape, dt=F32, to=ctx):
            return to.enter_context(nc.sbuf_tensor(name, shape, dt))

        def sem(name):
            return ctx.enter_context(nc.semaphore(name))

        X = sb("residual", [P, QT, D])
        Y = sb("branch", [P, QT, D])
        Z = sb("normed", [P, QT, D])
        sqz = sb("squares", [P, QT, D])
        lnT = sb("normed_T", [P, NQ])
        stat = sb("stat", [P, 4, 64])
        ident = sb("identity", [P, P])
        mhalf = sb("minus_half", [P, 64])
        phalf = sb("plus_half", [P, 64])
        gates = sb("gates", [P, 4])
        scores = ctx.enter_context(nc.psum_tensor("scores_ps", [P, 2, NQ], F32))
        outs = ctx.enter_context(nc.psum_tensor("out_ps", [P, NQ], F32))
        proj = ctx.enter_context(nc.psum_tensor("proj_ps", [P, 512], F32))
        spare = ctx.enter_context(nc.psum_tensor("spare_ps", [P, 512], F32))

        loaded, made, gated = sem("x_loaded"), sem("const_made"), sem("gates_ready")
        with nc.Block() as block:
            @block.sync
            def _(sp):
                sp.dma_start(X[:, :, :], A["x"].rearrange("(t p) d -> p t d", p=P)).then_inc(loaded, 16)
                sp.dma_start(gates[:, 0:2], A["g_xattn"].partition_broadcast(P)).then_inc(loaded, 16)
                sp.dma_start(gates[:, 2:4], A["g_ffn"].partition_broadcast(P)).then_inc(loaded, 16)
                sp.wait_ge(loaded, 48)

            @block.gpsimd
            def _(pool):
                step = Steps(pool, made)
                step(nc.gpsimd.memset(mhalf[:, :], -0.5))
                step(nc.gpsimd.memset(phalf[:, :], 0.5))
                step(nc.gpsimd.memset(ident[:, :], 0.0))
                step(nc.gpsimd.affine_select(out=ident[:, :], in_=ident[:, :], compare_op=ALU.not_equal,
                                             fill=1.0, base=0, pattern=[[-1, P]], channel_multiplier=1))

            @block.scalar
            def _(act):
                act.wait_ge(loaded, 48)
                nc.scalar.activation(gates[:, :], gates[:, :], ACT.Tanh).then_inc(gated, 1)

        def layer_norm(dve, step, x, dst, sq, T, var_ready, rstd_ready, n):
            shape = [P, T, D]
            step(nc.vector.tensor_reduce(stat[:, 0, 0:T], x, AX.X, ALU.add))
            step(nc.vector.tensor_scalar(stat[:, 1, 0:T], stat[:, 0, 0:T], 1.0 / D, None, ALU.mult))
            step(nc.vector.tensor_tensor(dst, x, over(stat[:, 1, 0:T], shape), ALU.subtract))
            step(nc.vector.tensor_tensor(sq, dst, dst, ALU.mult))
            step(nc.vector.tensor_reduce(stat[:, 2, 0:T], sq, AX.X, ALU.add))
            nc.vector.tensor_scalar(stat[:, 3, 0:T], stat[:, 2, 0:T], 1.0 / D, LN_EPS,
                                    ALU.mult, ALU.add).then_inc(var_ready, 1)
            dve.wait_ge(rstd_ready, n)
            step(nc.vector.tensor_tensor(dst, dst, over(stat[:, 0, 0:T], shape), ALU.mult))

        def rstd(pool, T, var_ready, rstd_ready, n):
            pool.wait_ge(var_ready, n)
            nc.gpsimd.tensor_tensor(stat[:, 0, 0:T], stat[:, 3, 0:T], mhalf[:, 0:T],
                                    ALU.pow).then_inc(rstd_ready, 1)

        for L in range(2):
            attention_layer(nc, A, L, sem, sb, layer_norm, rstd,
                            dict(X=X, Y=Y, Z=Z, sqz=sqz, lnT=lnT, stat=stat, ident=ident, mhalf=mhalf,
                                 phalf=phalf, gates=gates, scores=scores, outs=outs, proj=proj))
            moe_layer(nc, A, L, sem, sb, layer_norm, rstd, out,
                      dict(X=X, Y=Y, Z=Z, sqz=sqz, lnT=lnT, stat=stat, ident=ident, mhalf=mhalf,
                           gates=gates, scores=scores, outs=outs, proj=proj, spare=spare))


def attention_layer(nc, A, L, sem_, sb_, layer_norm, rstd, B):
    X, Y, Z, sqz, stat, ident = B["X"], B["Y"], B["Z"], B["sqz"], B["stat"], B["ident"]
    mhalf, phalf, gates = B["mhalf"], B["phalf"], B["gates"]
    scores, outs, proj = B["scores"], B["outs"], B["proj"]
    QK_NORM = L == 0
    LAT0 = CTX_FULL
    REST = CTX_FULL + (QT if L == 0 else 0)
    NTILES = REST + 1
    NFULL = (NTILES - TAIL) // CT
    PAIRS = NFULL // 2
    assert NFULL * CT + TAIL == NTILES and NFULL % 2 == 0
    PAD_TILES = (NFULL + 1) * CT
    NSTEP = NTILES * GH
    NITEM = PAD_TILES
    NUNIT = (NFULL + 1) * GH
    NAME = "L%d_xattn_" % L

    def sem(name):
        return sem_("a%d_%s" % (L, name))

    scope = ExitStack()
    with scope:
        def sb(name, shape, dt=F32, to=scope):
            return sb_("a%d_%s" % (L, name), shape, dt, to)

        xT = sb("keys_in_T", [P, PAD_TILES * P])
        w_kv = sb("w_kv", [P, NG, 2, GH * DH])
        w_q = sb("w_q", [P, H * DH])
        w_o = sb("w_o", [DH + 1, H, D + 1])
        mask = sb("key_mask", [P, PAD_TILES])
        kbound2 = sb("key_bound2", [P, H])
        row = sb("rows", [P, 4, D])
        col = sb("cols", [P, 4])
        lnT = xT[:, LAT0 * P:(LAT0 + QT) * P] if L == 0 else B["lnT"][:, :]

        w_in, c_in = sem("weights_in"), sem("ctx_in")
        ln_step, var_ready, rstd_ready = sem("ln_step"), sem("var_ready"), sem("rstd_ready")
        lat_ready, ctx_ready, zeroed = sem("lat_ready"), sem("ctx_ready"), sem("zeroed")
        tr_done, tr_read = sem("tr_done"), sem("tr_read")
        mask_f, prep_pool, bnd_in, bnd_out = sem("mask_f"), sem("prep_pool"), sem("bnd_in"), sem("bnd_out")
        mask_in, rest_in = sem("mask_in"), sem("rest_in")
        ln_parts = [(0, 17), (17, 34), (34, CTX_FULL + 1)]
        with ExitStack() as prep:
            raw = sb("ctx_rows", [P, CTX_FULL + 1, D], F32, prep)
            sq = sb("ctx_sq", [P, 17, D], F32, prep)
            m8 = sb("mask_u8", [CTX_FULL, P], U8, prep)
            mf = sb("mask_f32", [CTX_FULL, P], F32, prep)
            m8r = sb("mask_rest_u8", [CTX_REST, 1], U8, prep)
            wsq = sb("w_sq", [P, H, DH], F32, prep)
            jobs = [("lat", list(range(i, i + 4)), i) for i in (0, 4)]
            jobs += [("ctx", list(range(i, min(i + 4, CTX_FULL))), i) for i in range(0, CTX_FULL, 4)]
            jobs += [("rest", [CTX_FULL], REST)]

            with nc.Block() as block:
                @block.sync
                def _(sp):
                    sp.wait_ge(zeroed, 1)
                    sp.dma_start(raw[:, 0:CTX_FULL, :],
                                 A["ctx"][0:CTX_FULL * P, :].rearrange("(t p) d -> p t d", p=P)).then_inc(c_in, 16)
                    sp.dma_start(raw[0:CTX_REST, CTX_FULL, :], A["ctx"][CTX_FULL * P:NCTX, :]).then_inc(c_in, 16)
                    if L == 0:
                        sp.dma_start(m8[:, :], A["mask"][0:CTX_FULL * P].rearrange("(t p) -> t p", p=P)).then_inc(mask_in, 16)
                        sp.dma_start(m8r[:, :], A["mask"][CTX_FULL * P:NCTX].unsqueeze(1)).then_inc(mask_in, 16)

                @block.scalar
                def _(act):
                    n = 0
                    W = A[NAME + "Wkv"]
                    for g in range(NG):
                        for kv in range(2):
                            c0 = kv * H * DH + g * GH * DH
                            act.dma_start(w_kv[:, g, kv, :], W[:, c0:c0 + GH * DH]).then_inc(w_in, 16)
                            n += 16
                    act.dma_start(w_q[:, :], A[NAME + "Wq"]).then_inc(w_in, 16)
                    act.dma_start(w_o[0:DH, :, 0:D],
                                  A[NAME + ("Wout" if L == 0 else "Wo")].rearrange("(h d) n -> d h n", d=DH)).then_inc(w_in, 16)
                    n += 32
                    if L == 0:
                        for i, name in enumerate(("ln_x_g", "ln_x_b", "ln_l_g", "ln_l_b")):
                            act.dma_start(col[:, i:i + 1], A[NAME + name].unsqueeze(1)).then_inc(w_in, 16)
                        act.dma_start(row[:, 0, :], A[NAME + "bout"].partition_broadcast(P)).then_inc(w_in, 16)
                        act.dma_start(row[:, 1, 0:DH], A[NAME + "qn_g"].partition_broadcast(P)).then_inc(w_in, 16)
                        act.dma_start(row[:, 2, 0:DH], A[NAME + "kn_g"].partition_broadcast(P)).then_inc(w_in, 16)
                        n += 16 * 7
                    else:
                        act.dma_start(col[:, 0:1], A[NAME + "g_in"].unsqueeze(1)).then_inc(w_in, 16)
                        act.dma_start(row[:, 0, :], A[NAME + "g_out"].partition_broadcast(P)).then_inc(w_in, 16)
                        act.dma_start(row[:, 1, 0:DH], A[NAME + "null_kv"][0].partition_broadcast(P)).then_inc(w_in, 16)
                        act.dma_start(col[0:DH, 1:2], A[NAME + "null_kv"][0].unsqueeze(1)).then_inc(w_in, 16)
                        act.dma_start(col[DH:P, 1:2], A[NAME + "null_kv"][0].unsqueeze(1)).then_inc(w_in, 16)
                        n += 16 * 5
                    act.wait_ge(w_in, n)
                    for i, (kind, tiles, at) in enumerate(jobs):
                        act.wait_ge(tr_done, i + 1)
                        w = len(tiles) * P
                        src = scores[:, i % 2, 0:w]
                        if kind == "lat":
                            dst = lnT[:, at * P:at * P + w]
                            if L == 0:
                                ins = nc.scalar.activation(dst, src, ACT.Identity, bias=col[:, 3:4], scale=col[:, 2:3])
                            else:
                                ins = nc.scalar.activation(dst, src, ACT.Copy, scale=col[:, 0:1])
                        else:
                            dst = xT[:, at * P:at * P + w]
                            if L == 0:
                                ins = nc.scalar.activation(dst, src, ACT.Identity, bias=col[:, 1:2], scale=col[:, 0:1])
                            else:
                                ins = nc.scalar.activation(dst, src, ACT.Copy)
                        ins.then_inc(tr_read, 1)

                @block.gpsimd
                def _(pool):
                    step = Steps(pool, prep_pool)
                    step(nc.gpsimd.memset(mask[:, :], 0.0))
                    nc.gpsimd.memset(raw[:, CTX_FULL, :], 0.0).then_inc(zeroed, 1)
                    step(nc.gpsimd.memset(xT[:, NTILES * P:PAD_TILES * P], 0.0))
                    step(nc.gpsimd.memset(Y[:, :, :], 0.0))
                    step(nc.gpsimd.memset(w_o[:, :, D:D + 1], 0.0))
                    step(nc.gpsimd.memset(w_o[DH:DH + 1, :, 0:D], 0.0))
                    step(nc.gpsimd.memset(w_o[DH:DH + 1, :, D:D + 1], 1.0))
                    if L == 0:
                        step(nc.gpsimd.memset(mask[:, LAT0:LAT0 + QT], 1.0))
                        step(nc.gpsimd.memset(kbound2[:, :], float(DH)))
                    else:
                        step(nc.gpsimd.memset(mask[:, 0:CTX_FULL], 1.0))
                        step(nc.gpsimd.memset(mask[0:CTX_REST + 1, REST:REST + 1], 1.0))
                    n = 0
                    for T in ([QT, QT] + ([b - a for a, b in ln_parts] if L == 0 else [])):
                        n += 1
                        rstd(pool, T, var_ready, rstd_ready, n)
                    if L == 1:
                        pool.wait_ge(bnd_in, 1)
                        nc.gpsimd.partition_all_reduce(stat[:, 1, 0:1], stat[:, 0, 0:1], P, RMAX).then_inc(bnd_out, 1)
                        nc.gpsimd.partition_all_reduce(stat[:, 1, 16:32], stat[:, 0, 16:32], P, RADD).then_inc(bnd_out, 1)

                @block.vector
                def _(dve):
                    step = Steps(dve, ln_step)
                    layer_norm(dve, step, X[:, :, :], Z[:, :, :], sqz[:, :, :], QT, var_ready, rstd_ready, 1)
                    if L == 1:
                        step(nc.vector.tensor_reduce(stat[:, 0, 0:QT], Z[:, :, :], AX.X, ALU.max))
                        step(nc.vector.reciprocal(stat[:, 1, 0:QT], stat[:, 0, 0:QT]))
                        step(nc.vector.tensor_tensor(Z[:, :, :], Z[:, :, :], over(stat[:, 1, 0:QT], [P, QT, D]), ALU.mult))
                    layer_norm(dve, step, Z[:, :, :], Z[:, :, :], sqz[:, :, :], QT, var_ready, rstd_ready, 2)
                    dve.sem_inc(lat_ready, 1)
                    dve.wait_ge(c_in, 32)
                    if L == 0:
                        for i, (a, b) in enumerate(ln_parts):
                            layer_norm(dve, step, raw[:, a:b, :], raw[:, a:b, :], sq[:, 0:b - a, :], b - a,
                                       var_ready, rstd_ready, 3 + i)
                            dve.sem_inc(ctx_ready, 1)
                        dve.wait_ge(mask_in, 32)
                        nc.vector.tensor_copy(mf[:, :], m8[:, :]).then_inc(mask_f, 1)
                        dve.wait_ge(prep_pool, 1)
                        nc.vector.tensor_copy(mask[0:CTX_REST, REST:REST + 1], m8r[:, :]).then_inc(mask_f, 1)
                        dve.wait_ge(tr_done, len(jobs) + 1)
                        nc.vector.tensor_copy(mask[:, 0:CTX_FULL], outs[:, 0:CTX_FULL]).then_inc(mask_f, 1)
                        dve.wait_ge(w_in, 16 * (2 * NG + 9))
                        step(nc.vector.tensor_tensor(row[:, 3, 0:DH], row[:, 1, 0:DH], row[:, 2, 0:DH], ALU.mult))
                        step(nc.vector.tensor_scalar(row[:, 1, 0:DH], row[:, 3, 0:DH], SCALE, None, ALU.mult))
                    else:
                        for i, (a, b) in enumerate(ln_parts):
                            step(nc.vector.tensor_tensor(sq[:, 0:b - a, :], raw[:, a:b, :], raw[:, a:b, :], ALU.mult))
                            step(nc.vector.tensor_reduce(stat[:, 2, a:b], sq[:, 0:b - a, :], AX.X, ALU.add))
                        step(nc.vector.tensor_reduce(stat[:, 0, 0:1], stat[:, 2, 0:CTX_FULL + 1], AX.X, ALU.max))
                        dve.wait_ge(w_in, 16 * (2 * NG + 7))
                        wk = w_kv[:, :, 0, :]
                        wsq4 = wsq[:, :, :].rearrange("p (g h) d -> p g (h d)", g=NG)
                        step(nc.vector.tensor_tensor(wsq4, wk, wk, ALU.mult))
                        nc.vector.tensor_reduce(stat[:, 0, 16:32], wsq[:, :, :], AX.X, ALU.add).then_inc(bnd_in, 1)
                        dve.wait_ge(bnd_out, 2)
                        step(nc.vector.tensor_scalar(kbound2[:, :], stat[:, 1, 16:32], stat[:, 1, 0:1], None, ALU.mult))

                @block.tensor
                def _(pe):
                    for i, (kind, tiles, at) in enumerate(jobs):
                        if kind == "lat":
                            pe.wait_ge(lat_ready, 1)
                        elif L == 0:
                            pe.wait_ge(ctx_ready, 1 + sum(tiles[-1] >= b for a, b in ln_parts))
                        else:
                            pe.wait_ge(c_in, 32)
                        if i >= 2:
                            pe.wait_ge(tr_read, i - 1)
                        src = Z if kind == "lat" else raw
                        for j, t in enumerate(tiles):
                            last = nc.tensor.transpose(scores[:, i % 2, j * P:(j + 1) * P], src[:, t, :], ident[:, :])
                        last.then_inc(tr_done, 1)
                    if L == 0:
                        pe.wait_ge(mask_f, 1)
                        nc.tensor.transpose(outs[:, 0:CTX_FULL], mf[:, :], ident[0:CTX_FULL, 0:CTX_FULL]).then_inc(tr_done, 1)

        q1 = sb("q1", [P, GH, NQ], R32)
        q2 = sb("q2", [P, GH, NQ], R32)
        k1 = sb("k1", [P, 2, GH, CT, P], R32)
        k2 = sb("k2", [P, 2, GH, CT, P], R32)
        v = sb("v", [P, 2, GH, CT, DH + 1])
        probs = sb("probs", [P, 2, NQ])
        oacc_all = sb("out_acc", [P, GH, NQ])
        oacc = oacc_all[0:DH + 1]
        xc = sb("keys_in_chunk", [P, 2, CT * P])
        krow = Z[:, 0:2, :].rearrange("p a (b c) -> p (a b) c", c=DH)
        ksq = Z[:, 2:4, :].rearrange("p a (b c) -> p (a b) c", c=DH)
        kst = sb("k_stat", [P, 3, GH])
        qa = sb("q_hi_twice", [P, QT, GH, 2, DH], R32)
        qb = sb("q_lo_bound", [P, QT, GH, P], R32)
        qsq = oacc_all[:, 0:2, :].rearrange("p a (b c) -> p (a b) c", c=DH)
        qst = sb("q_stat", [P, 4, QT * GH])
        fin = sqz[:, 0:GH, :]
        frec = sb("fin_rec", [P, GH])
        fsum = sqz[:, GH, :]
        ones = sb("ones", [P, GH])
        nullc = sb("null_cols", [P, 4])
        qf = probs[:, :, :].rearrange("p a (b c) -> p (a b) c", c=DH)
        qps = scores[:, :, :].rearrange("p a (b c) -> p (a b) c", c=DH)
        fin_ps = scores[:, :, :].rearrange("p a (k c) -> p a k c", k=2)

        xc_in = [sem("xc_in0"), sem("xc_in1")]
        kv_done, kv_read, kn_var, kn_rstd, kn_ready = (sem(s) for s in ("kv_done", "kv_read", "kn_var", "kn_rstd", "kn_ready"))
        kt_done, hi_done, lo_done, k2_done = (sem(s) for s in ("kt_done", "k_hi_done", "k_lo_done", "k2_done"))
        s_ready, p_ready, o_ready, o_added, o_zero = (sem(s) for s in ("s_ready", "p_ready", "o_ready", "o_added", "o_zero"))
        q_mm, q_rows, q_var, q_rstd, q_c2, q_c, q_final, q_hi, q_lo, qt_done, q1_read, q2_read = (
            sem(s) for s in ("q_mm", "q_rows", "q_var", "q_rstd", "q_c2", "q_c", "q_final", "q_hi", "q_lo", "qt_done", "q1_read", "q2_read"))
        fin_mm, fin_read, steps_s, consts, null_in, null_fix = (
            sem(s) for s in ("fin_mm", "fin_read", "dve_step", "consts", "null_in", "null_fix"))

        passed = sem("passed")

        def hold(eng, s, value):
            eng.wait_ge(s, value)
            eng.sem_inc(passed, 1)

        ONE = 1

        with nc.Block() as block:
            @block.sync
            def _(sp):
                def load(par, g, c, used):
                    sp.wait_ge(kv_done, ONE + g * NITEM + used)
                    sp.dma_start(xc[:, par, :], xT[:, bass.ds(c * (CT * P), CT * P)]).then_inc(xc_in[par], 16)
                with sp.Fori(0, NG) as g:
                    load(0, g, 0, 0)
                    with sp.Fori(0, PAIRS) as i:
                        load(1, g, i * 2 + 1, i * (2 * CT))
                        load(0, g, i * 2 + 2, i * (2 * CT) + CT)
                    if L == 1:
                        sp.wait_ge(kv_read, (g + 1) * NITEM)
                        for h in range(GH):
                            sp.dma_start(v[CTX_REST:CTX_REST + 1, 0, h, TAIL - 1, 0:DH],
                                         A[NAME + "null_kv"][1:2, :]).then_inc(null_in, 16)

            @block.gpsimd
            def _(pool):
                k2f = k2[:, :, :, :, :].bitcast(F32)
                step = Steps(pool, consts)
                step(nc.gpsimd.memset(k2f[:, 0], 0.0))
                step(nc.gpsimd.memset(k2f[:, 1], 0.0))
                step(nc.gpsimd.memset(ones[:, :], 1.0))
                step(nc.gpsimd.memset(qb[:, :, :, :].bitcast(F32), 0.0))
                for par in range(2):
                    for h in range(GH):
                        r = DH if h % 2 == 0 else 0
                        step(nc.gpsimd.memset(k2f[r:r + 1, par, h], 1.0))

                def item(g, c, j, par):
                    k = g * NITEM + c * CT + j
                    if QK_NORM:
                        pool.wait_ge(kn_var, k + 1)
                        nc.gpsimd.tensor_tensor(kst[:, 2, :], kst[:, 1, :], mhalf[:, 0:GH], ALU.pow).then_inc(kn_rstd, 1)
                    hold(pool, hi_done, k + 1)
                    for e, (a, b) in enumerate(((0, DH), (DH, P))):
                        nc.gpsimd.tensor_copy(k2[a:b, par, e::2, j, :],
                                              k1[a:b, par, e::2, j, :].bitcast(F32)).then_inc(k2_done, 1)
                        hold(pool, k2_done, 2 * k + e + 1)

                with pool.Fori(0, NG) as g:
                    for j in range(CT):
                        item(g, 0, j, 0)
                    if QK_NORM:
                        pool.wait_ge(q_var, g + 1)
                        nc.gpsimd.tensor_tensor(qst[:, 2, :], qst[:, 1, :], mhalf[:, 0:QT * GH], ALU.pow).then_inc(q_rstd, 1)
                    pool.wait_ge(q_c2, g + 1)
                    nc.gpsimd.tensor_tensor(qst[:, 2, :], qst[:, 1, :], phalf[:, 0:QT * GH], ALU.pow).then_inc(q_c, 1)
                    hold(pool, q_lo, g + 1)
                    nc.gpsimd.memset(oacc_all[:, :, :], 0.0).then_inc(o_zero, 1)
                    with pool.Fori(0, PAIRS) as i:
                        for half in range(2):
                            for h in range(GH):
                                item(g, i * 2 + half + 1, h, 1 - half)

            @block.scalar
            def _(act):
                def read_kv(g, c, j, par):
                    k = g * NITEM + c * CT + j
                    act.wait_ge(kv_done, ONE + k + 1)
                    m = mask[:, bass.ds(c * CT + j, 1)]
                    nc.scalar.activation(krow[:, :, :], proj[:, 0:GH * DH].rearrange("p (h d) -> p h d", d=DH), ACT.Copy)
                    nc.scalar.activation(v[:, par, :, j, DH], ones[:, :], ACT.Copy, scale=m)
                    nc.scalar.activation(v[:, par, :, j, 0:DH],
                                         proj[:, GH * DH:2 * GH * DH].rearrange("p (h d) -> p h d", d=DH),
                                         ACT.Copy, scale=m).then_inc(kv_read, 1)

                def k_hi(g, c, j, par):
                    k = g * NITEM + c * CT + j
                    act.wait_ge(kt_done, k + 1)
                    for e, (a, b) in enumerate(((0, DH), (DH, P))):
                        last = nc.scalar.activation(k1[a:b, par, e::2, j, :],
                                                    proj[a:b, 0:2 * P].rearrange("p (n k) -> p n k", k=P), ACT.Copy)
                    last.then_inc(hi_done, 1)

                def exp(s, b):
                    act.wait_ge(s_ready, s + 1)
                    nc.scalar.activation(probs[:, b, :], scores[:, b, :], ACT.Exp).then_inc(p_ready, 1)

                act.wait_ge(consts, 4 + 2 * GH)
                with act.Fori(0, NG) as g:
                    act.wait_ge(q_mm, g + 1)
                    nc.scalar.activation(qf, qps, ACT.Copy, scale=1.0 if QK_NORM else SCALE).then_inc(q_rows, 1)
                    for j in range(CT):
                        read_kv(g, 0, j, 0)
                        k_hi(g, 0, j, 0)
                    act.wait_ge(q_final, g + 1)
                    q4 = qf.rearrange("p (t h) d -> p t h d", h=GH)
                    nc.scalar.activation(qa[:, :, :, 0, :], q4, ACT.Copy).then_inc(q_hi, 1)
                    nc.scalar.activation(qa[:, :, :, 1, :], q4, ACT.Copy).then_inc(q_hi, 1)
                    for h in range(GH):
                        act.wait_ge(qt_done, g * (2 * GH) + 2 * h + 1)
                        nc.scalar.activation(q1[:, h, :], scores[:, 0, :], ACT.Copy).then_inc(q1_read, 1)
                    with act.Fori(0, PAIRS) as i:
                        for half in range(2):
                            for h in range(GH):
                                for t in range(CT):
                                    exp(g * NSTEP + i * (2 * CT * GH) + (half * GH + h) * CT + t, t % 2)
                                    if t == 1:
                                        read_kv(g, i * 2 + half + 1, h, 1 - half)
                                k_hi(g, i * 2 + half + 1, h, 1 - half)
                    for n in range(GH * TAIL):
                        exp(g * NSTEP + NFULL * CT * GH + n, n % 2)

            @block.vector
            def _(dve):
                def k_norm(g, c, j, link):
                    k = g * NITEM + c * CT + j
                    dve.wait_ge(kv_read, k + 1)
                    link(nc.vector.tensor_tensor(ksq[:, :, :], krow[:, :, :], krow[:, :, :], ALU.mult))
                    link(nc.vector.tensor_reduce(kst[:, 0, :], ksq[:, :, :], AX.X, ALU.add))
                    nc.vector.tensor_scalar(kst[:, 1, :], kst[:, 0, :], 1.0 / DH, 1e-16, ALU.mult, ALU.max).then_inc(kn_var, 1)
                    dve.wait_ge(kn_rstd, k + 1)
                    nc.vector.tensor_tensor(krow[:, :, :], krow[:, :, :], over(kst[:, 2, :], [P, GH, DH]), ALU.mult).then_inc(kn_ready, 1)

                def k_lo(g, c, j, par):
                    k = g * NITEM + c * CT + j
                    dve.wait_ge(hi_done, k + 1)
                    for e, (a, b, a2, b2) in enumerate(((0, DH, DH, P), (DH, P, 0, DH))):
                        last = nc.vector.tensor_tensor(k1[a2:b2, par, e::2, j, :],
                                                       proj[a:b, 0:2 * P].rearrange("p (n k) -> p n k", k=P),
                                                       k1[a:b, par, e::2, j, :].bitcast(F32), ALU.subtract)
                    last.then_inc(lo_done, 1)

                def add_out(u, h):
                    dve.wait_ge(o_ready, u + 1)
                    nc.vector.tensor_tensor(oacc[:, h, :], outs[0:DH + 1, :], oacc[:, h, :], ALU.add).then_inc(o_added, 1)

                ITEM_LINKS = 2 if QK_NORM else 0
                Q_LINKS = 6
                FIN_LINKS = 4
                NULL_LINKS = 0 if QK_NORM else 4
                PER_GROUP = NITEM * ITEM_LINKS + Q_LINKS + QT * FIN_LINKS
                dve.wait_ge(consts, 4 + 2 * GH)
                for s in (lo_done, o_added, fin_read):
                    dve.sem_inc(s, ONE)
                if L == 1:
                    link = Steps(dve, steps_s, 0)
                    link(nc.vector.tensor_copy(nullc[:, 0:1].bitcast(R32), col[:, 1:2]))
                    link(nc.vector.tensor_tensor(nullc[:, 1:2], col[:, 1:2], nullc[:, 0:1], ALU.subtract))
                    nc.vector.tensor_copy(nullc[0:DH, 2:3], nullc[0:DH, 0:1])
                    nc.vector.tensor_copy(nullc[DH:P, 2:3], nullc[DH:P, 1:2])
                    link(nc.vector.tensor_copy(nullc[0:DH, 3:4], nullc[0:DH, 1:2]))
                    link(nc.vector.tensor_copy(nullc[DH:P, 3:4], nullc[DH:P, 0:1]))
                with dve.Fori(0, NG) as g:
                    link0 = g * PER_GROUP + NULL_LINKS
                    for j in range(CT):
                        if QK_NORM:
                            k_norm(g, 0, j, Steps(dve, steps_s, link0 + ITEM_LINKS * j))
                        k_lo(g, 0, j, 0)
                    link = Steps(dve, steps_s, link0 + ITEM_LINKS * CT)
                    rows = [P, QT * GH, DH]
                    dve.wait_ge(q_rows, g + 1)
                    if QK_NORM:
                        link(nc.vector.tensor_tensor(qsq[:, :, :], qf, qf, ALU.mult))
                        link(nc.vector.tensor_reduce(qst[:, 0, :], qsq[:, :, :], AX.X, ALU.add))
                        nc.vector.tensor_scalar(qst[:, 1, :], qst[:, 0, :], 1.0 / DH, 1e-16, ALU.mult, ALU.max).then_inc(q_var, 1)
                        dve.wait_ge(q_rstd, g + 1)
                        link(nc.vector.tensor_tensor(qf, qf, over(qst[:, 2, :], rows), ALU.mult))
                        nc.vector.tensor_tensor(qf, qf, row[:, 1:2, 0:DH].broadcast_to(rows), ALU.mult).then_inc(q_final, 1)
                    else:
                        dve.sem_inc(q_final, 1)
                    dve.wait_ge(q_final, g + 1)
                    link(nc.vector.tensor_tensor(qsq[:, :, :], qf, qf, ALU.mult))
                    link(nc.vector.tensor_reduce(qst[:, 0, :], qsq[:, :, :], AX.X, ALU.add))
                    link(nc.vector.tensor_tensor(qst[:, 3, :].rearrange("p (t h) -> p t h", h=GH),
                                                 qst[:, 0, :].rearrange("p (t h) -> p t h", h=GH),
                                                 kbound2[:, bass.ds(g * GH, GH)].unsqueeze(1).broadcast_to([P, QT, GH]), ALU.mult))
                    nc.vector.tensor_scalar(qst[:, 1, :], qst[:, 3, :], 1e-30, None, ALU.max).then_inc(q_c2, 1)
                    dve.wait_ge(q_c, g + 1)
                    if not QK_NORM:
                        link(nc.vector.tensor_tensor(qsq[:, :, :], qf, row[:, 1:2, 0:DH].broadcast_to(rows), ALU.mult))
                        link(nc.vector.tensor_reduce(qst[:, 0, :], qsq[:, :, :], AX.X, ALU.add))
                        link(nc.vector.tensor_tensor(qst[:, 2, :], qst[:, 0, :], qst[:, 2, :], ALU.max))
                    dve.wait_ge(q_hi, 2 * (g + 1))
                    q4 = qf.rearrange("p (t h) d -> p t h d", h=GH)
                    c4 = qst[:, 2, :].rearrange("p (t h) -> p t h", h=GH)
                    for e in range(2):
                        at, cat = (0, DH) if e == 0 else (DH, 0)
                        nc.vector.tensor_tensor(qb[:, :, e::2, at:at + DH], q4[:, :, e::2, :],
                                                qa[:, :, e::2, 0, :].bitcast(F32), ALU.subtract)
                        last = nc.vector.tensor_scalar(qb[:, :, e::2, cat], c4[:, :, e::2], -1.0, None, ALU.mult)
                    last.then_inc(q_lo, 1)
                    for h in range(GH):
                        dve.wait_ge(qt_done, g * (2 * GH) + 2 * h + 2)
                        nc.vector.tensor_copy(q2[:, h, :], scores[:, 1, :]).then_inc(q2_read, 1)
                    hold(dve, o_zero, g + 1)
                    with dve.Fori(0, PAIRS) as i:
                        for half in range(2):
                            for h in range(GH):
                                n = half * GH + h
                                if QK_NORM:
                                    k_norm(g, i * 2 + half + 1, h,
                                           Steps(dve, steps_s, link0 + ITEM_LINKS * CT + Q_LINKS
                                                 + i * (2 * CT * ITEM_LINKS) + n * ITEM_LINKS))
                                k_lo(g, i * 2 + half + 1, h, 1 - half)
                                add_out(g * NUNIT + i * (2 * GH) + n, h)
                    if L == 1:
                        dve.wait_ge(k2_done, (g + 1) * (2 * NITEM))
                        dve.wait_ge(lo_done, ONE + (g + 1) * NITEM)
                        at = CTX_REST
                        for e in range(2):
                            nc.vector.tensor_copy(k1[:, 0, e::2, TAIL - 1, at:at + 1],
                                                  nullc[:, 2 + e:3 + e].unsqueeze(1).broadcast_to([P, GH // 2, 1]))
                            a, b = (0, DH) if e == 0 else (DH, P)
                            last = nc.vector.tensor_copy(k2[a:b, 0, e::2, TAIL - 1, at:at + 1],
                                                         nullc[a:b, 0:1].unsqueeze(1).broadcast_to([DH, GH // 2, 1]))
                        last.then_inc(null_fix, 1)
                    for h in range(GH):
                        add_out(g * NUNIT + NFULL * GH + h, h)
                    link = Steps(dve, steps_s, link0 + NITEM * ITEM_LINKS + Q_LINKS)
                    for t in range(QT):
                        dve.wait_ge(fin_mm, g * QT + t + 1)
                        src = fin_ps[:, t % 2]
                        link(nc.vector.reciprocal(frec[:, :].rearrange("p (k h) -> p k h", k=2),
                                                  src[:, :, 0:2 * (D + 1)].rearrange("p k (h n) -> p k h n", h=2)[:, :, :, D]))
                        for k in range(2):
                            last = nc.vector.tensor_tensor(
                                fin[:, 2 * k:2 * k + 2, :], src[:, k, 0:2 * (D + 1)].rearrange("p (h n) -> p h n", h=2)[:, :, 0:D],
                                over(frec[:, 2 * k:2 * k + 2], [P, 2, D]), ALU.mult)
                        last.then_inc(fin_read, 1)
                        dve.wait_ge(fin_read, ONE + g * QT + t + 1)
                        link(nc.vector.tensor_tensor(fin[:, 0:2, :], fin[:, 0:2, :], fin[:, 2:4, :], ALU.add))
                        link(nc.vector.tensor_tensor(fsum, fin[:, 0, :], fin[:, 1, :], ALU.add))
                        link(nc.vector.tensor_tensor(Y[:, t, :], fsum, Y[:, t, :], ALU.add))

            @block.tensor
            def _(pe):
                def project_kv(g, c, j, par, loads):
                    k = g * NITEM + c * CT + j
                    pe.wait_ge(lo_done, ONE + k)
                    if j == 0:
                        pe.wait_ge(xc_in[par], loads * 16)
                    nc.tensor.matmul(proj[:, :], xc[:, par, j * P:(j + 1) * P],
                                     w_kv[:, bass.ds(g, 1), :, :].rearrange("p g a n -> p (g a n)"),
                                     start=True, stop=True).then_inc(kv_done, 1)

                def transpose_k(g, c, j):
                    k = g * NITEM + c * CT + j
                    pe.wait_ge(kn_ready if QK_NORM else kv_read, k + 1)
                    for n in range(GH // 2):
                        last = nc.tensor.transpose(proj[:, n * P:(n + 1) * P],
                                                   krow[:, 2 * n:2 * n + 2, :].rearrange("p h d -> p (h d)"), ident[:, :])
                    last.then_inc(kt_done, 1)

                def score(b, h, t, par, item=None):
                    if item is not None:
                        pe.wait_ge(lo_done, ONE + item + 1)
                        pe.wait_ge(k2_done, 2 * item + 2)
                    for kk, qq, first in ((k1, q1, True), (k2, q2, False)):
                        for n in range(NQ // 512):
                            last = nc.tensor.matmul(scores[:, b, n * 512:(n + 1) * 512], kk[:, par, h, t, :],
                                                    qq[:, h, n * 512:(n + 1) * 512], start=first, stop=not first)
                    last.then_inc(s_ready, 1)

                def mix(s, b, h, t, par, last_t, u):
                    pe.wait_ge(p_ready, s + 1)
                    if t == 0:
                        pe.wait_ge(o_added, ONE + u)
                    for n in range(NQ // 512):
                        last = nc.tensor.matmul(outs[0:DH + 1, n * 512:(n + 1) * 512], v[:, par, h, t, :],
                                                probs[:, b, n * 512:(n + 1) * 512], start=t == 0, stop=t == last_t)
                    if t == last_t:
                        last.then_inc(o_ready, 1)

                pe.wait_ge(consts, 4 + 2 * GH)
                pe.sem_inc(kv_done, ONE)
                with pe.Fori(0, NG) as g:
                    pe.wait_ge(fin_read, ONE + g * QT)
                    for t in range(QT):
                        last = nc.tensor.matmul(qps[:, t * GH:(t + 1) * GH, :].rearrange("p h d -> p (h d)"),
                                                lnT[:, t * P:(t + 1) * P], w_q[:, bass.ds(g * (GH * DH), GH * DH)],
                                                start=t % 2 == 0, stop=True, skip_group_check=True)
                    last.then_inc(q_mm, 1)
                    for j in range(CT):
                        project_kv(g, 0, j, 0, g * (PAIRS + 1) + 1)
                        transpose_k(g, 0, j)
                    pe.wait_ge(q_lo, g + 1)
                    for h in range(GH):
                        if h:
                            pe.wait_ge(q1_read, g * GH + h)
                        for t in range(QT):
                            last = nc.tensor.transpose(scores[:, 0, t * P:(t + 1) * P],
                                                       qa[:, t, h, :, :].rearrange("p a d -> p (a d)").bitcast(F32), ident[:, :])
                        last.then_inc(qt_done, 1)
                        if h:
                            pe.wait_ge(q2_read, g * GH + h)
                        for t in range(QT):
                            last = nc.tensor.transpose(scores[:, 1, t * P:(t + 1) * P], qb[:, t, h, :].bitcast(F32), ident[:, :])
                        last.then_inc(qt_done, 1)
                    pe.wait_ge(q1_read, (g + 1) * GH)
                    pe.wait_ge(q2_read, (g + 1) * GH)
                    score(0, 0, 0, 0, g * NITEM)
                    with pe.Fori(0, PAIRS) as i:
                        for half in range(2):
                            for h in range(GH):
                                for t in range(CT):
                                    n = (half * GH + h) * CT + t
                                    s = g * NSTEP + i * (2 * GH * CT) + n
                                    n2 = n + 1
                                    half2, h2, t2 = n2 // (GH * CT), n2 // CT % GH, n2 % CT
                                    item = g * NITEM + i * (2 * CT) + half2 * CT + t2 if h2 == 0 else None
                                    score(n2 % 2, h2, t2, half2 % 2, item)
                                    if t == 0:
                                        project_kv(g, i * 2 + half + 1, h, 1 - half,
                                                   g * (PAIRS + 1) + i + 2 if half else g * PAIRS + i + 1)
                                    if t == CT - 1:
                                        transpose_k(g, i * 2 + half + 1, h)
                                    mix(s, n % 2, h, t, half, CT - 1, g * NUNIT + i * (2 * GH) + half * GH + h)
                    for h in range(GH):
                        for t in range(TAIL):
                            n = h * TAIL + t
                            n2 = n + 1
                            if n2 < GH * TAIL:
                                h2, t2 = n2 // TAIL, n2 % TAIL
                                if L == 1 and n2 == TAIL - 1:
                                    pe.wait_ge(null_fix, g + 1)
                                    pe.wait_ge(null_in, (g + 1) * (16 * GH))
                                score(n2 % 2, h2, t2, 0, g * NITEM + NFULL * CT + t2 if h2 == 0 else None)
                            mix(g * NSTEP + NFULL * CT * GH + n, n % 2, h, t, 0, TAIL - 1, g * NUNIT + NFULL * GH + h)
                    pe.wait_ge(o_added, ONE + (g + 1) * NUNIT)
                    for t in range(QT):
                        if t >= 2:
                            pe.wait_ge(fin_read, ONE + g * QT + t - 1)
                        for h in range(GH):
                            last = nc.tensor.matmul(fin_ps[:, t % 2, h // 2, (h % 2) * (D + 1):(h % 2 + 1) * (D + 1)],
                                                    oacc[:, h, t * P:(t + 1) * P],
                                                    w_o[:, bass.ds(g * GH + h, 1), :].rearrange("p h n -> p (h n)"),
                                                    start=h % 2 == 0, stop=True, skip_group_check=True)
                        last.then_inc(fin_mm, 1)

        end_step, var2, rstd2 = sem("end_step"), sem("var2"), sem("rstd2")
        with nc.Block() as block:
            @block.gpsimd
            def _(pool):
                if L == 1:
                    rstd(pool, QT, var2, rstd2, 1)

            @block.vector
            def _(dve):
                step = Steps(dve, end_step)
                full = [P, QT, D]
                if L == 1:
                    step(nc.vector.tensor_reduce(stat[:, 0, 0:QT], Y[:, :, :], AX.X, ALU.max))
                    step(nc.vector.reciprocal(stat[:, 1, 0:QT], stat[:, 0, 0:QT]))
                    step(nc.vector.tensor_tensor(Y[:, :, :], Y[:, :, :], over(stat[:, 1, 0:QT], full), ALU.mult))
                    layer_norm(dve, step, Y[:, :, :], Y[:, :, :], sqz[:, :, :], QT, var2, rstd2, 1)
                op = ALU.add if L == 0 else ALU.mult
                step(nc.vector.tensor_tensor(Y[:, :, :], Y[:, :, :], row[:, 0:1, :].broadcast_to(full), op))
                step(nc.vector.scalar_tensor_tensor(out=X[:, :, :], in0=Y[:, :, :], scalar=gates[:, L:L + 1],
                                                    in1=X[:, :, :], op0=ALU.mult, op1=ALU.add))


def moe_layer(nc, A, L, sem_, sb_, layer_norm, rstd, out, B):
    X, Y, Z, sqz, stat, ident, lnT = (B[n] for n in ("X", "Y", "Z", "sqz", "stat", "ident", "lnT"))
    gates, scores, outs, proj, spare = (B[n] for n in ("gates", "scores", "outs", "proj", "spare"))
    FH = 512 if L == 0 else 64
    FC = NE * FH // P
    FE = FH // P if L == 0 else 1
    KH = P if L == 0 else FH
    NAME = "L%d_ffn_" % L

    def sem(name):
        return sem_("m%d_%s" % (L, name))

    scope = ExitStack()
    with scope:
        def sb(name, shape, dt=F32):
            return sb_("m%d_%s" % (L, name), shape, dt, scope)
        w1 = sb("w1", [P, NE * FH])
        w2 = sb("w2", [P, FC, D])
        wg = sb("wg", [P, NE])
        hid = sb("hidden", [P, 4 if L == 0 else 1, NQ])
        logit = sb("logit", [P, QT, NE])
        top = sb("top", [P, QT, NE])
        topi = sb("top_index", [P, QT, NE], U32)
        topf = sb("top_index_f", [P, QT, 2])
        ids = sb("expert_ids", [P, NE])
        gate = sb("gate", [P, 3, QT])
        one = sb("one_hot", [P, 2, QT, NE])
        comb = sb("combine", [P, QT, NE])

        w_in, step_s, var, rs, z_ready = (sem(s) for s in ("w_in", "step", "var", "rstd", "z_ready"))
        zt_done, zt_read, lg_done, e_in, e_out, ids_ok = (sem(s) for s in ("zt_done", "zt_read", "lg_done", "e_in", "e_out", "ids"))
        h_done, h_read, y_done, y_read, out_in = (sem(s) for s in ("h_done", "h_read", "y_done", "y_read", "out"))
        NH = FC // (4 if L == 0 else 1)
        HT = FC // NH
        EPR = NE // NH
        zt_ps = scores[:, 0, :]
        h_ps = scores
        y_ps = [proj, spare]

        with nc.Block() as block:
            @block.sync
            def _(sp):
                sp.dma_start(wg[:, :], A[NAME + "gateT"]).then_inc(w_in, 16)
                sp.dma_start(w1[:, :], A[NAME + "w1T"]).then_inc(w_in, 16)
                sp.dma_start(w2[:, :, :], A[NAME + "w2T"]).then_inc(w_in, 16)
                if L == 1:
                    sp.wait_ge(y_read, 2 * NE)
                    sp.dma_start(out.rearrange("(t p) d -> p t d", p=P), X[:, :, :]).then_inc(out_in, 16)
                    sp.wait_ge(out_in, 16)

            @block.gpsimd
            def _(pool):
                nc.gpsimd.iota(ids[:, :], [[1, NE]], base=0, channel_multiplier=0,
                               allow_small_or_imprecise_dtypes=True).then_inc(ids_ok, 1)
                rstd(pool, QT, var, rs, 1)

            @block.scalar
            def _(act):
                act.wait_ge(zt_done, 1)
                nc.scalar.activation(lnT[:, :], zt_ps, ACT.Copy).then_inc(zt_read, 1)
                act.wait_ge(e_in, 1)
                nc.scalar.activation(gate[:, 0, :], gate[:, 0, :], ACT.Exp).then_inc(e_out, 1)
                for n in range(NH):
                    for j in range(HT):
                        k = n * HT + j
                        act.wait_ge(h_done, k + 1)
                        if n and j == 0:
                            act.wait_ge(y_done, n * (2 * EPR))
                        nc.scalar.activation(hid[:, j, :], h_ps[:, k % 2, :],
                                             ACT.Relu if L == 0 else ACT.Gelu).then_inc(h_read, 1)

            @block.vector
            def _(dve):
                step = Steps(dve, step_s)
                layer_norm(dve, step, X[:, :, :], Z[:, :, :], sqz[:, :, :], QT, var, rs, 1)
                dve.sem_inc(z_ready, 1)
                dve.wait_ge(lg_done, 1)
                step(nc.vector.tensor_copy(logit[:, :, :], proj[:, 0:QT * NE].rearrange("p (t e) -> p t e", e=NE)))
                for t in range(QT):
                    nc.vector.max(top[:, t, :], logit[:, t, :]).then_inc(step_s, 1)
                step.n += QT
                dve.wait_ge(step_s, step.n)
                for t in range(QT):
                    nc.vector.max_index(topi[:, t, :], top[:, t, :], logit[:, t, :]).then_inc(step_s, 1)
                step.n += QT
                dve.wait_ge(step_s, step.n)
                step(nc.vector.tensor_copy(topf[:, :, :], topi[:, :, 0:2]))
                nc.vector.tensor_tensor(gate[:, 0, :], top[:, :, 1], top[:, :, 0], ALU.subtract).then_inc(e_in, 1)
                dve.wait_ge(e_out, 1)
                step(nc.vector.tensor_scalar(gate[:, 1, :], gate[:, 0, :], 1.0, None, ALU.add))
                step(nc.vector.reciprocal(gate[:, 2, :], gate[:, 1, :]))
                step(nc.vector.tensor_tensor(gate[:, 1, :], gate[:, 0, :], gate[:, 2, :], ALU.mult))
                dve.wait_ge(ids_ok, 1)
                full = [P, QT, NE]
                for k, w in ((0, 2), (1, 1)):
                    step(nc.vector.tensor_tensor(one[:, k], ids[:, :].unsqueeze(1).broadcast_to(full),
                                                 over(topf[:, :, k], full), ALU.is_equal))
                    step(nc.vector.tensor_tensor(one[:, k], one[:, k], over(gate[:, w, :], full), ALU.mult))
                step(nc.vector.tensor_tensor(comb[:, :, :], one[:, 0], one[:, 1], ALU.add))
                step(nc.vector.tensor_scalar(comb[:, :, :], comb[:, :, :], gates[:, 2 + L:3 + L], None, ALU.mult))
                for n in range(NE):
                    for half in range(2):
                        k = n * 2 + half
                        dve.wait_ge(y_done, k + 1)
                        for t in range(4):
                            q = half * 4 + t
                            last = nc.vector.scalar_tensor_tensor(
                                out=X[:, q, :], in0=y_ps[k % 2][:, t * P:(t + 1) * P], scalar=comb[:, q, n:n + 1],
                                in1=X[:, q, :], op0=ALU.mult, op1=ALU.add)
                        last.then_inc(y_read, 1)
                        dve.wait_ge(y_read, k + 1)

            @block.tensor
            def _(pe):
                pe.wait_ge(z_ready, 1)
                for t in range(QT):
                    last = nc.tensor.transpose(zt_ps[:, t * P:(t + 1) * P], Z[:, t, :], ident[:, :])
                last.then_inc(zt_done, 1)
                pe.wait_ge(zt_read, 1)
                pe.wait_ge(w_in, 48)
                for t in range(QT):
                    last = nc.tensor.matmul(proj[:, t * NE:(t + 1) * NE], lnT[:, t * P:(t + 1) * P], wg[:, :],
                                            start=True, stop=True, skip_group_check=True)
                last.then_inc(lg_done, 1)

                def hidden(k):
                    if k >= 2:
                        pe.wait_ge(h_read, k - 1)
                    for c in range(NQ // 512):
                        last = nc.tensor.matmul(h_ps[:, k % 2, c * 512:(c + 1) * 512], w1[:, k * P:(k + 1) * P],
                                                lnT[:, c * 512:(c + 1) * 512], start=True, stop=True)
                    last.then_inc(h_done, 1)

                hidden(0)
                hidden(1)
                for n in range(NH):
                    for j in range(2, HT):
                        hidden(n * HT + j)
                    for e in range(EPR):
                        for half in range(2):
                            k = (n * EPR + e) * 2 + half
                            if e == 0 and half == 0:
                                pe.wait_ge(h_read, (n + 1) * HT)
                            if k == 0:
                                pe.wait_ge(step_s, 6 + 1)
                            if k >= 2:
                                pe.wait_ge(y_read, k - 1)
                            a = 0 if L == 0 else e * FH
                            for t in range(4):
                                q = half * 4 + t
                                for j in range(FE):
                                    last = nc.tensor.matmul(
                                        y_ps[k % 2][:, t * P:(t + 1) * P], hid[a:a + KH, j, q * P:(q + 1) * P],
                                        w2[a:a + KH, n * HT + j, :], start=t == 0 and j == 0, stop=j == FE - 1,
                                        skip_group_check=True)
                            last.then_inc(y_done, 1)
                    if n + 1 < NH:
                        for j in range(min(2, HT)):
                            k = (n + 1) * HT + j
                            if L == 0 or k >= 2:
                                hidden(k)


_OUT = ((1, NQ, D), "float32")


def kernel(**inputs):
    import numpy as np
    import concourse.bacc as bacc
    from concourse.bass_utils import run_bass_kernel_spmd as run

    inp = {k: np.asarray(a) for k, a in inputs.items()}
    lay = {
        "x": inp["x"][0], "ctx": inp["ctx_1024"][0], "mask": inp["mask_BxS2_bf1"][0].view(np.uint8),
        "g_xattn": inp["g_xattn"], "g_ffn": inp["g_ffn"],
        "L0_ffn_gateT": inp["L0_ffn_gate_w"].T, "L1_ffn_gateT": inp["L1_ffn_w_gate"].T,
        "L0_ffn_w1T": inp["L0_ffn_w1"].reshape(-1, D).T, "L1_ffn_w1T": inp["L1_ffn_w_fc"].reshape(-1, D).T,
        "L0_ffn_w2T": inp["L0_ffn_w2"].transpose(0, 2, 1).reshape(-1, P, D).transpose(1, 0, 2),
        "L1_ffn_w2T": inp["L1_ffn_w_proj"].transpose(0, 2, 1).reshape(-1, P, D).transpose(1, 0, 2),
    }
    for k, a in inp.items():
        if "xattn_" in k and k[0] == "L":
            lay[k] = a
    nc = bacc.Bacc("TRN2", target_bir_lowering=False, num_devices=1)
    arrays, A = {}, {}
    for name, a in lay.items():
        a = np.ascontiguousarray(a)
        arrays["in_" + name] = a
        A[name] = nc.dram_tensor("in_" + name, a.shape, mybir.dt.from_np(a.dtype), kind="ExternalInput").ap()
    out = nc.dram_tensor("out", (NQ, D), F32, kind="ExternalOutput").ap()
    flamingo(nc, A, out)
    r = run(nc, [arrays], core_ids=[0])
    return r.results[0]["out"].reshape(_OUT[0])
```

```python
import concourse.bass as bass
from concourse import mybir
from contextlib import ExitStack

F32, R32, F16, B16 = mybir.dt.float32, mybir.dt.float32r, mybir.dt.float16, mybir.dt.bfloat16
U8, U32 = mybir.dt.uint8, mybir.dt.uint32
ALU = mybir.AluOpType
ACT = mybir.ActivationFunctionType
AX = mybir.AxisListType
RADD = bass.bass_isa.ReduceOp.add
RMAX = bass.bass_isa.ReduceOp.max

P = 128
D = 128
NQ = 1024
QT = NQ // P
NCTX = 6404
CTX_FULL = NCTX // P
CTX_REST = NCTX - CTX_FULL * P
H, DH = 16, 64
GH = 4
NG = H // GH
CT = 4
TAIL = 3
NE = 8
LN_EPS = 1e-5
LIFT = 2.0 ** 11
SCALE = DH ** -0.5


class Steps:

    def __init__(self, eng, sem, base=0):
        self.eng, self.sem, self.base, self.n = eng, sem, base, 0

    def __call__(self, ins):
        ins.then_inc(self.sem, 1)
        self.n += 1
        self.eng.wait_ge(self.sem, self.base + self.n)


def over(ap, shape):
    return ap.unsqueeze(2).broadcast_to(shape)


def flamingo(nc, A, out):
    ctx = ExitStack()
    with ctx:
        def sb(name, shape, dt=F32, to=ctx):
            return to.enter_context(nc.sbuf_tensor(name, shape, dt))

        def sem(name):
            return ctx.enter_context(nc.semaphore(name))

        X = sb("residual", [P, QT, D])
        Y = sb("branch", [P, QT, D])
        Z = sb("normed", [P, QT, D])
        sqz = sb("squares", [P, QT, D])
        lnT = sb("normed_T", [P, NQ])
        stat = sb("stat", [P, 4, 64])
        ident = sb("identity", [P, P])
        mhalf = sb("minus_half", [P, 64])
        phalf = sb("plus_half", [P, 64])
        gates = sb("gates", [P, 4])
        scores = ctx.enter_context(nc.psum_tensor("scores_ps", [P, 2, NQ], F32))
        outs = ctx.enter_context(nc.psum_tensor("out_ps", [P, NQ], F32))
        proj = ctx.enter_context(nc.psum_tensor("proj_ps", [P, 512], F32))
        spare = ctx.enter_context(nc.psum_tensor("spare_ps", [P, 512], F32))

        loaded, made, gated = sem("x_loaded"), sem("const_made"), sem("gates_ready")
        with nc.Block() as block:
            @block.sync
            def _(sp):
                sp.dma_start(X[:, :, :], A["x"].rearrange("(t p) d -> p t d", p=P)).then_inc(loaded, 16)
                sp.dma_start(gates[:, 0:2], A["g_xattn"].partition_broadcast(P)).then_inc(loaded, 16)
                sp.dma_start(gates[:, 2:4], A["g_ffn"].partition_broadcast(P)).then_inc(loaded, 16)
                sp.wait_ge(loaded, 48)

            @block.gpsimd
            def _(pool):
                step = Steps(pool, made)
                step(nc.gpsimd.memset(mhalf[:, :], -0.5))
                step(nc.gpsimd.memset(phalf[:, :], 0.5))
                step(nc.gpsimd.memset(ident[:, :], 0.0))
                step(nc.gpsimd.affine_select(out=ident[:, :], in_=ident[:, :], compare_op=ALU.not_equal,
                                             fill=1.0, base=0, pattern=[[-1, P]], channel_multiplier=1))

            @block.scalar
            def _(act):
                act.wait_ge(loaded, 48)
                nc.scalar.activation(gates[:, :], gates[:, :], ACT.Tanh).then_inc(gated, 1)

        def layer_norm(dve, step, x, dst, sq, T, var_ready, rstd_ready, n):
            shape = [P, T, D]
            step(nc.vector.tensor_reduce(stat[:, 0, 0:T], x, AX.X, ALU.add))
            step(nc.vector.tensor_scalar(stat[:, 1, 0:T], stat[:, 0, 0:T], 1.0 / D, None, ALU.mult))
            step(nc.vector.tensor_tensor(dst, x, over(stat[:, 1, 0:T], shape), ALU.subtract))
            step(nc.vector.tensor_tensor(sq, dst, dst, ALU.mult))
            step(nc.vector.tensor_reduce(stat[:, 2, 0:T], sq, AX.X, ALU.add))
            nc.vector.tensor_scalar(stat[:, 3, 0:T], stat[:, 2, 0:T], 1.0 / D, LN_EPS,
                                    ALU.mult, ALU.add).then_inc(var_ready, 1)
            dve.wait_ge(rstd_ready, n)
            step(nc.vector.tensor_tensor(dst, dst, over(stat[:, 0, 0:T], shape), ALU.mult))

        def rstd(pool, T, var_ready, rstd_ready, n):
            pool.wait_ge(var_ready, n)
            nc.gpsimd.tensor_tensor(stat[:, 0, 0:T], stat[:, 3, 0:T], mhalf[:, 0:T],
                                    ALU.pow).then_inc(rstd_ready, 1)

        for L in range(2):
            attention_layer(nc, A, L, sem, sb, layer_norm, rstd,
                            dict(X=X, Y=Y, Z=Z, sqz=sqz, lnT=lnT, stat=stat, ident=ident, mhalf=mhalf,
                                 phalf=phalf, gates=gates, scores=scores, outs=outs, proj=proj, spare=spare))
            moe_layer(nc, A, L, sem, sb, layer_norm, rstd, out,
                      dict(X=X, Y=Y, Z=Z, sqz=sqz, lnT=lnT, stat=stat, ident=ident, mhalf=mhalf,
                           gates=gates, scores=scores, outs=outs, proj=proj, spare=spare))


def attention_layer(nc, A, L, sem_, sb_, layer_norm, rstd, B):
    X, Y, Z, sqz, stat, ident = B["X"], B["Y"], B["Z"], B["sqz"], B["stat"], B["ident"]
    mhalf, phalf, gates = B["mhalf"], B["phalf"], B["gates"]
    scores, outs, proj = B["scores"], B["outs"], B["proj"]
    QK_NORM = L == 0
    LAT0 = CTX_FULL
    REST = CTX_FULL + (QT if L == 0 else 0)
    NTILES = REST + 1
    NFULL = (NTILES - TAIL) // CT
    PAIRS = NFULL // 2
    assert NFULL * CT + TAIL == NTILES and NFULL % 2 == 0
    PAD_TILES = (NFULL + 1) * CT
    NSTEP = NTILES * GH
    NITEM = PAD_TILES
    NUNIT = (NFULL + 1) * GH
    NAME = "L%d_xattn_" % L

    def sem(name):
        return sem_("a%d_%s" % (L, name))

    scope = ExitStack()
    with scope:
        def sb(name, shape, dt=F32, to=scope):
            return sb_("a%d_%s" % (L, name), shape, dt, to)

        xT = sb("keys_in_T", [P, PAD_TILES * P])
        w_kv = sb("w_kv", [P, NG, 2, GH * DH])
        w_q = sb("w_q", [P, H * DH])
        w_o = sb("w_o", [P, H, D + 1])
        w_e = sb("w_e", [P, GH, D])
        mask = sb("key_mask", [P, PAD_TILES])
        kbound2 = sb("key_bound2", [P, H])
        row = sb("rows", [P, 4, D])
        col = sb("cols", [P, 4])
        lnT = xT[:, LAT0 * P:(LAT0 + QT) * P] if L == 0 else B["lnT"][:, :]

        w_in, c_in = sem("weights_in"), sem("ctx_in")
        ln_step, var_ready, rstd_ready = sem("ln_step"), sem("var_ready"), sem("rstd_ready")
        lat_ready, ctx_ready, zeroed = sem("lat_ready"), sem("ctx_ready"), sem("zeroed")
        tr_done, tr_read = sem("tr_done"), sem("tr_read")
        mask_f, prep_pool, bnd_in, bnd_out = sem("mask_f"), sem("prep_pool"), sem("bnd_in"), sem("bnd_out")
        mask_in, rest_in = sem("mask_in"), sem("rest_in")
        ln_parts = [(0, 17), (17, 34), (34, CTX_FULL + 1)]
        with ExitStack() as prep:
            raw = sb("ctx_rows", [P, CTX_FULL + 1, D], F32, prep)
            sq = sb("ctx_sq", [P, 17, D], F32, prep)
            m8 = sb("mask_u8", [CTX_FULL, P], U8, prep)
            mf = sb("mask_f32", [CTX_FULL, P], F32, prep)
            m8r = sb("mask_rest_u8", [CTX_REST, 1], U8, prep)
            wsq = sb("w_sq", [P, H, DH], F32, prep)
            jobs = [("lat", list(range(i, i + 4)), i) for i in (0, 4)]
            jobs += [("ctx", list(range(i, min(i + 4, CTX_FULL))), i) for i in range(0, CTX_FULL, 4)]
            jobs += [("rest", [CTX_FULL], REST)]

            with nc.Block() as block:
                @block.sync
                def _(sp):
                    sp.wait_ge(zeroed, 1)
                    sp.dma_start(raw[:, 0:CTX_FULL, :],
                                 A["ctx"][0:CTX_FULL * P, :].rearrange("(t p) d -> p t d", p=P)).then_inc(c_in, 16)
                    sp.dma_start(raw[0:CTX_REST, CTX_FULL, :], A["ctx"][CTX_FULL * P:NCTX, :]).then_inc(c_in, 16)
                    if L == 0:
                        sp.dma_start(m8[:, :], A["mask"][0:CTX_FULL * P].rearrange("(t p) -> t p", p=P)).then_inc(mask_in, 16)
                        sp.dma_start(m8r[:, :], A["mask"][CTX_FULL * P:NCTX].unsqueeze(1)).then_inc(mask_in, 16)

                @block.scalar
                def _(act):
                    n = 0
                    W = A[NAME + "Wkv"]
                    for g in range(NG):
                        for kv in range(2):
                            c0 = kv * H * DH + g * GH * DH
                            act.dma_start(w_kv[:, g, kv, :], W[:, c0:c0 + GH * DH]).then_inc(w_in, 16)
                            n += 16
                    act.dma_start(w_q[:, :], A[NAME + "Wq"]).then_inc(w_in, 16)
                    w_rows = A[NAME + ("Wout" if L == 0 else "Wo")].rearrange("(h d) n -> d h n", d=DH)
                    act.dma_start(w_o[0:DH, :, 0:D], w_rows).then_inc(w_in, 16)
                    act.wait_ge(prep_pool, 6)
                    act.dma_start(w_o[DH:P - 1, :, 0:D], w_rows[0:DH - 1]).then_inc(w_in, 16)
                    n += 48
                    if L == 0:
                        for i, name in enumerate(("ln_x_g", "ln_x_b", "ln_l_g", "ln_l_b")):
                            act.dma_start(col[:, i:i + 1], A[NAME + name].unsqueeze(1)).then_inc(w_in, 16)
                        act.dma_start(row[:, 0, :], A[NAME + "bout"].partition_broadcast(P)).then_inc(w_in, 16)
                        act.dma_start(row[:, 1, 0:DH], A[NAME + "qn_g"].partition_broadcast(P)).then_inc(w_in, 16)
                        act.dma_start(row[:, 2, 0:DH], A[NAME + "kn_g"].partition_broadcast(P)).then_inc(w_in, 16)
                        n += 16 * 7
                    else:
                        act.dma_start(col[:, 0:1], A[NAME + "g_in"].unsqueeze(1)).then_inc(w_in, 16)
                        act.dma_start(row[:, 0, :], A[NAME + "g_out"].partition_broadcast(P)).then_inc(w_in, 16)
                        act.dma_start(row[:, 1, 0:DH], A[NAME + "null_kv"][0].partition_broadcast(P)).then_inc(w_in, 16)
                        act.dma_start(row[0:1, 2, 0:DH], A[NAME + "null_kv"][1:2, :]).then_inc(w_in, 16)
                        act.dma_start(col[0:DH, 1:2], A[NAME + "null_kv"][0].unsqueeze(1)).then_inc(w_in, 16)
                        act.dma_start(col[DH:P, 1:2], A[NAME + "null_kv"][0].unsqueeze(1)).then_inc(w_in, 16)
                        n += 16 * 6
                    act.wait_ge(w_in, n)
                    nc.scalar.activation(w_o[DH:P, :, 0:D], w_o[DH:P, :, 0:D], ACT.Copy, scale=1.0 / LIFT)
                    for i, (kind, tiles, at) in enumerate(jobs):
                        act.wait_ge(tr_done, i + 1)
                        w = len(tiles) * P
                        src = scores[:, i % 2, 0:w]
                        if kind == "lat":
                            dst = lnT[:, at * P:at * P + w]
                            if L == 0:
                                ins = nc.scalar.activation(dst, src, ACT.Identity, bias=col[:, 3:4], scale=col[:, 2:3])
                            else:
                                ins = nc.scalar.activation(dst, src, ACT.Copy, scale=col[:, 0:1])
                        else:
                            dst = xT[:, at * P:at * P + w]
                            if L == 0:
                                ins = nc.scalar.activation(dst, src, ACT.Identity, bias=col[:, 1:2], scale=col[:, 0:1])
                            else:
                                ins = nc.scalar.activation(dst, src, ACT.Copy)
                        ins.then_inc(tr_read, 1)

                @block.gpsimd
                def _(pool):
                    step = Steps(pool, prep_pool)
                    step(nc.gpsimd.memset(mask[:, :], 0.0))
                    nc.gpsimd.memset(raw[:, CTX_FULL, :], 0.0).then_inc(zeroed, 1)
                    step(nc.gpsimd.memset(xT[:, NTILES * P:PAD_TILES * P], 0.0))
                    step(nc.gpsimd.memset(Y[:, :, :], 0.0))
                    step(nc.gpsimd.memset(w_o[:, :, D:D + 1], 0.0))
                    step(nc.gpsimd.memset(w_o[DH:P, :, 0:D], 0.0))
                    step(nc.gpsimd.memset(w_e[:, :, :], 0.0))
                    step(nc.gpsimd.affine_select(out=w_o[:, :, D], in_=w_o[:, :, D], compare_op=ALU.not_equal,
                                                 fill=1.0, base=1 - P, pattern=[[0, H]], channel_multiplier=1))
                    if L == 0:
                        step(nc.gpsimd.memset(mask[:, LAT0:LAT0 + QT], 1.0))
                        step(nc.gpsimd.memset(kbound2[:, :], float(DH)))
                    else:
                        step(nc.gpsimd.memset(mask[:, 0:CTX_FULL], 1.0))
                        step(nc.gpsimd.memset(mask[0:CTX_REST + 1, REST:REST + 1], 1.0))
                    n = 0
                    for T in ([QT, QT] + ([b - a for a, b in ln_parts] if L == 0 else [])):
                        n += 1
                        rstd(pool, T, var_ready, rstd_ready, n)
                    if L == 1:
                        pool.wait_ge(bnd_in, 1)
                        nc.gpsimd.partition_all_reduce(stat[:, 1, 0:1], stat[:, 0, 0:1], P, RMAX).then_inc(bnd_out, 1)
                        nc.gpsimd.partition_all_reduce(stat[:, 1, 16:32], stat[:, 0, 16:32], P, RADD).then_inc(bnd_out, 1)

                @block.vector
                def _(dve):
                    step = Steps(dve, ln_step)
                    layer_norm(dve, step, X[:, :, :], Z[:, :, :], sqz[:, :, :], QT, var_ready, rstd_ready, 1)
                    if L == 1:
                        step(nc.vector.tensor_reduce(stat[:, 0, 0:QT], Z[:, :, :], AX.X, ALU.max))
                        step(nc.vector.reciprocal(stat[:, 1, 0:QT], stat[:, 0, 0:QT]))
                        step(nc.vector.tensor_tensor(Z[:, :, :], Z[:, :, :], over(stat[:, 1, 0:QT], [P, QT, D]), ALU.mult))
                    layer_norm(dve, step, Z[:, :, :], Z[:, :, :], sqz[:, :, :], QT, var_ready, rstd_ready, 2)
                    dve.sem_inc(lat_ready, 1)
                    dve.wait_ge(c_in, 32)
                    if L == 0:
                        for i, (a, b) in enumerate(ln_parts):
                            layer_norm(dve, step, raw[:, a:b, :], raw[:, a:b, :], sq[:, 0:b - a, :], b - a,
                                       var_ready, rstd_ready, 3 + i)
                            dve.sem_inc(ctx_ready, 1)
                        dve.wait_ge(mask_in, 32)
                        nc.vector.tensor_copy(mf[:, :], m8[:, :]).then_inc(mask_f, 1)
                        dve.wait_ge(prep_pool, 1)
                        nc.vector.tensor_copy(mask[0:CTX_REST, REST:REST + 1], m8r[:, :]).then_inc(mask_f, 1)
                        dve.wait_ge(tr_done, len(jobs) + 1)
                        nc.vector.tensor_copy(mask[:, 0:CTX_FULL], outs[:, 0:CTX_FULL]).then_inc(mask_f, 1)
                        dve.wait_ge(w_in, 16 * (2 * NG + 10))
                        step(nc.vector.tensor_tensor(row[:, 3, 0:DH], row[:, 1, 0:DH], row[:, 2, 0:DH], ALU.mult))
                        step(nc.vector.tensor_scalar(row[:, 1, 0:DH], row[:, 3, 0:DH], SCALE, None, ALU.mult))
                    else:
                        for i, (a, b) in enumerate(ln_parts):
                            step(nc.vector.tensor_tensor(sq[:, 0:b - a, :], raw[:, a:b, :], raw[:, a:b, :], ALU.mult))
                            step(nc.vector.tensor_reduce(stat[:, 2, a:b], sq[:, 0:b - a, :], AX.X, ALU.add))
                        step(nc.vector.tensor_reduce(stat[:, 0, 0:1], stat[:, 2, 0:CTX_FULL + 1], AX.X, ALU.max))
                        dve.wait_ge(w_in, 16 * (2 * NG + 9))
                        wk = w_kv[:, :, 0, :]
                        wsq4 = wsq[:, :, :].rearrange("p (g h) d -> p g (h d)", g=NG)
                        step(nc.vector.tensor_tensor(wsq4, wk, wk, ALU.mult))
                        nc.vector.tensor_reduce(stat[:, 0, 16:32], wsq[:, :, :], AX.X, ALU.add).then_inc(bnd_in, 1)
                        dve.wait_ge(bnd_out, 2)
                        step(nc.vector.tensor_scalar(kbound2[:, :], stat[:, 1, 16:32], stat[:, 1, 0:1], None, ALU.mult))

                @block.tensor
                def _(pe):
                    for i, (kind, tiles, at) in enumerate(jobs):
                        if kind == "lat":
                            pe.wait_ge(lat_ready, 1)
                        elif L == 0:
                            pe.wait_ge(ctx_ready, 1 + sum(tiles[-1] >= b for a, b in ln_parts))
                        else:
                            pe.wait_ge(c_in, 32)
                        if i >= 2:
                            pe.wait_ge(tr_read, i - 1)
                        src = Z if kind == "lat" else raw
                        for j, t in enumerate(tiles):
                            last = nc.tensor.transpose(scores[:, i % 2, j * P:(j + 1) * P], src[:, t, :], ident[:, :])
                        last.then_inc(tr_done, 1)
                    if L == 0:
                        pe.wait_ge(mask_f, 1)
                        nc.tensor.transpose(outs[:, 0:CTX_FULL], mf[:, :], ident[0:CTX_FULL, 0:CTX_FULL]).then_inc(tr_done, 1)

        q1 = sb("q1", [P, GH, NQ], R32)
        q2 = sb("q2", [P, GH, NQ], R32)
        k1 = sb("k1", [P, 2, GH, CT, P], R32)
        k2 = sb("k2", [P, 2, GH, CT, P], R32)
        v16 = sb("v16", [P, 2, GH, CT, P], F16)
        v32 = sb("v32", [P, 2, GH, CT, P], R32)
        vlast = sb("v_last", [P, 2, GH, CT, 32], F16)
        zero32 = sb("zero32", [P, 32], F16)
        probs = sb("probs", [P, 2, NQ])
        plow = sb("probs_lo", [P, 2, NQ], R32)
        oacc_all = sb("out_acc", [P, GH, NQ])
        oacc = oacc_all
        esb = sb("last_col_sums", [P, 512])
        xc = sb("keys_in_chunk", [P, 2, CT * P])
        krow = Z[:, 0:2, :].rearrange("p a (b c) -> p (a b) c", c=DH)
        ksq = Z[:, 2:4, :].rearrange("p a (b c) -> p (a b) c", c=DH)
        kst = sb("k_stat", [P, 3, GH])
        vrow = Z[:, 4:6, :].rearrange("p a (b c) -> p (a b) c", c=DH)
        vres = Z[:, 6:8, :].rearrange("p a (b c) -> p (a b) c", c=DH)
        qa = [k1[:, 1].rearrange("p a b k -> p (a b) k").rearrange("p (t h) k -> p t h k", h=GH),
              v32[:, 1].rearrange("p a b k -> p (a b) k").rearrange("p (t h) k -> p t h k", h=GH)]
        qb = oacc_all[:, :, :].rearrange("p a (b k) -> p (a b) k", k=P).rearrange("p (t h) k -> p t h k", h=GH)
        qsq = oacc_all[:, 0:2, :].rearrange("p a (b c) -> p (a b) c", c=DH)
        qst = sb("q_stat", [P, 4, QT * GH])
        fin = sqz[:, 0:GH, :]
        frec = sb("fin_rec", [P, GH])
        fsum = sqz[:, GH, :]
        ones = sb("ones", [P, GH])
        nullc = sb("null_cols", [P, 4])
        nullv = sb("null_v", [1, 2, DH])
        null16 = sb("null16", [1, P], F16)
        null32 = sb("null32", [1, P], R32)
        qf = probs[:, :, :].rearrange("p a (b c) -> p (a b) c", c=DH)
        last_ps = B["spare"]
        p_hi = probs[:, :, :].bitcast(B16).rearrange("p a (q w) -> p a q w", w=2)[:, :, :, 1]
        qps = scores[:, :, :].rearrange("p a (b c) -> p (a b) c", c=DH)
        fin_ps = scores[:, :, :].rearrange("p a (k c) -> p a k c", k=2)

        xc_in = [sem("xc_in0"), sem("xc_in1")]
        kv_done, kv_read, kn_var, kn_rstd, kn_ready = (sem(s) for s in ("kv_done", "kv_read", "kn_var", "kn_rstd", "kn_ready"))
        kt_done, hi_done, lo_done, k2_done = (sem(s) for s in ("kt_done", "k_hi_done", "k_lo_done", "k2_done"))
        s_ready, p_ready, o_ready, o_added, o_zero = (sem(s) for s in ("s_ready", "p_ready", "o_ready", "o_added", "o_zero"))
        q_mm, q_rows, q_var, q_rstd, q_c2, q_c, q_final, q_hi, q_lo, qt_done, q1_read, q2_read = (
            sem(s) for s in ("q_mm", "q_rows", "q_var", "q_rstd", "q_c2", "q_c", "q_final", "q_hi", "q_lo", "qt_done", "q1_read", "q2_read"))
        v_hi_done, v16_done, v_ready, plo_ready, e_read, we_in, e_done = (
            sem(s) for s in ("v_hi_done", "v16_done", "v_ready", "plo_ready", "e_read", "w_last_in", "e_done"))
        fin_mm, fin_read, steps_s, consts, null_in, null_fix = (
            sem(s) for s in ("fin_mm", "fin_read", "dve_step", "consts", "null_in", "null_fix"))

        passed = sem("passed")

        def hold(eng, s, value):
            eng.wait_ge(s, value)
            eng.sem_inc(passed, 1)

        ONE = 1

        with nc.Block() as block:
            @block.sync
            def _(sp):
                def load(par, g, c, used):
                    sp.wait_ge(kv_done, ONE + g * NITEM + used)
                    sp.dma_start(xc[:, par, :], xT[:, bass.ds(c * (CT * P), CT * P)]).then_inc(xc_in[par], 16)
                with sp.Fori(0, NG) as g:
                    load(0, g, 0, 0)
                    sp.wait_ge(fin_read, ONE + g * QT)
                    for h in range(GH):
                        src = A[NAME + ("Wout" if L == 0 else "Wo")].rearrange("(h d) n -> h d n", d=DH)[
                            bass.ds(g * GH + h, 1), DH - 1, :]
                        for j in range(4):
                            sp.dma_start(w_e[32 * j + h:32 * j + h + 1, h, :], src).then_inc(we_in, 16)
                    with sp.Fori(0, PAIRS) as i:
                        load(1, g, i * 2 + 1, i * (2 * CT))
                        load(0, g, i * 2 + 2, i * (2 * CT) + CT)
                    if L == 1:
                        sp.wait_ge(v_ready, (g + 1) * NITEM)
                        r_ = CTX_REST
                        for h in range(GH):
                            sp.dma_start(v16[r_:r_ + 1, 0, h, TAIL - 1, 0:P - 1], null16[0:1, 0:P - 1]).then_inc(null_in, 16)
                            sp.dma_start(v32[r_:r_ + 1, 0, h, TAIL - 1, 0:P - 1].bitcast(F32), null32[0:1, 0:P - 1].bitcast(F32)).then_inc(null_in, 16)
                            sp.dma_start(vlast[r_:r_ + 1, 0, h, TAIL - 1, h:h + 1], null16[0:1, P - 1:P]).then_inc(null_in, 16)

            @block.gpsimd
            def _(pool):
                k2f = k2[:, :, :, :, :].bitcast(F32)
                step = Steps(pool, consts)
                step(nc.gpsimd.memset(k2f[:, 0], 0.0))
                step(nc.gpsimd.memset(k2f[:, 1], 0.0))
                step(nc.gpsimd.memset(ones[:, :], 1.0))
                step(nc.gpsimd.memset(oacc_all[:, :, :], 0.0))
                step(nc.gpsimd.memset(vlast[:, :, :, :, :], 0.0))
                step(nc.gpsimd.memset(zero32[:, :], 0.0))
                for par in range(2):
                    for h in range(GH):
                        r = DH if h % 2 == 0 else 0
                        step(nc.gpsimd.memset(k2f[r:r + 1, par, h], 1.0))

                def item(g, c, j, par):
                    k = g * NITEM + c * CT + j
                    if QK_NORM:
                        pool.wait_ge(kn_var, k + 1)
                        nc.gpsimd.tensor_tensor(kst[:, 2, :], kst[:, 1, :], mhalf[:, 0:GH], ALU.pow).then_inc(kn_rstd, 1)
                    hold(pool, hi_done, k + 1)
                    for e, (a, b) in enumerate(((0, DH), (DH, P))):
                        nc.gpsimd.tensor_copy(k2[a:b, par, e::2, j, :],
                                              k1[a:b, par, e::2, j, :].bitcast(F32)).then_inc(k2_done, 1)
                        hold(pool, k2_done, 2 * k + e + 1)

                with pool.Fori(0, NG) as g:
                    for j in range(CT):
                        item(g, 0, j, 0)
                    if QK_NORM:
                        pool.wait_ge(q_var, g + 1)
                        nc.gpsimd.tensor_tensor(qst[:, 2, :], qst[:, 1, :], mhalf[:, 0:QT * GH], ALU.pow).then_inc(q_rstd, 1)
                    pool.wait_ge(q_c2, g + 1)
                    nc.gpsimd.tensor_tensor(qst[:, 2, :], qst[:, 1, :], phalf[:, 0:QT * GH], ALU.pow).then_inc(q_c, 1)
                    hold(pool, qt_done, (g + 1) * (2 * GH))
                    nc.gpsimd.memset(oacc_all[:, :, :], 0.0).then_inc(o_zero, 1)
                    with pool.Fori(0, PAIRS) as i:
                        for half in range(2):
                            for h in range(GH):
                                item(g, i * 2 + half + 1, h, 1 - half)

            @block.scalar
            def _(act):
                def read_kv(g, c, j, par):
                    k = g * NITEM + c * CT + j
                    act.wait_ge(kv_done, ONE + k + 1)
                    m = mask[:, bass.ds(c * CT + j, 1)]
                    nc.scalar.activation(krow, proj[:, 0:GH * DH].rearrange("p (h d) -> p h d", d=DH), ACT.Copy)
                    nc.scalar.activation(vrow, proj[:, GH * DH:2 * GH * DH].rearrange("p (h d) -> p h d", d=DH),
                                         ACT.Copy, scale=m).then_inc(kv_read, 1)
                    nc.scalar.activation(v16[:, par, :, j, P - 1], ones[:, :], ACT.Copy, scale=m)

                def v_hi(g, c, j, par):
                    act.wait_ge(kv_read, g * NITEM + c * CT + j + 1)
                    nc.scalar.activation(v16[:, par, :, j, 0:DH], vrow, ACT.Copy).then_inc(v_hi_done, 1)

                def v_wide(g, c, j, par):
                    act.wait_ge(v16_done, g * NITEM + c * CT + j + 1)
                    nc.scalar.activation(v32[:, par, :, j, :], v16[:, par, :, j, :], ACT.Copy).then_inc(v_ready, 1)

                def k_hi(g, c, j, par):
                    k = g * NITEM + c * CT + j
                    act.wait_ge(kt_done, k + 1)
                    for e, (a, b) in enumerate(((0, DH), (DH, P))):
                        last = nc.scalar.activation(k1[a:b, par, e::2, j, :],
                                                    proj[a:b, 0:2 * P].rearrange("p (n k) -> p n k", k=P), ACT.Copy)
                    last.then_inc(hi_done, 1)

                def exp(s, b):
                    act.wait_ge(s_ready, s + 1)
                    nc.scalar.activation(probs[:, b, :], scores[:, b, :], ACT.Exp).then_inc(p_ready, 1)

                act.wait_ge(consts, 6 + 2 * GH)
                act.sem_inc(e_read, ONE)
                with act.Fori(0, NG) as g:
                    act.wait_ge(q_mm, g + 1)
                    nc.scalar.activation(qf, qps, ACT.Copy, scale=1.0 if QK_NORM else SCALE).then_inc(q_rows, 1)
                    for j in range(CT):
                        read_kv(g, 0, j, 0)
                        v_hi(g, 0, j, 0)
                        k_hi(g, 0, j, 0)
                        v_wide(g, 0, j, 0)
                    act.wait_ge(q_final, g + 1)
                    q4 = qf.rearrange("p (t h) d -> p t h d", h=GH)
                    for n in range(2):
                        for b in range(2):
                            nc.scalar.activation(qa[n][:, :, :, b * DH:(b + 1) * DH], q4[:, 4 * n:4 * n + 4],
                                                 ACT.Copy).then_inc(q_hi, 1)
                    for h in range(GH):
                        act.wait_ge(qt_done, g * (2 * GH) + 2 * h + 1)
                        nc.scalar.activation(q1[:, h, :], scores[:, 0, :], ACT.Copy).then_inc(q1_read, 1)
                    with act.Fori(0, PAIRS) as i:
                        for half in range(2):
                            for h in range(GH):
                                for t in range(CT):
                                    exp(g * NSTEP + i * (2 * CT * GH) + (half * GH + h) * CT + t, t % 2)
                                    if t == 1:
                                        read_kv(g, i * 2 + half + 1, h, 1 - half)
                                    if t == 2:
                                        v_hi(g, i * 2 + half + 1, h, 1 - half)
                                k_hi(g, i * 2 + half + 1, h, 1 - half)
                                v_wide(g, i * 2 + half + 1, h, 1 - half)
                    for n in range(GH * TAIL):
                        exp(g * NSTEP + NFULL * CT * GH + n, n % 2)
                    act.wait_ge(e_done, g + 1)
                    nc.scalar.activation(esb[:, :], last_ps[:, :], ACT.Copy, scale=1.0 / LIFT).then_inc(e_read, 1)

            @block.vector
            def _(dve):
                def k_var(g, c, j, link):
                    dve.wait_ge(kv_read, g * NITEM + c * CT + j + 1)
                    link(nc.vector.tensor_tensor(ksq, krow, krow, ALU.mult))
                    link(nc.vector.tensor_reduce(kst[:, 0, :], ksq, AX.X, ALU.add))
                    nc.vector.tensor_scalar(kst[:, 1, :], kst[:, 0, :], 1.0 / DH, 1e-16, ALU.mult, ALU.max).then_inc(kn_var, 1)

                def k_scale(g, c, j):
                    dve.wait_ge(kn_rstd, g * NITEM + c * CT + j + 1)
                    nc.vector.tensor_tensor(krow, krow, over(kst[:, 2, :], [P, GH, DH]), ALU.mult).then_inc(kn_ready, 1)

                def v_lo(g, c, j, par, link):
                    dve.wait_ge(v_hi_done, g * NITEM + c * CT + j + 1)
                    link(nc.vector.tensor_tensor(vres, vrow, v16[:, par, :, j, 0:DH], ALU.subtract))
                    for h in range(GH):
                        nc.vector.tensor_scalar(vlast[:, par, h, j, h:h + 1], vres[:, h, DH - 1:DH], LIFT, None, ALU.mult)
                    nc.vector.tensor_scalar(v16[:, par, :, j, DH:P - 1], vres[:, :, 0:DH - 1], LIFT, None,
                                            ALU.mult).then_inc(v16_done, 1)

                def p_lo(s, b):
                    dve.wait_ge(p_ready, s + 1)
                    nc.vector.tensor_tensor(plow[:, b, :], probs[:, b, :], p_hi[:, b], ALU.subtract).then_inc(plo_ready, 1)

                def k_lo(g, c, j, par):
                    k = g * NITEM + c * CT + j
                    dve.wait_ge(hi_done, k + 1)
                    for e, (a, b, a2, b2) in enumerate(((0, DH, DH, P), (DH, P, 0, DH))):
                        last = nc.vector.tensor_tensor(k1[a2:b2, par, e::2, j, :],
                                                       proj[a:b, 0:2 * P].rearrange("p (n k) -> p n k", k=P),
                                                       k1[a:b, par, e::2, j, :].bitcast(F32), ALU.subtract)
                    last.then_inc(lo_done, 1)

                def add_out(u, h):
                    dve.wait_ge(o_ready, u + 1)
                    nc.vector.tensor_tensor(oacc[:, h, :], outs[:, :], oacc[:, h, :], ALU.add).then_inc(o_added, 1)

                ITEM_LINKS = 3 if QK_NORM else 1
                Q_LINKS = 6
                FIN_LINKS = 4
                NULL_LINKS = 0 if QK_NORM else 6
                PER_GROUP = NITEM * ITEM_LINKS + Q_LINKS + QT * FIN_LINKS
                dve.wait_ge(consts, 6 + 2 * GH)
                for s in (lo_done, o_added, fin_read):
                    dve.sem_inc(s, ONE)
                if L == 1:
                    link = Steps(dve, steps_s, 0)
                    link(nc.vector.tensor_copy(nullc[:, 0:1].bitcast(R32), col[:, 1:2]))
                    link(nc.vector.tensor_tensor(nullc[:, 1:2], col[:, 1:2], nullc[:, 0:1], ALU.subtract))
                    nc.vector.tensor_copy(nullc[0:DH, 2:3], nullc[0:DH, 0:1])
                    nc.vector.tensor_copy(nullc[DH:P, 2:3], nullc[DH:P, 1:2])
                    link(nc.vector.tensor_copy(nullc[0:DH, 3:4], nullc[0:DH, 1:2]))
                    link(nc.vector.tensor_copy(nullc[DH:P, 3:4], nullc[DH:P, 0:1]))
                    link(nc.vector.tensor_copy(null16[:, 0:DH], row[0:1, 2, 0:DH]))
                    nc.vector.tensor_tensor(nullv[:, 0, :], row[0:1, 2, 0:DH], null16[:, 0:DH], ALU.subtract).then_inc(null_fix, 1)
                    dve.wait_ge(null_fix, 1)
                    link(nc.vector.tensor_scalar(null16[:, DH:P], nullv[:, 0, :], LIFT, None, ALU.mult))
                    nc.vector.tensor_copy(null32[:, :], null16[:, :]).then_inc(null_fix, 1)
                with dve.Fori(0, NG) as g:
                    link0 = g * PER_GROUP + NULL_LINKS
                    for j in range(CT):
                        link = Steps(dve, steps_s, link0 + ITEM_LINKS * j)
                        if QK_NORM:
                            k_var(g, 0, j, link)
                            k_scale(g, 0, j)
                        v_lo(g, 0, j, 0, link)
                        k_lo(g, 0, j, 0)
                    link = Steps(dve, steps_s, link0 + ITEM_LINKS * CT)
                    rows = [P, QT * GH, DH]
                    dve.wait_ge(q_rows, g + 1)
                    if QK_NORM:
                        link(nc.vector.tensor_tensor(qsq[:, :, :], qf, qf, ALU.mult))
                        link(nc.vector.tensor_reduce(qst[:, 0, :], qsq[:, :, :], AX.X, ALU.add))
                        nc.vector.tensor_scalar(qst[:, 1, :], qst[:, 0, :], 1.0 / DH, 1e-16, ALU.mult, ALU.max).then_inc(q_var, 1)
                        dve.wait_ge(q_rstd, g + 1)
                        link(nc.vector.tensor_tensor(qf, qf, over(qst[:, 2, :], rows), ALU.mult))
                        nc.vector.tensor_tensor(qf, qf, row[:, 1:2, 0:DH].broadcast_to(rows), ALU.mult).then_inc(q_final, 1)
                    else:
                        dve.sem_inc(q_final, 1)
                    dve.wait_ge(q_final, g + 1)
                    link(nc.vector.tensor_tensor(qsq[:, :, :], qf, qf, ALU.mult))
                    link(nc.vector.tensor_reduce(qst[:, 0, :], qsq[:, :, :], AX.X, ALU.add))
                    link(nc.vector.tensor_tensor(qst[:, 3, :].rearrange("p (t h) -> p t h", h=GH),
                                                 qst[:, 0, :].rearrange("p (t h) -> p t h", h=GH),
                                                 kbound2[:, bass.ds(g * GH, GH)].unsqueeze(1).broadcast_to([P, QT, GH]), ALU.mult))
                    nc.vector.tensor_scalar(qst[:, 1, :], qst[:, 3, :], 1e-30, None, ALU.max).then_inc(q_c2, 1)
                    dve.wait_ge(q_c, g + 1)
                    if not QK_NORM:
                        link(nc.vector.tensor_tensor(qsq[:, :, :], qf, row[:, 1:2, 0:DH].broadcast_to(rows), ALU.mult))
                        link(nc.vector.tensor_reduce(qst[:, 0, :], qsq[:, :, :], AX.X, ALU.add))
                        link(nc.vector.tensor_tensor(qst[:, 2, :], qst[:, 0, :], qst[:, 2, :], ALU.max))
                    dve.wait_ge(q_hi, 4 * (g + 1))
                    q4 = qf.rearrange("p (t h) d -> p t h d", h=GH)
                    c4 = qst[:, 2, :].rearrange("p (t h) -> p t h", h=GH)
                    for e in range(2):
                        at, cat = (0, DH) if e == 0 else (DH, 0)
                        for n in range(2):
                            nc.vector.tensor_tensor(qb[:, 4 * n:4 * n + 4, e::2, at:at + DH], q4[:, 4 * n:4 * n + 4, e::2, :],
                                                    qa[n][:, :, e::2, 0:DH].bitcast(F32), ALU.subtract)
                        last = nc.vector.tensor_scalar(qb[:, :, e::2, cat], c4[:, :, e::2], -1.0, None, ALU.mult)
                    last.then_inc(q_lo, 1)
                    for h in range(GH):
                        dve.wait_ge(qt_done, g * (2 * GH) + 2 * h + 2)
                        nc.vector.tensor_copy(q2[:, h, :], scores[:, 1, :]).then_inc(q2_read, 1)
                    hold(dve, o_zero, g + 1)
                    p_lo(g * NSTEP, 0)
                    with dve.Fori(0, PAIRS) as i:
                        for half in range(2):
                            for h in range(GH):
                                n = half * GH + h
                                s0 = g * NSTEP + i * (2 * CT * GH) + n * CT
                                item = (g, i * 2 + half + 1, h)
                                link = Steps(dve, steps_s, link0 + ITEM_LINKS * CT + Q_LINKS
                                             + i * (2 * CT * ITEM_LINKS) + n * ITEM_LINKS)
                                p_lo(s0 + 1, 1)
                                if QK_NORM:
                                    k_var(*item, link)
                                p_lo(s0 + 2, 0)
                                if QK_NORM:
                                    k_scale(*item)
                                v_lo(*item, 1 - half, link)
                                p_lo(s0 + 3, 1)
                                k_lo(*item, 1 - half)
                                p_lo(s0 + 4, 0)
                                add_out(g * NUNIT + i * (2 * GH) + n, h)
                    if L == 1:
                        dve.wait_ge(k2_done, (g + 1) * (2 * NITEM))
                        dve.wait_ge(lo_done, ONE + (g + 1) * NITEM)
                        at = CTX_REST
                        for e in range(2):
                            nc.vector.tensor_copy(k1[:, 0, e::2, TAIL - 1, at:at + 1],
                                                  nullc[:, 2 + e:3 + e].unsqueeze(1).broadcast_to([P, GH // 2, 1]))
                            a, b = (0, DH) if e == 0 else (DH, P)
                            last = nc.vector.tensor_copy(k2[a:b, 0, e::2, TAIL - 1, at:at + 1],
                                                         nullc[a:b, 0:1].unsqueeze(1).broadcast_to([DH, GH // 2, 1]))
                        last.then_inc(null_fix, 1)
                    for n in range(1, GH * TAIL):
                        p_lo(g * NSTEP + NFULL * CT * GH + n, n % 2)
                        if n % TAIL == 0:
                            add_out(g * NUNIT + NFULL * GH + n // TAIL - 1, n // TAIL - 1)
                    add_out(g * NUNIT + NFULL * GH + GH - 1, GH - 1)
                    link = Steps(dve, steps_s, link0 + NITEM * ITEM_LINKS + Q_LINKS)
                    for t in range(QT):
                        dve.wait_ge(fin_mm, g * QT + t + 1)
                        src = fin_ps[:, t % 2]
                        link(nc.vector.reciprocal(frec[:, :].rearrange("p (k h) -> p k h", k=2),
                                                  src[:, :, 0:2 * (D + 1)].rearrange("p k (h n) -> p k h n", h=2)[:, :, :, D]))
                        for k in range(2):
                            last = nc.vector.tensor_tensor(
                                fin[:, 2 * k:2 * k + 2, :], src[:, k, 0:2 * (D + 1)].rearrange("p (h n) -> p h n", h=2)[:, :, 0:D],
                                over(frec[:, 2 * k:2 * k + 2], [P, 2, D]), ALU.mult)
                        last.then_inc(fin_read, 1)
                        dve.wait_ge(fin_read, ONE + g * QT + t + 1)
                        link(nc.vector.tensor_tensor(fin[:, 0:2, :], fin[:, 0:2, :], fin[:, 2:4, :], ALU.add))
                        link(nc.vector.tensor_tensor(fsum, fin[:, 0, :], fin[:, 1, :], ALU.add))
                        link(nc.vector.tensor_tensor(Y[:, t, :], fsum, Y[:, t, :], ALU.add))

            @block.tensor
            def _(pe):
                def project_kv(g, c, j, par, loads):
                    k = g * NITEM + c * CT + j
                    pe.wait_ge(lo_done, ONE + k)
                    if j == 0:
                        pe.wait_ge(xc_in[par], loads * 16)
                    nc.tensor.matmul(proj[:, :], xc[:, par, j * P:(j + 1) * P],
                                     w_kv[:, bass.ds(g, 1), :, :].rearrange("p g a n -> p (g a n)"),
                                     start=True, stop=True).then_inc(kv_done, 1)

                def transpose_k(g, c, j):
                    k = g * NITEM + c * CT + j
                    pe.wait_ge(kn_ready if QK_NORM else kv_read, k + 1)
                    for n in range(GH // 2):
                        last = nc.tensor.transpose(proj[:, n * P:(n + 1) * P],
                                                   krow[:, 2 * n:2 * n + 2, :].rearrange("p h d -> p (h d)"), ident[:, :])
                    last.then_inc(kt_done, 1)

                def score(b, h, t, par, item=None):
                    if item is not None:
                        pe.wait_ge(lo_done, ONE + item + 1)
                        pe.wait_ge(k2_done, 2 * item + 2)
                    for kk, qq, first in ((k1, q1, True), (k2, q2, False)):
                        for n in range(NQ // 512):
                            last = nc.tensor.matmul(scores[:, b, n * 512:(n + 1) * 512], kk[:, par, h, t, :],
                                                    qq[:, h, n * 512:(n + 1) * 512], start=first, stop=not first)
                    last.then_inc(s_ready, 1)

                def mix(s, b, h, t, par, last_t, u, item=None):
                    if item is not None:
                        pe.wait_ge(v_ready, item + 1)
                    pe.wait_ge(p_ready, s + 1)
                    if t == 0:
                        pe.wait_ge(o_added, ONE + u)
                    halves = [slice(n * 512, (n + 1) * 512) for n in range(NQ // 512)]
                    for q in halves:
                        nc.tensor.matmul(outs[:, q], v16[:, par, h, t, :], p_hi[:, b, q], start=t == 0, stop=False)
                    for n, q in enumerate(halves):
                        j = 32 * (2 * n + t % 2)
                        last_e = nc.tensor.matmul(last_ps[j:j + 32, :], vlast[:, par, h, t, :], p_hi[:, b, q],
                                                  start=False, stop=True, skip_group_check=True)
                    pe.wait_ge(plo_ready, s + 1)
                    for q in halves:
                        last = nc.tensor.matmul(outs[:, q], v32[:, par, h, t, :], plow[:, b, q],
                                                start=False, stop=t == last_t)
                    if t == last_t:
                        last.then_inc(o_ready, 1)
                    return last_e

                pe.wait_ge(consts, 6 + 2 * GH)
                pe.sem_inc(kv_done, ONE)
                with pe.Fori(0, NG) as g:
                    pe.wait_ge(fin_read, ONE + g * QT)
                    for t in range(QT):
                        last = nc.tensor.matmul(qps[:, t * GH:(t + 1) * GH, :].rearrange("p h d -> p (h d)"),
                                                lnT[:, t * P:(t + 1) * P], w_q[:, bass.ds(g * (GH * DH), GH * DH)],
                                                start=t % 2 == 0, stop=True, skip_group_check=True)
                    last.then_inc(q_mm, 1)
                    for j in range(CT):
                        project_kv(g, 0, j, 0, g * (PAIRS + 1) + 1)
                        transpose_k(g, 0, j)
                    pe.wait_ge(q_lo, g + 1)
                    for h in range(GH):
                        if h:
                            pe.wait_ge(q1_read, g * GH + h)
                        for t in range(QT):
                            last = nc.tensor.transpose(scores[:, 0, t * P:(t + 1) * P],
                                                       qa[t // 4][:, t % 4, h, :].bitcast(F32), ident[:, :])
                        last.then_inc(qt_done, 1)
                        if h:
                            pe.wait_ge(q2_read, g * GH + h)
                        for t in range(QT):
                            last = nc.tensor.transpose(scores[:, 1, t * P:(t + 1) * P], qb[:, t, h, :], ident[:, :])
                        last.then_inc(qt_done, 1)
                    pe.wait_ge(q1_read, (g + 1) * GH)
                    pe.wait_ge(q2_read, (g + 1) * GH)
                    score(0, 0, 0, 0, g * NITEM)
                    pe.wait_ge(e_read, ONE + g)
                    for j in range(4):
                        nc.tensor.matmul(last_ps[32 * j:32 * j + 32, :], zero32[:, :], vlast[:, 0, :, :, :].rearrange("p h t k -> p (h t k)"),
                                         start=True, stop=True, skip_group_check=True)
                    with pe.Fori(0, PAIRS) as i:
                        for half in range(2):
                            for h in range(GH):
                                for t in range(CT):
                                    n = (half * GH + h) * CT + t
                                    s = g * NSTEP + i * (2 * GH * CT) + n
                                    n2 = n + 1
                                    half2, h2, t2 = n2 // (GH * CT), n2 // CT % GH, n2 % CT
                                    item = g * NITEM + i * (2 * CT) + half2 * CT + t2 if h2 == 0 else None
                                    score(n2 % 2, h2, t2, half2 % 2, item)
                                    if t == 0:
                                        project_kv(g, i * 2 + half + 1, h, 1 - half,
                                                   g * (PAIRS + 1) + i + 2 if half else g * PAIRS + i + 1)
                                    if t == CT - 1:
                                        transpose_k(g, i * 2 + half + 1, h)
                                    mix(s, n % 2, h, t, half, CT - 1, g * NUNIT + i * (2 * GH) + half * GH + h,
                                        g * NITEM + i * (2 * CT) + half * CT + t if h == 0 else None)
                    for h in range(GH):
                        for t in range(TAIL):
                            n = h * TAIL + t
                            n2 = n + 1
                            if n2 < GH * TAIL:
                                h2, t2 = n2 // TAIL, n2 % TAIL
                                if L == 1 and n2 == TAIL - 1:
                                    pe.wait_ge(null_fix, 2 + g + 1)
                                    pe.wait_ge(null_in, (g + 1) * (16 * 3 * GH))
                                score(n2 % 2, h2, t2, 0, g * NITEM + NFULL * CT + t2 if h2 == 0 else None)
                            last_e = mix(g * NSTEP + NFULL * CT * GH + n, n % 2, h, t, 0, TAIL - 1,
                                         g * NUNIT + NFULL * GH + h,
                                         g * NITEM + NFULL * CT + t if h == 0 else None)
                    last_e.then_inc(e_done, 1)
                    pe.wait_ge(o_added, ONE + (g + 1) * NUNIT)
                    pe.wait_ge(e_read, ONE + g + 1)
                    pe.wait_ge(we_in, (g + 1) * (16 * 4 * GH))
                    for t in range(QT):
                        if t >= 2:
                            pe.wait_ge(fin_read, ONE + g * QT + t - 1)
                        e0 = DH * (t // 4)
                        for h in range(GH):
                            at = (h % 2) * (D + 1)
                            nc.tensor.matmul(fin_ps[:, t % 2, h // 2, at:at + D + 1],
                                             oacc[:, h, t * P:(t + 1) * P],
                                             w_o[:, bass.ds(g * GH + h, 1), :].rearrange("p h n -> p (h n)"),
                                             start=h % 2 == 0, stop=False, skip_group_check=True)
                            last = nc.tensor.matmul(fin_ps[:, t % 2, h // 2, at:at + D],
                                                    esb[e0:e0 + DH, (t % 4) * P:(t % 4 + 1) * P], w_e[e0:e0 + DH, h, :],
                                                    start=False, stop=True, skip_group_check=True)
                        last.then_inc(fin_mm, 1)

        end_step, var2, rstd2 = sem("end_step"), sem("var2"), sem("rstd2")
        with nc.Block() as block:
            @block.gpsimd
            def _(pool):
                if L == 1:
                    rstd(pool, QT, var2, rstd2, 1)

            @block.vector
            def _(dve):
                step = Steps(dve, end_step)
                full = [P, QT, D]
                if L == 1:
                    step(nc.vector.tensor_reduce(stat[:, 0, 0:QT], Y[:, :, :], AX.X, ALU.max))
                    step(nc.vector.reciprocal(stat[:, 1, 0:QT], stat[:, 0, 0:QT]))
                    step(nc.vector.tensor_tensor(Y[:, :, :], Y[:, :, :], over(stat[:, 1, 0:QT], full), ALU.mult))
                    layer_norm(dve, step, Y[:, :, :], Y[:, :, :], sqz[:, :, :], QT, var2, rstd2, 1)
                op = ALU.add if L == 0 else ALU.mult
                step(nc.vector.tensor_tensor(Y[:, :, :], Y[:, :, :], row[:, 0:1, :].broadcast_to(full), op))
                step(nc.vector.scalar_tensor_tensor(out=X[:, :, :], in0=Y[:, :, :], scalar=gates[:, L:L + 1],
                                                    in1=X[:, :, :], op0=ALU.mult, op1=ALU.add))


def moe_layer(nc, A, L, sem_, sb_, layer_norm, rstd, out, B):
    X, Y, Z, sqz, stat, ident, lnT = (B[n] for n in ("X", "Y", "Z", "sqz", "stat", "ident", "lnT"))
    gates, scores, outs, proj, spare = (B[n] for n in ("gates", "scores", "outs", "proj", "spare"))
    FH = 512 if L == 0 else 64
    FC = NE * FH // P
    FE = FH // P if L == 0 else 1
    KH = P if L == 0 else FH
    NAME = "L%d_ffn_" % L

    def sem(name):
        return sem_("m%d_%s" % (L, name))

    scope = ExitStack()
    with scope:
        def sb(name, shape, dt=F32):
            return sb_("m%d_%s" % (L, name), shape, dt, scope)
        w1 = sb("w1", [P, NE * FH])
        w2 = sb("w2", [P, FC, D])
        wg = sb("wg", [P, NE])
        hid = sb("hidden", [P, 4 if L == 0 else 1, NQ])
        logit = sb("logit", [P, QT, NE])
        top = sb("top", [P, QT, NE])
        topi = sb("top_index", [P, QT, NE], U32)
        topf = sb("top_index_f", [P, QT, 2])
        ids = sb("expert_ids", [P, NE])
        gate = sb("gate", [P, 3, QT])
        one = sb("one_hot", [P, 2, QT, NE])
        comb = sb("combine", [P, QT, NE])

        w_in, step_s, var, rs, z_ready = (sem(s) for s in ("w_in", "step", "var", "rstd", "z_ready"))
        zt_done, zt_read, lg_done, e_in, e_out, ids_ok = (sem(s) for s in ("zt_done", "zt_read", "lg_done", "e_in", "e_out", "ids"))
        h_done, h_read, y_done, y_read, out_in = (sem(s) for s in ("h_done", "h_read", "y_done", "y_read", "out"))
        NH = FC // (4 if L == 0 else 1)
        HT = FC // NH
        EPR = NE // NH
        zt_ps = scores[:, 0, :]
        h_ps = scores
        y_ps = [proj, spare]

        with nc.Block() as block:
            @block.sync
            def _(sp):
                sp.dma_start(wg[:, :], A[NAME + "gateT"]).then_inc(w_in, 16)
                sp.dma_start(w1[:, :], A[NAME + "w1T"]).then_inc(w_in, 16)
                sp.dma_start(w2[:, :, :], A[NAME + "w2T"]).then_inc(w_in, 16)
                if L == 1:
                    sp.wait_ge(y_read, 2 * NE)
                    sp.dma_start(out.rearrange("(t p) d -> p t d", p=P), X[:, :, :]).then_inc(out_in, 16)
                    sp.wait_ge(out_in, 16)

            @block.gpsimd
            def _(pool):
                nc.gpsimd.iota(ids[:, :], [[1, NE]], base=0, channel_multiplier=0,
                               allow_small_or_imprecise_dtypes=True).then_inc(ids_ok, 1)
                rstd(pool, QT, var, rs, 1)

            @block.scalar
            def _(act):
                act.wait_ge(zt_done, 1)
                nc.scalar.activation(lnT[:, :], zt_ps, ACT.Copy).then_inc(zt_read, 1)
                act.wait_ge(e_in, 1)
                nc.scalar.activation(gate[:, 0, :], gate[:, 0, :], ACT.Exp).then_inc(e_out, 1)
                for n in range(NH):
                    for j in range(HT):
                        k = n * HT + j
                        act.wait_ge(h_done, k + 1)
                        if n and j == 0:
                            act.wait_ge(y_done, n * (2 * EPR))
                        nc.scalar.activation(hid[:, j, :], h_ps[:, k % 2, :],
                                             ACT.Relu if L == 0 else ACT.Gelu).then_inc(h_read, 1)

            @block.vector
            def _(dve):
                step = Steps(dve, step_s)
                layer_norm(dve, step, X[:, :, :], Z[:, :, :], sqz[:, :, :], QT, var, rs, 1)
                dve.sem_inc(z_ready, 1)
                dve.wait_ge(lg_done, 1)
                step(nc.vector.tensor_copy(logit[:, :, :], proj[:, 0:QT * NE].rearrange("p (t e) -> p t e", e=NE)))
                for t in range(QT):
                    nc.vector.max(top[:, t, :], logit[:, t, :]).then_inc(step_s, 1)
                step.n += QT
                dve.wait_ge(step_s, step.n)
                for t in range(QT):
                    nc.vector.max_index(topi[:, t, :], top[:, t, :], logit[:, t, :]).then_inc(step_s, 1)
                step.n += QT
                dve.wait_ge(step_s, step.n)
                step(nc.vector.tensor_copy(topf[:, :, :], topi[:, :, 0:2]))
                nc.vector.tensor_tensor(gate[:, 0, :], top[:, :, 1], top[:, :, 0], ALU.subtract).then_inc(e_in, 1)
                dve.wait_ge(e_out, 1)
                step(nc.vector.tensor_scalar(gate[:, 1, :], gate[:, 0, :], 1.0, None, ALU.add))
                step(nc.vector.reciprocal(gate[:, 2, :], gate[:, 1, :]))
                step(nc.vector.tensor_tensor(gate[:, 1, :], gate[:, 0, :], gate[:, 2, :], ALU.mult))
                dve.wait_ge(ids_ok, 1)
                full = [P, QT, NE]
                for k, w in ((0, 2), (1, 1)):
                    step(nc.vector.tensor_tensor(one[:, k], ids[:, :].unsqueeze(1).broadcast_to(full),
                                                 over(topf[:, :, k], full), ALU.is_equal))
                    step(nc.vector.tensor_tensor(one[:, k], one[:, k], over(gate[:, w, :], full), ALU.mult))
                step(nc.vector.tensor_tensor(comb[:, :, :], one[:, 0], one[:, 1], ALU.add))
                step(nc.vector.tensor_scalar(comb[:, :, :], comb[:, :, :], gates[:, 2 + L:3 + L], None, ALU.mult))
                for n in range(NE):
                    for half in range(2):
                        k = n * 2 + half
                        dve.wait_ge(y_done, k + 1)
                        for t in range(4):
                            q = half * 4 + t
                            last = nc.vector.scalar_tensor_tensor(
                                out=X[:, q, :], in0=y_ps[k % 2][:, t * P:(t + 1) * P], scalar=comb[:, q, n:n + 1],
                                in1=X[:, q, :], op0=ALU.mult, op1=ALU.add)
                        last.then_inc(y_read, 1)
                        dve.wait_ge(y_read, k + 1)

            @block.tensor
            def _(pe):
                pe.wait_ge(z_ready, 1)
                for t in range(QT):
                    last = nc.tensor.transpose(zt_ps[:, t * P:(t + 1) * P], Z[:, t, :], ident[:, :])
                last.then_inc(zt_done, 1)
                pe.wait_ge(zt_read, 1)
                pe.wait_ge(w_in, 48)
                for t in range(QT):
                    last = nc.tensor.matmul(proj[:, t * NE:(t + 1) * NE], lnT[:, t * P:(t + 1) * P], wg[:, :],
                                            start=True, stop=True, skip_group_check=True)
                last.then_inc(lg_done, 1)

                def hidden(k):
                    if k >= 2:
                        pe.wait_ge(h_read, k - 1)
                    for c in range(NQ // 512):
                        last = nc.tensor.matmul(h_ps[:, k % 2, c * 512:(c + 1) * 512], w1[:, k * P:(k + 1) * P],
                                                lnT[:, c * 512:(c + 1) * 512], start=True, stop=True)
                    last.then_inc(h_done, 1)

                hidden(0)
                hidden(1)
                for n in range(NH):
                    for j in range(2, HT):
                        hidden(n * HT + j)
                    for e in range(EPR):
                        for half in range(2):
                            k = (n * EPR + e) * 2 + half
                            if e == 0 and half == 0:
                                pe.wait_ge(h_read, (n + 1) * HT)
                            if k == 0:
                                pe.wait_ge(step_s, 6 + 1)
                            if k >= 2:
                                pe.wait_ge(y_read, k - 1)
                            a = 0 if L == 0 else e * FH
                            for t in range(4):
                                q = half * 4 + t
                                for j in range(FE):
                                    last = nc.tensor.matmul(
                                        y_ps[k % 2][:, t * P:(t + 1) * P], hid[a:a + KH, j, q * P:(q + 1) * P],
                                        w2[a:a + KH, n * HT + j, :], start=t == 0 and j == 0, stop=j == FE - 1,
                                        skip_group_check=True)
                            last.then_inc(y_done, 1)
                    if n + 1 < NH:
                        for j in range(min(2, HT)):
                            k = (n + 1) * HT + j
                            if L == 0 or k >= 2:
                                hidden(k)


_OUT = ((1, NQ, D), "float32")


def kernel(**inputs):
    import numpy as np
    import concourse.bacc as bacc
    from concourse.bass_utils import run_bass_kernel_spmd as run

    inp = {k: np.asarray(a) for k, a in inputs.items()}
    lay = {
        "x": inp["x"][0], "ctx": inp["ctx_1024"][0], "mask": inp["mask_BxS2_bf1"][0].view(np.uint8),
        "g_xattn": inp["g_xattn"], "g_ffn": inp["g_ffn"],
        "L0_ffn_gateT": inp["L0_ffn_gate_w"].T, "L1_ffn_gateT": inp["L1_ffn_w_gate"].T,
        "L0_ffn_w1T": inp["L0_ffn_w1"].reshape(-1, D).T, "L1_ffn_w1T": inp["L1_ffn_w_fc"].reshape(-1, D).T,
        "L0_ffn_w2T": inp["L0_ffn_w2"].transpose(0, 2, 1).reshape(-1, P, D).transpose(1, 0, 2),
        "L1_ffn_w2T": inp["L1_ffn_w_proj"].transpose(0, 2, 1).reshape(-1, P, D).transpose(1, 0, 2),
    }
    for k, a in inp.items():
        if "xattn_" in k and k[0] == "L":
            lay[k] = a
    nc = bacc.Bacc("TRN2", target_bir_lowering=False, num_devices=1)
    arrays, A = {}, {}
    for name, a in lay.items():
        a = np.ascontiguousarray(a)
        arrays["in_" + name] = a
        A[name] = nc.dram_tensor("in_" + name, a.shape, mybir.dt.from_np(a.dtype), kind="ExternalInput").ap()
    out = nc.dram_tensor("out", (NQ, D), F32, kind="ExternalOutput").ap()
    flamingo(nc, A, out)
    r = run(nc, [arrays], core_ids=[0])
    return r.results[0]["out"].reshape(_OUT[0])
```

```python
import concourse.bass as bass
from concourse import mybir
from contextlib import ExitStack

F32, R32, F16, B16 = mybir.dt.float32, mybir.dt.float32r, mybir.dt.float16, mybir.dt.bfloat16
U8, U32 = mybir.dt.uint8, mybir.dt.uint32
ALU = mybir.AluOpType
ACT = mybir.ActivationFunctionType
AX = mybir.AxisListType
RADD = bass.bass_isa.ReduceOp.add
RMAX = bass.bass_isa.ReduceOp.max

P = 128
D = 128
NQ = 1024
QT = NQ // P
NCTX = 6404
CTX_FULL = NCTX // P
CTX_REST = NCTX - CTX_FULL * P
H, DH = 16, 64
GH = 4
NG = H // GH
CT = 4
NB = 4
TAIL = 3
NE = 8
LN_EPS = 1e-5
LIFT = 2.0 ** 11
SCALE = DH ** -0.5


class Steps:

    def __init__(self, eng, sem, base=0):
        self.eng, self.sem, self.base, self.n = eng, sem, base, 0

    def __call__(self, ins):
        ins.then_inc(self.sem, 1)
        self.n += 1
        self.eng.wait_ge(self.sem, self.base + self.n)


def over(ap, shape):
    return ap.unsqueeze(2).broadcast_to(shape)


def flamingo(nc, A, out):
    ctx = ExitStack()
    with ctx:
        def sb(name, shape, dt=F32, to=ctx):
            return to.enter_context(nc.sbuf_tensor(name, shape, dt))

        def sem(name):
            return ctx.enter_context(nc.semaphore(name))

        X = sb("residual", [P, QT, D])
        Y = sb("branch", [P, QT, D])
        Z = sb("normed", [P, QT, D])
        sqz = sb("squares", [P, QT, D])
        lnT = sb("normed_T", [P, NQ])
        stat = sb("stat", [P, 4, 64])
        ident = sb("identity", [P, P])
        mhalf = sb("minus_half", [P, 64])
        phalf = sb("plus_half", [P, 64])
        gates = sb("gates", [P, 4])
        scores = ctx.enter_context(nc.psum_tensor("scores_ps", [P, 2, NQ], F32))
        outs = ctx.enter_context(nc.psum_tensor("out_ps", [P, NQ], F32))
        proj = ctx.enter_context(nc.psum_tensor("proj_ps", [P, 512], F32))
        spare = ctx.enter_context(nc.psum_tensor("spare_ps", [P, 512], F32))

        loaded, made, gated = sem("x_loaded"), sem("const_made"), sem("gates_ready")
        with nc.Block() as block:
            @block.sync
            def _(sp):
                sp.dma_start(X[:, :, :], A["x"].rearrange("(t p) d -> p t d", p=P)).then_inc(loaded, 16)
                sp.dma_start(gates[:, 0:2], A["g_xattn"].partition_broadcast(P)).then_inc(loaded, 16)
                sp.dma_start(gates[:, 2:4], A["g_ffn"].partition_broadcast(P)).then_inc(loaded, 16)
                sp.wait_ge(loaded, 48)

            @block.gpsimd
            def _(pool):
                step = Steps(pool, made)
                step(nc.gpsimd.memset(mhalf[:, :], -0.5))
                step(nc.gpsimd.memset(phalf[:, :], 0.5))
                step(nc.gpsimd.memset(ident[:, :], 0.0))
                step(nc.gpsimd.affine_select(out=ident[:, :], in_=ident[:, :], compare_op=ALU.not_equal,
                                             fill=1.0, base=0, pattern=[[-1, P]], channel_multiplier=1))

            @block.scalar
            def _(act):
                act.wait_ge(loaded, 48)
                nc.scalar.activation(gates[:, :], gates[:, :], ACT.Tanh).then_inc(gated, 1)

        def layer_norm(dve, step, x, dst, sq, T, var_ready, rstd_ready, n):
            shape = [P, T, D]
            step(nc.vector.tensor_reduce(stat[:, 0, 0:T], x, AX.X, ALU.add))
            step(nc.vector.tensor_scalar(stat[:, 1, 0:T], stat[:, 0, 0:T], 1.0 / D, None, ALU.mult))
            step(nc.vector.tensor_tensor(dst, x, over(stat[:, 1, 0:T], shape), ALU.subtract))
            step(nc.vector.tensor_tensor(sq, dst, dst, ALU.mult))
            step(nc.vector.tensor_reduce(stat[:, 2, 0:T], sq, AX.X, ALU.add))
            nc.vector.tensor_scalar(stat[:, 3, 0:T], stat[:, 2, 0:T], 1.0 / D, LN_EPS,
                                    ALU.mult, ALU.add).then_inc(var_ready, 1)
            dve.wait_ge(rstd_ready, n)
            step(nc.vector.tensor_tensor(dst, dst, over(stat[:, 0, 0:T], shape), ALU.mult))

        def rstd(pool, T, var_ready, rstd_ready, n):
            pool.wait_ge(var_ready, n)
            nc.gpsimd.tensor_tensor(stat[:, 0, 0:T], stat[:, 3, 0:T], mhalf[:, 0:T],
                                    ALU.pow).then_inc(rstd_ready, 1)

        for L in range(2):
            attention_layer(nc, A, L, sem, sb, layer_norm, rstd,
                            dict(X=X, Y=Y, Z=Z, sqz=sqz, lnT=lnT, stat=stat, ident=ident, mhalf=mhalf,
                                 phalf=phalf, gates=gates, scores=scores, outs=outs, proj=proj, spare=spare))
            moe_layer(nc, A, L, sem, sb, layer_norm, rstd, out,
                      dict(X=X, Y=Y, Z=Z, sqz=sqz, lnT=lnT, stat=stat, ident=ident, mhalf=mhalf,
                           gates=gates, scores=scores, outs=outs, proj=proj, spare=spare))


ONLY = dict(kn_var=0, kn_rstd=0, kn_ready=0, q_var=0, q_rstd=0, mask_f=0, mask_in=0,
            bnd_in=1, bnd_out=1, null_in=1, null_fix=1, var2=1, rstd2=1)


def attention_layer(nc, A, L, sem_, sb_, layer_norm, rstd, B):
    X, Y, Z, sqz, stat, ident = B["X"], B["Y"], B["Z"], B["sqz"], B["stat"], B["ident"]
    mhalf, phalf, gates = B["mhalf"], B["phalf"], B["gates"]
    scores, outs, proj = B["scores"], B["outs"], B["proj"]
    QK_NORM = L == 0
    LAT0 = CTX_FULL
    REST = CTX_FULL + (QT if L == 0 else 0)
    NTILES = REST + 1
    NFULL = (NTILES - TAIL) // CT
    PAIRS = NFULL // 2
    assert NFULL * CT + TAIL == NTILES and NFULL % 2 == 0
    PAD_TILES = (NFULL + 1) * CT
    NSTEP = NTILES * GH
    NITEM = PAD_TILES
    NUNIT = (NFULL + 1) * GH
    NAME = "L%d_xattn_" % L

    def sem(name):
        only = ONLY.get(name)
        return sem_("a%d_%s" % (L, name)) if only is None or only == L else None

    scope = ExitStack()
    with scope:
        def sb(name, shape, dt=F32, to=scope):
            return sb_("a%d_%s" % (L, name), shape, dt, to)

        xT = sb("keys_in_T", [P, (PAD_TILES + CT) * P])
        w_q = sb("w_q", [P, (H + GH) * DH])
        w_o = sb("w_o", [P, H, D + 1])
        w_e = sb("w_e", [P, GH, D]) if L == 1 else B["lnT"][:, 0:GH * D].rearrange("p (h n) -> p h n", h=GH)
        mask = sb("key_mask", [P, PAD_TILES])
        kbound2 = sb("key_bound2", [P, H])
        row = sb("rows", [P, 4, D])
        col = sb("cols", [P, 4])
        lnT = xT[:, LAT0 * P:(LAT0 + QT) * P] if L == 0 else B["lnT"][:, :]

        w_in, c_in = sem("weights_in"), sem("ctx_in")
        ln_step, var_ready, rstd_ready = sem("ln_step"), sem("var_ready"), sem("rstd_ready")
        lat_ready, ctx_ready, zeroed = sem("lat_ready"), sem("ctx_ready"), sem("zeroed")
        tr_done, tr_read = sem("tr_done"), sem("tr_read")
        mask_f, prep_pool, bnd_in, bnd_out = sem("mask_f"), sem("prep_pool"), sem("bnd_in"), sem("bnd_out")
        mask_in = sem("mask_in")
        ln_parts = [(0, 17), (17, 34), (34, CTX_FULL + 1)]
        with ExitStack() as prep:
            w_k = sb("w_k", [P, H * DH], F32, prep) if L == 1 else None
            raw = sb("ctx_rows", [P, CTX_FULL + 1, D], F32, prep)
            sq = sb("ctx_sq", [P, 17, D], F32, prep)
            m8 = sb("mask_u8", [CTX_FULL, P], U8, prep)
            mf = sb("mask_f32", [CTX_FULL, P], F32, prep)
            m8r = sb("mask_rest_u8", [CTX_REST, 1], U8, prep)
            wsq = sb("w_sq", [P, H, DH], F32, prep)
            jobs = [("lat", list(range(i, i + 4)), i) for i in (0, 4)]
            jobs += [("ctx", list(range(i, min(i + 4, CTX_FULL))), i) for i in range(0, CTX_FULL, 4)]
            jobs += [("rest", [CTX_FULL], REST)]

            with nc.Block() as block:
                @block.sync
                def _(sp):
                    sp.wait_ge(zeroed, 1)
                    sp.dma_start(raw[:, 0:CTX_FULL, :],
                                 A["ctx"][0:CTX_FULL * P, :].rearrange("(t p) d -> p t d", p=P)).then_inc(c_in, 16)
                    sp.dma_start(raw[0:CTX_REST, CTX_FULL, :], A["ctx"][CTX_FULL * P:NCTX, :]).then_inc(c_in, 16)
                    if L == 0:
                        sp.dma_start(m8[:, :], A["mask"][0:CTX_FULL * P].rearrange("(t p) -> t p", p=P)).then_inc(mask_in, 16)
                        sp.dma_start(m8r[:, :], A["mask"][CTX_FULL * P:NCTX].unsqueeze(1)).then_inc(mask_in, 16)

                @block.scalar
                def _(act):
                    n = 0
                    W = A[NAME + "Wkv"]
                    if L == 1:
                        act.dma_start(w_k[:, :], W[:, 0:H * DH]).then_inc(w_in, 16)
                        n += 16
                    act.dma_start(w_q[:, 0:H * DH], A[NAME + "Wq"]).then_inc(w_in, 16)
                    w_rows = A[NAME + ("Wout" if L == 0 else "Wo")].rearrange("(h d) n -> d h n", d=DH)
                    act.dma_start(w_o[0:DH, :, 0:D], w_rows).then_inc(w_in, 16)
                    act.wait_ge(prep_pool, 7)
                    act.dma_start(w_o[DH:P - 1, :, 0:D], w_rows[0:DH - 1]).then_inc(w_in, 16)
                    n += 48
                    if L == 0:
                        for i, name in enumerate(("ln_x_g", "ln_x_b", "ln_l_g", "ln_l_b")):
                            act.dma_start(col[:, i:i + 1], A[NAME + name].unsqueeze(1)).then_inc(w_in, 16)
                        act.dma_start(row[:, 0, :], A[NAME + "bout"].partition_broadcast(P)).then_inc(w_in, 16)
                        act.dma_start(row[:, 1, 0:DH], A[NAME + "qn_g"].partition_broadcast(P)).then_inc(w_in, 16)
                        act.dma_start(row[:, 2, 0:DH], A[NAME + "kn_g"].partition_broadcast(P)).then_inc(w_in, 16)
                        n += 16 * 7
                    else:
                        act.dma_start(col[:, 0:1], A[NAME + "g_in"].unsqueeze(1)).then_inc(w_in, 16)
                        act.dma_start(row[:, 0, :], A[NAME + "g_out"].partition_broadcast(P)).then_inc(w_in, 16)
                        act.dma_start(row[:, 1, 0:DH], A[NAME + "null_kv"][0].partition_broadcast(P)).then_inc(w_in, 16)
                        act.dma_start(row[0:1, 2, 0:DH], A[NAME + "null_kv"][1:2, :]).then_inc(w_in, 16)
                        act.dma_start(col[0:DH, 1:2], A[NAME + "null_kv"][0].unsqueeze(1)).then_inc(w_in, 16)
                        act.dma_start(col[DH:P, 1:2], A[NAME + "null_kv"][0].unsqueeze(1)).then_inc(w_in, 16)
                        n += 16 * 6
                    act.wait_ge(w_in, n)
                    nc.scalar.activation(w_o[DH:P, :, 0:D], w_o[DH:P, :, 0:D], ACT.Copy, scale=1.0 / LIFT)
                    for i, (kind, tiles, at) in enumerate(jobs):
                        act.wait_ge(tr_done, i + 1)
                        w = len(tiles) * P
                        src = scores[:, i % 2, 0:w]
                        if kind == "lat":
                            dst = lnT[:, at * P:at * P + w]
                            if L == 0:
                                ins = nc.scalar.activation(dst, src, ACT.Identity, bias=col[:, 3:4], scale=col[:, 2:3])
                            else:
                                ins = nc.scalar.activation(dst, src, ACT.Copy, scale=col[:, 0:1])
                        else:
                            dst = xT[:, at * P:at * P + w]
                            if L == 0:
                                ins = nc.scalar.activation(dst, src, ACT.Identity, bias=col[:, 1:2], scale=col[:, 0:1])
                            else:
                                ins = nc.scalar.activation(dst, src, ACT.Copy)
                        ins.then_inc(tr_read, 1)

                @block.gpsimd
                def _(pool):
                    step = Steps(pool, prep_pool)
                    step(nc.gpsimd.memset(mask[:, :], 0.0))
                    nc.gpsimd.memset(raw[:, CTX_FULL, :], 0.0).then_inc(zeroed, 1)
                    step(nc.gpsimd.memset(xT[:, NTILES * P:(PAD_TILES + CT) * P], 0.0))
                    step(nc.gpsimd.memset(Y[:, :, :], 0.0))
                    step(nc.gpsimd.memset(w_q[:, H * DH:(H + GH) * DH], 0.0))
                    step(nc.gpsimd.memset(w_o[:, :, D:D + 1], 0.0))
                    step(nc.gpsimd.memset(w_o[DH:P, :, 0:D], 0.0))
                    step(nc.gpsimd.memset(w_e[:, :, :], 0.0))
                    step(nc.gpsimd.affine_select(out=w_o[:, :, D], in_=w_o[:, :, D], compare_op=ALU.not_equal,
                                                 fill=1.0, base=1 - P, pattern=[[0, H]], channel_multiplier=1))
                    if L == 0:
                        step(nc.gpsimd.memset(mask[:, LAT0:LAT0 + QT], LIFT))
                        step(nc.gpsimd.memset(kbound2[:, :], float(DH)))
                    else:
                        step(nc.gpsimd.memset(mask[:, 0:CTX_FULL], LIFT))
                        step(nc.gpsimd.memset(mask[0:CTX_REST + 1, REST:REST + 1], LIFT))
                    n = 0
                    for T in ([QT, QT] + ([b - a for a, b in ln_parts] if L == 0 else [])):
                        n += 1
                        rstd(pool, T, var_ready, rstd_ready, n)
                    if L == 1:
                        pool.wait_ge(bnd_in, 1)
                        nc.gpsimd.partition_all_reduce(stat[:, 1, 0:1], stat[:, 0, 0:1], P, RMAX).then_inc(bnd_out, 1)
                        nc.gpsimd.partition_all_reduce(stat[:, 1, 16:32], stat[:, 0, 16:32], P, RADD).then_inc(bnd_out, 1)

                @block.vector
                def _(dve):
                    step = Steps(dve, ln_step)
                    layer_norm(dve, step, X[:, :, :], Z[:, :, :], sqz[:, :, :], QT, var_ready, rstd_ready, 1)
                    if L == 1:
                        step(nc.vector.tensor_reduce(stat[:, 0, 0:QT], Z[:, :, :], AX.X, ALU.max))
                        step(nc.vector.reciprocal(stat[:, 1, 0:QT], stat[:, 0, 0:QT]))
                        step(nc.vector.tensor_tensor(Z[:, :, :], Z[:, :, :], over(stat[:, 1, 0:QT], [P, QT, D]), ALU.mult))
                    layer_norm(dve, step, Z[:, :, :], Z[:, :, :], sqz[:, :, :], QT, var_ready, rstd_ready, 2)
                    dve.sem_inc(lat_ready, 1)
                    dve.wait_ge(c_in, 32)
                    if L == 0:
                        for i, (a, b) in enumerate(ln_parts):
                            layer_norm(dve, step, raw[:, a:b, :], raw[:, a:b, :], sq[:, 0:b - a, :], b - a,
                                       var_ready, rstd_ready, 3 + i)
                            dve.sem_inc(ctx_ready, 1)
                        dve.wait_ge(mask_in, 32)
                        nc.vector.tensor_copy(mf[:, :], m8[:, :]).then_inc(mask_f, 1)
                        dve.wait_ge(prep_pool, 1)
                        nc.vector.tensor_scalar(mask[0:CTX_REST, REST:REST + 1], m8r[:, :], LIFT, None, ALU.mult).then_inc(mask_f, 1)
                        dve.wait_ge(tr_done, len(jobs) + 1)
                        nc.vector.tensor_scalar(mask[:, 0:CTX_FULL], outs[:, 0:CTX_FULL], LIFT, None, ALU.mult).then_inc(mask_f, 1)
                        dve.wait_ge(w_in, 16 * 10)
                        step(nc.vector.tensor_tensor(row[:, 3, 0:DH], row[:, 1, 0:DH], row[:, 2, 0:DH], ALU.mult))
                        step(nc.vector.tensor_scalar(row[:, 1, 0:DH], row[:, 3, 0:DH], SCALE, None, ALU.mult))
                    else:
                        for i, (a, b) in enumerate(ln_parts):
                            step(nc.vector.tensor_tensor(sq[:, 0:b - a, :], raw[:, a:b, :], raw[:, a:b, :], ALU.mult))
                            step(nc.vector.tensor_reduce(stat[:, 2, a:b], sq[:, 0:b - a, :], AX.X, ALU.add))
                        step(nc.vector.tensor_reduce(stat[:, 0, 0:1], stat[:, 2, 0:CTX_FULL + 1], AX.X, ALU.max))
                        dve.wait_ge(w_in, 16 * (1 + 9))
                        wsq4 = wsq[:, :, :].rearrange("p h d -> p (h d)")
                        step(nc.vector.tensor_tensor(wsq4, w_k[:, :], w_k[:, :], ALU.mult))
                        nc.vector.tensor_reduce(stat[:, 0, 16:32], wsq[:, :, :], AX.X, ALU.add).then_inc(bnd_in, 1)
                        dve.wait_ge(bnd_out, 2)
                        step(nc.vector.tensor_scalar(kbound2[:, :], stat[:, 1, 16:32], stat[:, 1, 0:1], None, ALU.mult))

                @block.tensor
                def _(pe):
                    for i, (kind, tiles, at) in enumerate(jobs):
                        if kind == "lat":
                            pe.wait_ge(lat_ready, 1)
                        elif L == 0:
                            pe.wait_ge(ctx_ready, 1 + sum(tiles[-1] >= b for a, b in ln_parts))
                        else:
                            pe.wait_ge(c_in, 32)
                        if i >= 2:
                            pe.wait_ge(tr_read, i - 1)
                        src = Z if kind == "lat" else raw
                        for j, t in enumerate(tiles):
                            last = nc.tensor.transpose(scores[:, i % 2, j * P:(j + 1) * P], src[:, t, :], ident[:, :])
                        last.then_inc(tr_done, 1)
                    if L == 0:
                        pe.wait_ge(mask_f, 1)
                        nc.tensor.transpose(outs[:, 0:CTX_FULL], mf[:, :], ident[0:CTX_FULL, 0:CTX_FULL]).then_inc(tr_done, 1)

        q1 = sb("q1", [P, GH, NQ], R32)
        q2 = sb("q2", [P, GH, NQ], R32)
        k1 = sb("k1", [P, 2, GH, CT, P], R32)
        k2 = sb("k2", [P, 2, GH, CT, P], R32)
        v16 = sb("v16", [P, 2, GH, CT, P], F16)
        v32 = sb("v32", [P, 2, GH, CT, P], R32)
        vlast = sb("v_last", [P, 2, GH, CT, 32], F16)

        def vlast_at(par, j):
            step = CT * 32 + 1
            return vlast[:, par].rearrange("p h t k -> p (h t k)")[:, j * 32:j * 32 + (GH - 1) * step + 1:step]

        zero32 = sb("zero32", [P, 32], F16)
        probs = sb("probs", [P, NB, NQ])
        plow = sb("probs_lo", [P, 2, NQ], R32)
        oacc_all = sb("out_acc", [P, GH, NQ])
        oacc = oacc_all
        esb = sqz[:, 4:8, :].rearrange("p a b -> p (a b)")
        x_h, x_l = sb("chunk_hi", [P, CT * P], R32), sb("chunk_lo", [P, CT * P], R32)
        w_h, w_l = sb("w_kv_hi", [P, 2 * GH * DH], R32), sb("w_kv_lo", [P, 2 * GH * DH], R32)
        w_raw = sqz[:, 0:4, :].rearrange("p a b -> p (a b)")
        krow = Z[:, 0:2, :].rearrange("p a (b c) -> p (a b) c", c=DH)
        ksq = Z[:, 2:4, :].rearrange("p a (b c) -> p (a b) c", c=DH)
        kst = sb("k_stat", [P, 3, GH])
        vrow = Z[:, 4:6, :].rearrange("p a (b c) -> p (a b) c", c=DH)
        qa = [k1[:, 1].rearrange("p a b k -> p (a b) k").rearrange("p (t h) k -> p t h k", h=GH),
              v32[:, 1].rearrange("p a b k -> p (a b) k").rearrange("p (t h) k -> p t h k", h=GH)]
        qb = oacc_all[:, :, :].rearrange("p a (b k) -> p (a b) k", k=P).rearrange("p (t h) k -> p t h k", h=GH)
        qsq = oacc_all[:, 0:2, :].rearrange("p a (b c) -> p (a b) c", c=DH)
        qst = sb("q_stat", [P, 4, QT * GH]) if L == 1 else \
            B["lnT"][:, GH * D:GH * D + 4 * QT * GH].rearrange("p (a b) -> p a b", a=4)
        frec = sb("fin_rec", [P, GH])
        ones = sb("ones", [P, GH])
        nullc = sb("null_cols", [P, 4])
        if L == 1:
            nullv = row[0:1, 2, DH:P]
            null16 = sb("null16", [1, P], F16)
            null32 = row[0:1, 3, :].bitcast(R32)
        qf = probs[:, 0:2, :].rearrange("p a (b c) -> p (a b) c", c=DH)
        last_ps = B["spare"]
        p_hi = probs[:, :, :].bitcast(B16).rearrange("p a (q w) -> p a q w", w=2)[:, :, :, 1]
        qps = scores[:, :, :].rearrange("p a (b c) -> p (a b) c", c=DH)

        def fin_bank(t, k):
            return outs[:, k * 512:(k + 1) * 512] if t % 2 == 0 else (proj, last_ps)[k][:, :]


        wkv_in, x_hi, x_lo = sem("wkv_in"), sem("x_hi"), sem("x_lo")
        NSPLIT = NFULL + 3
        kv_done, kv_read, kn_var, kn_rstd, kn_ready = (sem(s) for s in ("kv_done", "kv_read", "kn_var", "kn_rstd", "kn_ready"))
        kt_done, hi_done, lo_done, k2_done = (sem(s) for s in ("kt_done", "k_hi_done", "k_lo_done", "k2_done"))
        s_ready, p_ready, mixed, o_added, o_zero = (sem(s) for s in ("s_ready", "p_ready", "mixed", "o_added", "o_zero"))
        q_mm, q_rows, q_var, q_rstd, q_c2, q_c, q_final, q_hi, q_lo, qt_done, q1_read, q2_read = (
            sem(s) for s in ("q_mm", "q_rows", "q_var", "q_rstd", "q_c2", "q_c", "q_final", "q_hi", "q_lo", "qt_done", "q1_read", "q2_read"))
        v_hi_done, v16_done, v_ready, plo_ready, e_read, we_in, e_done = (
            sem(s) for s in ("v_hi_done", "v16_done", "v_ready", "plo_ready", "e_read", "w_last_in", "e_done"))
        fin_mm, fin_read, steps_s, consts, null_in, null_fix = (
            sem(s) for s in ("fin_mm", "fin_read", "dve_step", "consts", "null_in", "null_fix"))

        passed = sem("passed")

        def hold(eng, s, value):
            eng.wait_ge(s, value)
            eng.sem_inc(passed, 1)

        ONE = 1
        MIX0 = 4

        with nc.Block() as block:
            @block.sync
            def _(sp):
                with sp.Fori(0, NG) as g:
                    sp.wait_ge(x_lo, ONE + g * NSPLIT)
                    for kv in range(2):
                        sp.dma_start(w_raw[:, kv * GH * DH:(kv + 1) * GH * DH],
                                     A[NAME + "Wkv"][:, bass.ds(g * (GH * DH) + kv * H * DH, GH * DH)]).then_inc(wkv_in, 16)
                    sp.wait_ge(fin_read, ONE + g * QT)
                    for h in range(GH):
                        src = A[NAME + ("Wout" if L == 0 else "Wo")].rearrange("(h d) n -> h d n", d=DH)[
                            bass.ds(g * GH + h, 1), DH - 1, :]
                        for j in range(4):
                            sp.dma_start(w_e[32 * j + h:32 * j + h + 1, h, :], src).then_inc(we_in, 16)
                    if L == 1:
                        sp.wait_ge(v_ready, (g + 1) * NITEM - (CT - TAIL))
                        r_ = CTX_REST
                        wide = [1, GH, P - 1]
                        sp.dma_start(v16[r_:r_ + 1, 0, :, TAIL - 1, 0:P - 1],
                                     null16[0:1, 0:P - 1].unsqueeze(1).broadcast_to(wide)).then_inc(null_in, 16)
                        sp.dma_start(v32[r_:r_ + 1, 0, :, TAIL - 1, 0:P - 1].bitcast(F32),
                                     null32[:, 0:P - 1].bitcast(F32).unsqueeze(1).broadcast_to(wide)).then_inc(null_in, 16)
                        for h in range(GH):
                            sp.dma_start(vlast[r_:r_ + 1, 0, h, TAIL - 1, h:h + 1], null16[0:1, P - 1:P]).then_inc(null_in, 16)

            @block.gpsimd
            def _(pool):
                k2f = k2[:, :, :, :, :].bitcast(F32)
                step = Steps(pool, consts)
                step(nc.gpsimd.memset(k2f[:, 0], 0.0))
                step(nc.gpsimd.memset(k2f[:, 1], 0.0))
                step(nc.gpsimd.memset(ones[:, :], 1.0 / LIFT))
                step(nc.gpsimd.memset(oacc_all[:, :, :], 0.0))
                step(nc.gpsimd.memset(vlast[:, :, :, :, :], 0.0))
                step(nc.gpsimd.memset(zero32[:, :], 0.0))
                for par in range(2):
                    for h in range(GH):
                        r = DH if h % 2 == 0 else 0
                        step(nc.gpsimd.memset(k2f[r:r + 1, par, h], 1.0))

                def k_rstd(g, c, j):
                    if QK_NORM:
                        pool.wait_ge(kn_var, g * NITEM + c * CT + j + 1)
                        nc.gpsimd.tensor_tensor(kst[:, 2, :], kst[:, 1, :], mhalf[:, 0:GH], ALU.pow).then_inc(kn_rstd, 1)

                def k_again(g, c, j, par):
                    k = g * NITEM + c * CT + j
                    hold(pool, hi_done, k + 1)
                    for e, (a, b) in enumerate(((0, DH), (DH, P))):
                        nc.gpsimd.tensor_copy(k2[a:b, par, e::2, j, :],
                                              k1[a:b, par, e::2, j, :].bitcast(F32)).then_inc(k2_done, 1)
                        hold(pool, k2_done, 2 * k + e + 1)

                with pool.Fori(0, NG) as g:
                    k_rstd(g, 0, 0)
                    if QK_NORM:
                        pool.wait_ge(q_var, g + 1)
                        nc.gpsimd.tensor_tensor(qst[:, 2, :], qst[:, 1, :], mhalf[:, 0:QT * GH], ALU.pow).then_inc(q_rstd, 1)
                    k_again(g, 0, 0, 0)
                    k_rstd(g, 0, 1)
                    pool.wait_ge(q_c2, g + 1)
                    nc.gpsimd.tensor_tensor(qst[:, 2, :], qst[:, 1, :], phalf[:, 0:QT * GH], ALU.pow).then_inc(q_c, 1)
                    k_again(g, 0, 1, 0)
                    for j in range(2, CT):
                        k_rstd(g, 0, j)
                        k_again(g, 0, j, 0)
                    hold(pool, qt_done, (g + 1) * (2 * GH))
                    nc.gpsimd.memset(oacc_all[:, :, :], 0.0).then_inc(o_zero, 1)
                    with pool.Fori(0, PAIRS) as i:
                        for half in range(2):
                            for h in range(GH):
                                k_rstd(g, i * 2 + half + 1, h)
                                k_again(g, i * 2 + half + 1, h, 1 - half)

            @block.scalar
            def _(act):
                def read_kv(g, c, j, par):
                    k = g * NITEM + c * CT + j
                    act.wait_ge(kv_done, ONE + k + 1)
                    m = mask[:, bass.ds(c * CT + j, 1)]
                    nc.scalar.activation(krow, proj[:, 0:GH * DH].rearrange("p (h d) -> p h d", d=DH), ACT.Copy)
                    if QK_NORM:
                        nc.scalar.activation(ksq, proj[:, 0:GH * DH].rearrange("p (h d) -> p h d", d=DH), ACT.Square)
                    nc.scalar.activation(vrow, proj[:, GH * DH:2 * GH * DH].rearrange("p (h d) -> p h d", d=DH),
                                         ACT.Copy, scale=m).then_inc(kv_read, 1)
                    nc.scalar.activation(v16[:, par, :, j, P - 1], ones[:, :], ACT.Copy, scale=m)

                def v_hi(g, c, j, par):
                    act.wait_ge(kv_read, g * NITEM + c * CT + j + 1)
                    nc.scalar.activation(v16[:, par, :, j, 0:DH], vrow, ACT.Copy, scale=1.0 / LIFT).then_inc(v_hi_done, 1)

                def v_wide(g, c, j, par):
                    act.wait_ge(v16_done, g * NITEM + c * CT + j + 1)
                    nc.scalar.activation(v32[:, par, :, j, :], v16[:, par, :, j, :], ACT.Copy).then_inc(v_ready, 1)

                def k_hi(g, c, j, par):
                    k = g * NITEM + c * CT + j
                    act.wait_ge(kt_done, k + 1)
                    for e, (a, b) in enumerate(((0, DH), (DH, P))):
                        last = nc.scalar.activation(k1[a:b, par, e::2, j, :],
                                                    proj[a:b, 0:2 * P].rearrange("p (n k) -> p n k", k=P), ACT.Copy)
                    last.then_inc(hi_done, 1)

                def exp(s, n):
                    act.wait_ge(s_ready, s + 1)
                    nc.scalar.activation(probs[:, n % NB, :], scores[:, n % 2, :], ACT.Exp).then_inc(p_ready, 1)

                def x_high(g, c):
                    nc.scalar.activation(x_h[:, :], xT[:, bass.ds(c * (CT * P), CT * P)], ACT.Copy).then_inc(x_hi, 1)

                act.wait_ge(consts, 6 + 2 * GH)
                act.sem_inc(e_read, ONE)
                with act.Fori(0, NG) as g:
                    def q1_part(h):
                        act.wait_ge(qt_done, g * (2 * GH) + 2 * h + 1)
                        nc.scalar.activation(q1[:, h, :], scores[:, 0, :], ACT.Copy).then_inc(q1_read, 1)

                    act.wait_ge(wkv_in, (g + 1) * 32)
                    act.wait_ge(kv_done, ONE + g * NITEM)
                    nc.scalar.activation(w_h[:, :], w_raw, ACT.Copy).then_inc(x_hi, 1)
                    nc.scalar.activation(x_h[:, :], xT[:, 0:CT * P], ACT.Copy).then_inc(x_hi, 1)
                    act.wait_ge(q_mm, g + 1)
                    nc.scalar.activation(qf, qps, ACT.Copy, scale=1.0 if QK_NORM else SCALE).then_inc(q_rows, 1)
                    read_kv(g, 0, 0, 0)
                    v_hi(g, 0, 0, 0)
                    k_hi(g, 0, 0, 0)
                    v_wide(g, 0, 0, 0)
                    read_kv(g, 0, 1, 0)
                    v_hi(g, 0, 1, 0)
                    act.wait_ge(q_final, g + 1)
                    q4 = qf.rearrange("p (t h) d -> p t h d", h=GH)
                    for n in range(2):
                        for b in range(2):
                            nc.scalar.activation(qa[n][:, :, :, b * DH:(b + 1) * DH], q4[:, 4 * n:4 * n + 4],
                                                 ACT.Copy).then_inc(q_hi, 1)
                    k_hi(g, 0, 1, 0)
                    v_wide(g, 0, 1, 0)
                    read_kv(g, 0, 2, 0)
                    v_hi(g, 0, 2, 0)
                    q1_part(0)
                    k_hi(g, 0, 2, 0)
                    v_wide(g, 0, 2, 0)
                    read_kv(g, 0, 3, 0)
                    v_hi(g, 0, 3, 0)
                    q1_part(1)
                    k_hi(g, 0, 3, 0)
                    v_wide(g, 0, 3, 0)
                    q1_part(2)
                    q1_part(3)
                    nc.scalar.activation(x_h[:, :], xT[:, CT * P:2 * CT * P], ACT.Copy).then_inc(x_hi, 1)
                    for n in range(2):
                        exp(g * NSTEP + n, n)
                    with act.Fori(0, PAIRS) as i:
                        for half in range(2):
                            for h in range(GH):
                                item = (g, i * 2 + half + 1, h, 1 - half)
                                for t in range(CT):
                                    n = (half * GH + h) * CT + t + 2
                                    exp(g * NSTEP + i * (2 * CT * GH) + n, n)
                                    if t == 0:
                                        read_kv(*item)
                                    if t == 1:
                                        v_hi(*item)
                                        if h == GH - 1:
                                            x_high(g, i * 2 + half + 2)
                                    if t == 2:
                                        k_hi(*item)
                                        v_wide(*item)
                    for n in range(2, GH * TAIL):
                        exp(g * NSTEP + NFULL * CT * GH + n, n)
                    act.wait_ge(e_done, g + 1)
                    nc.scalar.activation(esb[:, :], last_ps[:, :], ACT.Copy, scale=1.0 / LIFT).then_inc(e_read, 1)

            @block.vector
            def _(dve):
                def k_var(g, c, j, link):
                    dve.wait_ge(kv_read, g * NITEM + c * CT + j + 1)
                    link(nc.vector.tensor_reduce(kst[:, 0, :], ksq, AX.X, ALU.add))
                    nc.vector.tensor_scalar(kst[:, 1, :], kst[:, 0, :], 1.0 / DH, 1e-16, ALU.mult, ALU.max).then_inc(kn_var, 1)

                def k_scale(g, c, j):
                    dve.wait_ge(kn_rstd, g * NITEM + c * CT + j + 1)
                    nc.vector.tensor_tensor(krow, krow, over(kst[:, 2, :], [P, GH, DH]), ALU.mult).then_inc(kn_ready, 1)

                def v_lo(g, c, j, par):
                    dve.wait_ge(v_hi_done, g * NITEM + c * CT + j + 1)
                    hi = v16[:, par, :, j, 0:DH]
                    nc.vector.scalar_tensor_tensor(out=vlast_at(par, j), in0=hi[:, :, DH - 1], scalar=-LIFT,
                                                   in1=vrow[:, :, DH - 1], op0=ALU.mult, op1=ALU.add)
                    nc.vector.scalar_tensor_tensor(out=v16[:, par, :, j, DH:P - 1], in0=hi[:, :, 0:DH - 1], scalar=-LIFT,
                                                   in1=vrow[:, :, 0:DH - 1], op0=ALU.mult, op1=ALU.add).then_inc(v16_done, 1)

                def p_lo(s, n):
                    dve.wait_ge(p_ready, s + 1)
                    dve.wait_ge(mixed, 2 * s + 2)
                    nc.vector.tensor_tensor(plow[:, n % 2, :], probs[:, n % NB, :], p_hi[:, n % NB],
                                            ALU.subtract).then_inc(plo_ready, 1)

                def k_lo(g, c, j, par):
                    k = g * NITEM + c * CT + j
                    dve.wait_ge(hi_done, k + 1)
                    for e, (a, b, a2, b2) in enumerate(((0, DH, DH, P), (DH, P, 0, DH))):
                        last = nc.vector.tensor_tensor(k1[a2:b2, par, e::2, j, :],
                                                       proj[a:b, 0:2 * P].rearrange("p (n k) -> p n k", k=P),
                                                       k1[a:b, par, e::2, j, :].bitcast(F32), ALU.subtract)
                    last.then_inc(lo_done, 1)

                def x_low(n, c):
                    dve.wait_ge(x_hi, n + 1)
                    x = xT[:, c * CT * P:(c + 1) * CT * P] if isinstance(c, int) else xT[:, bass.ds(c * (CT * P), CT * P)]
                    nc.vector.tensor_tensor(x_l[:, :], x, x_h[:, :].bitcast(F32), ALU.subtract).then_inc(x_lo, 1)

                def add_out(s, h):
                    for n in range(2):
                        q = slice(n * 512, (n + 1) * 512)
                        dve.wait_ge(mixed, 2 * s + n + 1 + MIX0)
                        nc.vector.tensor_tensor(oacc[:, h, q], outs[:, q], oacc[:, h, q], ALU.add).then_inc(o_added, 1)

                ITEM_LINKS = 1 if QK_NORM else 0
                Q_LINKS = 6
                FIN_LINKS = 5
                NULL_LINKS = 0 if QK_NORM else 6
                PER_GROUP = NITEM * ITEM_LINKS + Q_LINKS + QT * FIN_LINKS
                dve.wait_ge(consts, 6 + 2 * GH)
                for s in (lo_done, fin_read, x_lo):
                    dve.sem_inc(s, ONE)
                dve.sem_inc(o_added, 2 * ONE)
                if L == 1:
                    link = Steps(dve, steps_s, 0)
                    link(nc.vector.tensor_copy(nullc[:, 0:1].bitcast(R32), col[:, 1:2]))
                    link(nc.vector.tensor_tensor(nullc[:, 1:2], col[:, 1:2], nullc[:, 0:1], ALU.subtract))
                    nc.vector.tensor_copy(nullc[0:DH, 2:3], nullc[0:DH, 0:1])
                    nc.vector.tensor_copy(nullc[DH:P, 2:3], nullc[DH:P, 1:2])
                    link(nc.vector.tensor_copy(nullc[0:DH, 3:4], nullc[0:DH, 1:2]))
                    link(nc.vector.tensor_copy(nullc[DH:P, 3:4], nullc[DH:P, 0:1]))
                    link(nc.vector.tensor_copy(null16[:, 0:DH], row[0:1, 2, 0:DH]))
                    nc.vector.tensor_tensor(nullv, row[0:1, 2, 0:DH], null16[:, 0:DH], ALU.subtract).then_inc(null_fix, 1)
                    dve.wait_ge(null_fix, 1)
                    link(nc.vector.tensor_scalar(null16[:, DH:P], nullv, LIFT, None, ALU.mult))
                    nc.vector.tensor_copy(null32, null16[:, :]).then_inc(null_fix, 1)
                with dve.Fori(0, NG) as g:
                    link0 = g * PER_GROUP + NULL_LINKS
                    link = Steps(dve, steps_s, link0)
                    rows = [P, QT * GH, DH]
                    q4 = qf.rearrange("p (t h) d -> p t h d", h=GH)
                    c4 = qst[:, 2, :].rearrange("p (t h) -> p t h", h=GH)

                    def square_q():
                        dve.wait_ge(q_rows, g + 1)
                        link(nc.vector.tensor_tensor(qsq[:, :, :], qf, qf, ALU.mult))

                    def sum_q():
                        link(nc.vector.tensor_reduce(qst[:, 0, :], qsq[:, :, :], AX.X, ALU.add))

                    def part_1(j):
                        if QK_NORM:
                            k_var(g, 0, j, link)

                    def part_2(j):
                        if QK_NORM:
                            k_scale(g, 0, j)
                        v_lo(g, 0, j, 0)

                    def q2_part(h):
                        dve.wait_ge(qt_done, g * (2 * GH) + 2 * h + 2)
                        nc.vector.tensor_copy(q2[:, h, :], scores[:, 1, :]).then_inc(q2_read, 1)

                    dve.wait_ge(x_hi, g * NSPLIT + 1)
                    nc.vector.tensor_tensor(w_l[:, :], w_raw, w_h[:, :].bitcast(F32), ALU.subtract).then_inc(x_lo, 1)
                    x_low(g * NSPLIT + 1, 0)
                    if QK_NORM:
                        square_q()
                    part_1(0)
                    if QK_NORM:
                        sum_q()
                        nc.vector.tensor_scalar(qst[:, 1, :], qst[:, 0, :], 1.0 / DH, 1e-16, ALU.mult, ALU.max).then_inc(q_var, 1)
                    part_2(0)
                    k_lo(g, 0, 0, 0)
                    part_1(1)
                    if QK_NORM:
                        dve.wait_ge(q_rstd, g + 1)
                        link(nc.vector.tensor_tensor(qf, qf, over(qst[:, 2, :], rows), ALU.mult))
                        nc.vector.tensor_tensor(qf, qf, row[:, 1:2, 0:DH].broadcast_to(rows), ALU.mult).then_inc(q_final, 1)
                    else:
                        dve.wait_ge(q_rows, g + 1)
                        dve.sem_inc(q_final, 1)
                    part_2(1)
                    dve.wait_ge(q_final, g + 1)
                    square_q()
                    sum_q()
                    link(nc.vector.tensor_tensor(qst[:, 3, :].rearrange("p (t h) -> p t h", h=GH),
                                                 qst[:, 0, :].rearrange("p (t h) -> p t h", h=GH),
                                                 kbound2[:, bass.ds(g * GH, GH)].unsqueeze(1).broadcast_to([P, QT, GH]), ALU.mult))
                    nc.vector.tensor_scalar(qst[:, 1, :], qst[:, 3, :], 1e-30, None, ALU.max).then_inc(q_c2, 1)
                    k_lo(g, 0, 1, 0)
                    if not QK_NORM:
                        link(nc.vector.tensor_tensor(qsq[:, :, :], qf, row[:, 1:2, 0:DH].broadcast_to(rows), ALU.mult))
                        sum_q()
                    dve.wait_ge(q_hi, 4 * (g + 1))
                    for e in range(2):
                        at = 0 if e == 0 else DH
                        for n in range(2):
                            nc.vector.tensor_tensor(qb[:, 4 * n:4 * n + 4, e::2, at:at + DH], q4[:, 4 * n:4 * n + 4, e::2, :],
                                                    qa[n][:, :, e::2, 0:DH].bitcast(F32), ALU.subtract)
                    part_1(2)
                    dve.wait_ge(q_c, g + 1)
                    if not QK_NORM:
                        link(nc.vector.tensor_tensor(qst[:, 2, :], qst[:, 0, :], qst[:, 2, :], ALU.max))
                    for e in range(2):
                        cat = DH if e == 0 else 0
                        last = nc.vector.tensor_scalar(qb[:, :, e::2, cat], c4[:, :, e::2], -1.0, None, ALU.mult)
                    last.then_inc(q_lo, 1)
                    part_2(2)
                    q2_part(0)
                    k_lo(g, 0, 2, 0)
                    part_1(3)
                    q2_part(1)
                    part_2(3)
                    q2_part(2)
                    k_lo(g, 0, 3, 0)
                    q2_part(3)
                    x_low(g * NSPLIT + 2, 1)
                    hold(dve, o_zero, g + 1)
                    p_lo(g * NSTEP, 0)
                    with dve.Fori(0, PAIRS) as i:
                        for half in range(2):
                            for h in range(GH):
                                n = half * GH + h
                                s0 = g * NSTEP + i * (2 * CT * GH) + n * CT
                                item = (g, i * 2 + half + 1, h)
                                link = Steps(dve, steps_s, link0 + ITEM_LINKS * CT + Q_LINKS
                                             + i * (2 * CT * ITEM_LINKS) + n * ITEM_LINKS)
                                p_lo(s0 + 1, 1)
                                if QK_NORM:
                                    k_var(*item, link)
                                p_lo(s0 + 2, 2)
                                if QK_NORM:
                                    k_scale(*item)
                                v_lo(*item, 1 - half)
                                p_lo(s0 + 3, 3)
                                p_lo(s0 + 4, 0)
                                if h == GH - 1:
                                    x_low(g * NSPLIT + 3 + i * 2 + half, i * 2 + half + 2)
                                k_lo(*item, 1 - half)
                                add_out(s0 + CT - 1, h)
                    if L == 1:
                        dve.wait_ge(k2_done, (g + 1) * (2 * NITEM) - 2 * (CT - TAIL))
                        at = CTX_REST
                        for e in range(2):
                            nc.vector.tensor_copy(k1[:, 0, e::2, TAIL - 1, at:at + 1],
                                                  nullc[:, 2 + e:3 + e].unsqueeze(1).broadcast_to([P, GH // 2, 1]))
                            a, b = (0, DH) if e == 0 else (DH, P)
                            last = nc.vector.tensor_copy(k2[a:b, 0, e::2, TAIL - 1, at:at + 1],
                                                         nullc[a:b, 0:1].unsqueeze(1).broadcast_to([DH, GH // 2, 1]))
                        last.then_inc(null_fix, 1)
                    for n in range(1, GH * TAIL):
                        p_lo(g * NSTEP + NFULL * CT * GH + n, n)
                        if n % TAIL == 0:
                            add_out(g * NSTEP + NFULL * CT * GH + n - 1, n // TAIL - 1)
                    add_out((g + 1) * NSTEP - 1, GH - 1)
                    link = Steps(dve, steps_s, link0 + NITEM * ITEM_LINKS + Q_LINKS)
                    for t in range(QT):
                        dve.wait_ge(fin_mm, g * QT + t + 1)
                        for k in range(2):
                            ins = nc.vector.reciprocal(frec[:, 2 * k:2 * k + 2], fin_bank(t, k)[:, 0:2 * (D + 1)]
                                                       .rearrange("p (h n) -> p h n", h=2)[:, :, D])
                        link(ins)
                        part = Z[:, 6 + t % 2, :]
                        ps = [fin_bank(t, h // 2)[:, (h % 2) * (D + 1):(h % 2) * (D + 1) + D] for h in range(GH)]
                        nc.vector.scalar_tensor_tensor(out=Y[:, t, :], in0=ps[0], scalar=frec[:, 0:1], in1=Y[:, t, :],
                                                       op0=ALU.mult, op1=ALU.add).then_inc(steps_s, 1)
                        nc.vector.tensor_scalar(part, ps[1], frec[:, 1:2], None, ALU.mult).then_inc(steps_s, 1)
                        dve.wait_ge(steps_s, link.base + link.n + 1)
                        nc.vector.scalar_tensor_tensor(out=Y[:, t, :], in0=ps[2], scalar=frec[:, 2:3], in1=Y[:, t, :],
                                                       op0=ALU.mult, op1=ALU.add).then_inc(steps_s, 1)
                        dve.wait_ge(steps_s, link.base + link.n + 2)
                        nc.vector.scalar_tensor_tensor(out=part, in0=ps[3], scalar=frec[:, 3:4], in1=part,
                                                       op0=ALU.mult, op1=ALU.add).then_inc(fin_read, 1)
                        link.n += 3
                        dve.wait_ge(steps_s, link.base + link.n)
                        dve.wait_ge(fin_read, ONE + g * QT + t + 1)
                        link(nc.vector.tensor_tensor(Y[:, t, :], Y[:, t, :], part, ALU.add))

            @block.tensor
            def _(pe):
                def project_kv(g, c, j):
                    k = g * NITEM + c * CT + j
                    pe.wait_ge(lo_done, ONE + k)
                    if j == 0:
                        pe.wait_ge(x_lo, ONE + g * NSPLIT + 2 + c)
                    for n, (x, w) in enumerate(((x_h, w_h), (x_h, w_l), (x_l, w_h))):
                        last = nc.tensor.matmul(proj[:, :], x[:, j * P:(j + 1) * P], w[:, :], start=n == 0, stop=n == 2)
                    last.then_inc(kv_done, 1)

                def transpose_k(g, c, j):
                    k = g * NITEM + c * CT + j
                    pe.wait_ge(kn_ready if QK_NORM else kv_read, k + 1)
                    for n in range(GH // 2):
                        last = nc.tensor.transpose(proj[:, n * P:(n + 1) * P],
                                                   krow[:, 2 * n:2 * n + 2, :].rearrange("p h d -> p (h d)"), ident[:, :])
                    last.then_inc(kt_done, 1)

                def score(b, h, t, par, item=None, freed=None):
                    if freed is not None:
                        pe.wait_ge(p_ready, freed + 1)
                    if item is not None:
                        pe.wait_ge(lo_done, ONE + item + 1)
                        pe.wait_ge(k2_done, 2 * item + 2)
                    for kk, qq, first in ((k1, q1, True), (k2, q2, False)):
                        for n in range(NQ // 512):
                            last = nc.tensor.matmul(scores[:, b, n * 512:(n + 1) * 512], kk[:, par, h, t, :],
                                                    qq[:, h, n * 512:(n + 1) * 512], start=first, stop=not first)
                    last.then_inc(s_ready, 1)

                def mix(s, n_, h, t, par, last_t, u, item=None):
                    if item is not None:
                        pe.wait_ge(v_ready, item + 1)
                    pe.wait_ge(p_ready, s + 1)
                    halves = [slice(n * 512, (n + 1) * 512) for n in range(NQ // 512)]
                    b, last_e = n_ % NB, None
                    if t % 2 or t == last_t:
                        for n, q in enumerate(halves):
                            for tt in ((t - 1, t) if t % 2 else (t,)):
                                j = 32 * (2 * n + tt % 2)
                                last_e = nc.tensor.matmul(last_ps[j:j + 32, :], vlast[:, par, h, tt, :],
                                                          p_hi[:, (n_ - t + tt) % NB, q],
                                                          start=False, stop=True, skip_group_check=True)
                    for n, q in enumerate(halves):
                        if t == 0:
                            pe.wait_ge(o_added, 2 * u + n + 1)
                        nc.tensor.matmul(outs[:, q], v16[:, par, h, t, :], p_hi[:, b, q], start=t == 0, stop=False)
                    pe.wait_ge(plo_ready, s + 1)
                    for q in halves:
                        nc.tensor.matmul(outs[:, q], v32[:, par, h, t, :], plow[:, b % 2, q],
                                         start=False, stop=t == last_t).then_inc(mixed, 1)
                    return last_e

                pe.wait_ge(consts, 6 + 2 * GH)
                pe.sem_inc(kv_done, ONE)
                pe.sem_inc(mixed, MIX0)

                def project_q(at):
                    for t in range(QT):
                        last = nc.tensor.matmul(qps[:, t * GH:(t + 1) * GH, :].rearrange("p h d -> p (h d)"),
                                                lnT[:, t * P:(t + 1) * P], w_q[:, bass.ds(at, GH * DH)],
                                                start=t % 2 == 0, stop=True, skip_group_check=True)
                    last.then_inc(q_mm, 1)

                project_q(0)
                with pe.Fori(0, NG) as g:
                    def project_first(j):
                        project_kv(g, 0, j)

                    def transpose_q(h):
                        if h:
                            pe.wait_ge(q1_read, g * GH + h)
                        for t in range(QT):
                            last = nc.tensor.transpose(scores[:, 0, t * P:(t + 1) * P],
                                                       qa[t // 4][:, t % 4, h, :].bitcast(F32), ident[:, :])
                        last.then_inc(qt_done, 1)
                        if h:
                            pe.wait_ge(q2_read, g * GH + h)
                        for t in range(QT):
                            last = nc.tensor.transpose(scores[:, 1, t * P:(t + 1) * P], qb[:, t, h, :], ident[:, :])
                        last.then_inc(qt_done, 1)

                    pe.wait_ge(fin_read, ONE + g * QT)
                    project_first(0)
                    transpose_k(g, 0, 0)
                    project_first(1)
                    transpose_k(g, 0, 1)
                    project_first(2)
                    pe.wait_ge(q_lo, g + 1)
                    transpose_q(0)
                    transpose_k(g, 0, 2)
                    project_first(3)
                    transpose_q(1)
                    transpose_k(g, 0, 3)
                    transpose_q(2)
                    transpose_q(3)
                    pe.wait_ge(q1_read, (g + 1) * GH)
                    pe.wait_ge(q2_read, (g + 1) * GH)
                    score(0, 0, 0, 0, g * NITEM)
                    score(1, 0, 1, 0, g * NITEM + 1)
                    pe.wait_ge(e_read, ONE + g)
                    for j in range(4):
                        nc.tensor.matmul(last_ps[32 * j:32 * j + 32, :], zero32[:, :], vlast[:, 0, :, :, :].rearrange("p h t k -> p (h t k)"),
                                         start=True, stop=True, skip_group_check=True)
                    with pe.Fori(0, PAIRS) as i:
                        for half in range(2):
                            for h in range(GH):
                                for t in range(CT):
                                    n = (half * GH + h) * CT + t
                                    s = g * NSTEP + i * (2 * GH * CT) + n
                                    n2 = n + 2
                                    half2, h2, t2 = n2 // (GH * CT), n2 // CT % GH, n2 % CT
                                    item = g * NITEM + i * (2 * CT) + half2 * CT + t2 if h2 == 0 else None
                                    if t == CT - 1:
                                        transpose_k(g, i * 2 + half + 1, h)
                                    score(n2 % 2, h2, t2, half2 % 2, item, s)
                                    if t == 0:
                                        project_kv(g, i * 2 + half + 1, h)
                                    mix(s, n, h, t, half, CT - 1, g * NUNIT + i * (2 * GH) + half * GH + h,
                                        g * NITEM + i * (2 * CT) + half * CT + t if h == 0 else None)
                    for h in range(GH):
                        for t in range(TAIL):
                            n = h * TAIL + t
                            s = g * NSTEP + NFULL * CT * GH + n
                            n2 = n + 2
                            if n2 < GH * TAIL:
                                h2, t2 = n2 // TAIL, n2 % TAIL
                                if L == 1 and n2 == TAIL - 1:
                                    pe.wait_ge(null_fix, 2 + g + 1)
                                score(n2 % 2, h2, t2, 0, g * NITEM + NFULL * CT + t2 if h2 == 0 else None, s)
                            if L == 1 and n == TAIL - 1:
                                pe.wait_ge(null_in, (g + 1) * (16 * (2 + GH)))
                            last_e = mix(s, n, h, t, 0, TAIL - 1, g * NUNIT + NFULL * GH + h,
                                         g * NITEM + NFULL * CT + t if h == 0 else None)
                    last_e.then_inc(e_done, 1)
                    project_q(g * (GH * DH) + GH * DH)
                    pe.wait_ge(o_added, (g + 1) * (2 * NUNIT) + 2 * ONE)
                    pe.wait_ge(e_read, ONE + g + 1)
                    pe.wait_ge(we_in, (g + 1) * (16 * 4 * GH))
                    for t in range(QT):
                        if t >= 2:
                            pe.wait_ge(fin_read, ONE + g * QT + t - 1)
                        e0 = DH * (t // 4)
                        for h in range(GH):
                            at = (h % 2) * (D + 1)
                            nc.tensor.matmul(fin_bank(t, h // 2)[:, at:at + D + 1],
                                             oacc[:, h, t * P:(t + 1) * P],
                                             w_o[:, bass.ds(g * GH + h, 1), :].rearrange("p h n -> p (h n)"),
                                             start=h % 2 == 0, stop=False, skip_group_check=True)
                            last = nc.tensor.matmul(fin_bank(t, h // 2)[:, at:at + D],
                                                    esb[e0:e0 + DH, (t % 4) * P:(t % 4 + 1) * P], w_e[e0:e0 + DH, h, :],
                                                    start=False, stop=True, skip_group_check=True)
                        last.then_inc(fin_mm, 1)

        end_step, var2, rstd2 = sem("end_step"), sem("var2"), sem("rstd2")
        with nc.Block() as block:
            @block.gpsimd
            def _(pool):
                if L == 1:
                    rstd(pool, QT, var2, rstd2, 1)

            @block.vector
            def _(dve):
                step = Steps(dve, end_step)
                full = [P, QT, D]
                if L == 1:
                    step(nc.vector.tensor_reduce(stat[:, 0, 0:QT], Y[:, :, :], AX.X, ALU.max))
                    step(nc.vector.reciprocal(stat[:, 1, 0:QT], stat[:, 0, 0:QT]))
                    step(nc.vector.tensor_tensor(Y[:, :, :], Y[:, :, :], over(stat[:, 1, 0:QT], full), ALU.mult))
                    layer_norm(dve, step, Y[:, :, :], Y[:, :, :], sqz[:, :, :], QT, var2, rstd2, 1)
                op = ALU.add if L == 0 else ALU.mult
                step(nc.vector.tensor_tensor(Y[:, :, :], Y[:, :, :], row[:, 0:1, :].broadcast_to(full), op))
                step(nc.vector.scalar_tensor_tensor(out=X[:, :, :], in0=Y[:, :, :], scalar=gates[:, L:L + 1],
                                                    in1=X[:, :, :], op0=ALU.mult, op1=ALU.add))


def moe_layer(nc, A, L, sem_, sb_, layer_norm, rstd, out, B):
    X, Y, Z, sqz, stat, ident, lnT = (B[n] for n in ("X", "Y", "Z", "sqz", "stat", "ident", "lnT"))
    gates, scores, outs, proj, spare = (B[n] for n in ("gates", "scores", "outs", "proj", "spare"))
    FH = 512 if L == 0 else 64
    FC = NE * FH // P
    FE = FH // P if L == 0 else 1
    KH = P if L == 0 else FH
    NAME = "L%d_ffn_" % L

    def sem(name):
        return sem_("m%d_%s" % (L, name))

    scope = ExitStack()
    with scope:
        def sb(name, shape, dt=F32):
            return sb_("m%d_%s" % (L, name), shape, dt, scope)
        w1 = sb("w1", [P, NE * FH])
        w2 = sb("w2", [P, FC, D])
        wg = sb("wg", [P, NE])
        hid = sb("hidden", [P, 4 if L == 0 else 1, NQ])
        logit = sb("logit", [P, QT, NE])
        top = sb("top", [P, QT, NE])
        topi = sb("top_index", [P, QT, NE], U32)
        topf = sb("top_index_f", [P, QT, 2])
        ids = sb("expert_ids", [P, NE])
        gate = sb("gate", [P, 3, QT])
        one = sb("one_hot", [P, 2, QT, NE])
        comb = sb("combine", [P, QT, NE])

        w_in, step_s, var, rs, z_ready = (sem(s) for s in ("w_in", "step", "var", "rstd", "z_ready"))
        zt_done, zt_read, lg_done, e_in, e_out, ids_ok = (sem(s) for s in ("zt_done", "zt_read", "lg_done", "e_in", "e_out", "ids"))
        h_done, h_read, y_done, y_read, out_in = (sem(s) for s in ("h_done", "h_read", "y_done", "y_read", "out"))
        NH = FC // (4 if L == 0 else 1)
        HT = FC // NH
        EPR = NE // NH
        zt_ps = scores[:, 0, :]
        h_ps = scores
        y_ps = [proj, spare]

        with nc.Block() as block:
            @block.sync
            def _(sp):
                sp.dma_start(wg[:, :], A[NAME + "gateT"]).then_inc(w_in, 16)
                sp.dma_start(w1[:, :], A[NAME + "w1T"]).then_inc(w_in, 16)
                sp.dma_start(w2[:, :, :], A[NAME + "w2T"]).then_inc(w_in, 16)
                if L == 1:
                    sp.wait_ge(y_read, 2 * NE)
                    sp.dma_start(out.rearrange("(t p) d -> p t d", p=P), X[:, :, :]).then_inc(out_in, 16)
                    sp.wait_ge(out_in, 16)

            @block.gpsimd
            def _(pool):
                nc.gpsimd.iota(ids[:, :], [[1, NE]], base=0, channel_multiplier=0,
                               allow_small_or_imprecise_dtypes=True).then_inc(ids_ok, 1)
                rstd(pool, QT, var, rs, 1)

            @block.scalar
            def _(act):
                act.wait_ge(zt_done, 1)
                nc.scalar.activation(lnT[:, :], zt_ps, ACT.Copy).then_inc(zt_read, 1)
                act.wait_ge(e_in, 1)
                nc.scalar.activation(gate[:, 0, :], gate[:, 0, :], ACT.Exp).then_inc(e_out, 1)
                for n in range(NH):
                    for j in range(HT):
                        k = n * HT + j
                        act.wait_ge(h_done, k + 1)
                        if n and j == 0:
                            act.wait_ge(y_done, n * (2 * EPR))
                        nc.scalar.activation(hid[:, j, :], h_ps[:, k % 2, :],
                                             ACT.Relu if L == 0 else ACT.Gelu).then_inc(h_read, 1)

            @block.vector
            def _(dve):
                step = Steps(dve, step_s)
                layer_norm(dve, step, X[:, :, :], Z[:, :, :], sqz[:, :, :], QT, var, rs, 1)
                dve.sem_inc(z_ready, 1)
                dve.wait_ge(lg_done, 1)
                step(nc.vector.tensor_copy(logit[:, :, :], proj[:, 0:QT * NE].rearrange("p (t e) -> p t e", e=NE)))
                for t in range(QT):
                    nc.vector.max(top[:, t, :], logit[:, t, :]).then_inc(step_s, 1)
                step.n += QT
                dve.wait_ge(step_s, step.n)
                for t in range(QT):
                    nc.vector.max_index(topi[:, t, :], top[:, t, :], logit[:, t, :]).then_inc(step_s, 1)
                step.n += QT
                dve.wait_ge(step_s, step.n)
                step(nc.vector.tensor_copy(topf[:, :, :], topi[:, :, 0:2]))
                nc.vector.tensor_tensor(gate[:, 0, :], top[:, :, 1], top[:, :, 0], ALU.subtract).then_inc(e_in, 1)
                dve.wait_ge(e_out, 1)
                step(nc.vector.tensor_scalar(gate[:, 1, :], gate[:, 0, :], 1.0, None, ALU.add))
                step(nc.vector.reciprocal(gate[:, 2, :], gate[:, 1, :]))
                step(nc.vector.tensor_tensor(gate[:, 1, :], gate[:, 0, :], gate[:, 2, :], ALU.mult))
                dve.wait_ge(ids_ok, 1)
                full = [P, QT, NE]
                for k, w in ((0, 2), (1, 1)):
                    step(nc.vector.tensor_tensor(one[:, k], ids[:, :].unsqueeze(1).broadcast_to(full),
                                                 over(topf[:, :, k], full), ALU.is_equal))
                    step(nc.vector.tensor_tensor(one[:, k], one[:, k], over(gate[:, w, :], full), ALU.mult))
                step(nc.vector.tensor_tensor(comb[:, :, :], one[:, 0], one[:, 1], ALU.add))
                step(nc.vector.tensor_scalar(comb[:, :, :], comb[:, :, :], gates[:, 2 + L:3 + L], None, ALU.mult))
                for n in range(NE):
                    for half in range(2):
                        k = n * 2 + half
                        dve.wait_ge(y_done, k + 1)
                        for t in range(4):
                            q = half * 4 + t
                            last = nc.vector.scalar_tensor_tensor(
                                out=X[:, q, :], in0=y_ps[k % 2][:, t * P:(t + 1) * P], scalar=comb[:, q, n:n + 1],
                                in1=X[:, q, :], op0=ALU.mult, op1=ALU.add)
                        last.then_inc(y_read, 1)
                        dve.wait_ge(y_read, k + 1)

            @block.tensor
            def _(pe):
                pe.wait_ge(z_ready, 1)
                for t in range(QT):
                    last = nc.tensor.transpose(zt_ps[:, t * P:(t + 1) * P], Z[:, t, :], ident[:, :])
                last.then_inc(zt_done, 1)
                pe.wait_ge(zt_read, 1)
                pe.wait_ge(w_in, 48)
                for t in range(QT):
                    last = nc.tensor.matmul(proj[:, t * NE:(t + 1) * NE], lnT[:, t * P:(t + 1) * P], wg[:, :],
                                            start=True, stop=True, skip_group_check=True)
                last.then_inc(lg_done, 1)

                def hidden(k):
                    if k >= 2:
                        pe.wait_ge(h_read, k - 1)
                    for c in range(NQ // 512):
                        last = nc.tensor.matmul(h_ps[:, k % 2, c * 512:(c + 1) * 512], w1[:, k * P:(k + 1) * P],
                                                lnT[:, c * 512:(c + 1) * 512], start=True, stop=True)
                    last.then_inc(h_done, 1)

                hidden(0)
                hidden(1)
                for n in range(NH):
                    for j in range(2, HT):
                        hidden(n * HT + j)
                    for e in range(EPR):
                        for half in range(2):
                            k = (n * EPR + e) * 2 + half
                            if e == 0 and half == 0:
                                pe.wait_ge(h_read, (n + 1) * HT)
                            if k == 0:
                                pe.wait_ge(step_s, 6 + 1)
                            if k >= 2:
                                pe.wait_ge(y_read, k - 1)
                            a = 0 if L == 0 else e * FH
                            for t in range(4):
                                q = half * 4 + t
                                for j in range(FE):
                                    last = nc.tensor.matmul(
                                        y_ps[k % 2][:, t * P:(t + 1) * P], hid[a:a + KH, j, q * P:(q + 1) * P],
                                        w2[a:a + KH, n * HT + j, :], start=t == 0 and j == 0, stop=j == FE - 1,
                                        skip_group_check=True)
                            last.then_inc(y_done, 1)
                    if n + 1 < NH:
                        for j in range(min(2, HT)):
                            k = (n + 1) * HT + j
                            if L == 0 or k >= 2:
                                hidden(k)


_OUT = ((1, NQ, D), "float32")


def kernel(**inputs):
    import numpy as np
    import concourse.bacc as bacc
    from concourse.bass_utils import run_bass_kernel_spmd as run

    inp = {k: np.asarray(a) for k, a in inputs.items()}
    lay = {
        "x": inp["x"][0], "ctx": inp["ctx_1024"][0], "mask": inp["mask_BxS2_bf1"][0].view(np.uint8),
        "g_xattn": inp["g_xattn"], "g_ffn": inp["g_ffn"],
        "L0_ffn_gateT": inp["L0_ffn_gate_w"].T, "L1_ffn_gateT": inp["L1_ffn_w_gate"].T,
        "L0_ffn_w1T": inp["L0_ffn_w1"].reshape(-1, D).T, "L1_ffn_w1T": inp["L1_ffn_w_fc"].reshape(-1, D).T,
        "L0_ffn_w2T": inp["L0_ffn_w2"].transpose(0, 2, 1).reshape(-1, P, D).transpose(1, 0, 2),
        "L1_ffn_w2T": inp["L1_ffn_w_proj"].transpose(0, 2, 1).reshape(-1, P, D).transpose(1, 0, 2),
    }
    for k, a in inp.items():
        if "xattn_" in k and k[0] == "L":
            lay[k] = a
    nc = bacc.Bacc("TRN2", target_bir_lowering=False, num_devices=1)
    arrays, A = {}, {}
    for name, a in lay.items():
        a = np.ascontiguousarray(a)
        arrays["in_" + name] = a
        A[name] = nc.dram_tensor("in_" + name, a.shape, mybir.dt.from_np(a.dtype), kind="ExternalInput").ap()
    out = nc.dram_tensor("out", (NQ, D), F32, kind="ExternalOutput").ap()
    flamingo(nc, A, out)
    r = run(nc, [arrays], core_ids=[0])
    return r.results[0]["out"].reshape(_OUT[0])
```
